# Optimizing a Trainium2 kernel written in Bass

```python
import numpy as np
import jax
import jax.numpy as jnp

def _softmax(x, axis=-1):
    return jax.nn.softmax(x, axis=axis)

def _gelu(x):
    return jax.nn.gelu(x, approximate=True)

def _silu(x):
    return jax.nn.silu(x)

def _sigmoid(x):
    return jax.nn.sigmoid(x)

def _layernorm(x, axis=-1, eps=1e-05):
    m = jnp.mean(x, axis=axis, keepdims=True)
    v = jnp.var(x, axis=axis, keepdims=True)
    return (x - m) / jnp.sqrt(v + eps)

def _scatter_add(tgt, idx, src, axis=0):
    return tgt.at[idx].add(src)

def _segment_sum(src, seg, n):
    return jax.ops.segment_sum(src, seg, n)
kernel_name = 'mk_gnn_preln_d2_gnn_r8_db41d7'

def setup_inputs(seed: int=0):
    np.random.seed(seed)
    _w = jnp.asarray

    def _rec_inputs():
        import jax
        import jax.numpy as jnp
        _gk = jax.random.key(seed)
        x = -0.0006008 + 1.001 * jax.random.normal(jax.random.fold_in(_gk, 1), (6250, 256), jnp.float32)
        src = jax.random.randint(jax.random.fold_in(_gk, 2), (100000,), 0, 6250, jnp.int32)
        dst = jnp.minimum((6250 * jax.random.uniform(jax.random.fold_in(_gk, 3), (100000,)) ** 2.0).astype(jnp.int32), 49999)
        _o = jnp.argsort(dst, stable=True)
        src = src[_o]
        dst = dst[_o]
        edge_type_16 = jax.random.randint(jax.random.fold_in(_gk, 13), (100000,), 0, 16, jnp.int32)
        return (x, src, dst, edge_type_16)
    x, src, dst, edge_type_16 = _rec_inputs()

    def _L0_gnn_setup():
        import jax, jax.numpy as jnp
        import numpy as np
        from jax.ops import segment_sum
        N_NODES = 1250
        N_EDGES = 20000
        IN_FEAT = 256
        OUT_FEAT = 256
        NUM_RELS = 16

        def _inv_degree(idx, n):
            deg = segment_sum(jnp.ones(idx.shape[0], dtype=jnp.float32), idx, num_segments=n)
            return jnp.where(deg > 0, 1.0 / deg, 0.0)

        def _typed_pass(feat, W, bias, src_idx, dst_idx, etypes, norm_per_edge, n):
            proj = jnp.einsum('ni,rio->rno', feat, W)
            m = proj[etypes, src_idx] + bias
            m = m * norm_per_edge[:, None]
            return segment_sum(m, dst_idx, num_segments=n)
        key = jax.random.key(seed)
        ks = jax.random.split(key, 8)
        feat = jax.random.normal(ks[0], (N_NODES, IN_FEAT), dtype=jnp.float32)
        Wf = jax.random.normal(ks[1], (NUM_RELS, IN_FEAT, OUT_FEAT), dtype=jnp.float32)
        Wb = jax.random.normal(ks[2], (NUM_RELS, IN_FEAT, OUT_FEAT), dtype=jnp.float32)
        loop_weight = jax.random.normal(ks[3], (IN_FEAT, OUT_FEAT), dtype=jnp.float32)
        forward_bias = jnp.zeros((OUT_FEAT,), dtype=jnp.float32)
        backward_bias = jnp.zeros((OUT_FEAT,), dtype=jnp.float32)
        self_bias = jnp.zeros((OUT_FEAT,), dtype=jnp.float32)
        src = jax.random.randint(ks[4], (N_EDGES,), 0, N_NODES, dtype=jnp.int32)
        dst = jax.random.randint(ks[5], (N_EDGES,), 0, N_NODES, dtype=jnp.int32)
        etypes = jax.random.randint(ks[6], (N_EDGES,), 0, NUM_RELS, dtype=jnp.int32)
        return {'feat': feat, 'Wf': Wf, 'Wb': Wb, 'loop_weight': loop_weight, 'forward_bias': forward_bias, 'backward_bias': backward_bias, 'self_bias': self_bias, 'src': src, 'dst': dst, 'etypes': etypes, 'use_dis_weight': 0, 'drop_out': 0}
    _L0_gnn_all = _L0_gnn_setup()
    _L0_gnn_in = {k: v for k, v in _L0_gnn_all.items() if k in ('Wf', 'Wb', 'loop_weight', 'forward_bias', 'backward_bias', 'self_bias')}
    del _L0_gnn_all

    def _L1_gnn_setup():
        import jax, jax.numpy as jnp
        import numpy as np
        N_NODES = 6250
        N_EDGES = 125000
        F_IN = 256
        HEADS = 8
        F_HEAD = 32
        NEG_SLOPE = 0.2
        key = jax.random.key(seed)
        ks = jax.random.split(key, 6)
        x = jax.random.normal(ks[0], (N_NODES, F_IN), dtype=jnp.float32)
        W = jax.random.normal(ks[1], (F_IN, HEADS * F_HEAD), dtype=jnp.float32) / np.sqrt(F_IN)
        att_src = jax.random.normal(ks[2], (HEADS, F_HEAD), dtype=jnp.float32) / np.sqrt(F_HEAD)
        att_dst = jax.random.normal(ks[3], (HEADS, F_HEAD), dtype=jnp.float32) / np.sqrt(F_HEAD)
        bias = jnp.zeros((HEADS * F_HEAD,), dtype=jnp.float32)
        edge_index = jax.random.randint(ks[4], (2, N_EDGES), 0, N_NODES, dtype=jnp.int64)
        return {'x': x, 'W': W, 'att_src': att_src, 'att_dst': att_dst, 'bias': bias, 'edge_index': edge_index}
    _L1_gnn_all = _L1_gnn_setup()
    _L1_gnn_in = {k: v for k, v in _L1_gnn_all.items() if k in ('W', 'att_src', 'att_dst', 'bias')}
    del _L1_gnn_all
    return {'x': x, 'src': src, 'dst': dst, 'edge_type_16': edge_type_16, 'L0_gnn_Wf': _L0_gnn_in['Wf'], 'L0_gnn_Wb': _L0_gnn_in['Wb'], 'L0_gnn_loop_weight': _L0_gnn_in['loop_weight'], 'L0_gnn_forward_bias': _L0_gnn_in['forward_bias'], 'L0_gnn_backward_bias': _L0_gnn_in['backward_bias'], 'L0_gnn_self_bias': _L0_gnn_in['self_bias'], 'L1_gnn_W': _L1_gnn_in['W'], 'L1_gnn_att_src': _L1_gnn_in['att_src'], 'L1_gnn_att_dst': _L1_gnn_in['att_dst'], 'L1_gnn_bias': _L1_gnn_in['bias']}

def reference(x, src, dst, edge_type_16, L0_gnn_Wf, L0_gnn_Wb, L0_gnn_loop_weight, L0_gnn_forward_bias, L0_gnn_backward_bias, L0_gnn_self_bias, L1_gnn_W, L1_gnn_att_src, L1_gnn_att_dst, L1_gnn_bias):
    import jax
    import jax.numpy as jnp

    def _L0_gnn_ref(feat, Wf, Wb, loop_weight, forward_bias, backward_bias, self_bias, src, dst, etypes, use_dis_weight, drop_out):
        import jax, jax.numpy as jnp
        import numpy as np
        from jax.ops import segment_sum
        N_NODES = 1250
        N_EDGES = 20000
        IN_FEAT = 256
        OUT_FEAT = 256
        NUM_RELS = 16

        def _inv_degree(idx, n):
            deg = segment_sum(jnp.ones(idx.shape[0], dtype=jnp.float32), idx, num_segments=n)
            return jnp.where(deg > 0, 1.0 / deg, 0.0)

        def _typed_pass(feat, W, bias, src_idx, dst_idx, etypes, norm_per_edge, n):
            proj = jnp.einsum('ni,rio->rno', feat, W)
            m = proj[etypes, src_idx] + bias
            m = m * norm_per_edge[:, None]
            return segment_sum(m, dst_idx, num_segments=n)
        n = feat.shape[0]
        norm_f = _inv_degree(dst, n)[dst]
        m_forward = _typed_pass(feat, Wf, forward_bias, src, dst, etypes, norm_f, n)
        norm_b = _inv_degree(src, n)[src]
        m_backward = _typed_pass(feat, Wb, backward_bias, dst, src, etypes, norm_b, n)
        s = feat @ loop_weight
        s = s + s + self_bias
        return s + m_forward + m_backward

    def _L1_gnn_ref(x, W, att_src, att_dst, bias, edge_index):
        import jax, jax.numpy as jnp
        import numpy as np
        N_NODES = 6250
        N_EDGES = 125000
        F_IN = 256
        HEADS = 8
        F_HEAD = 32
        NEG_SLOPE = 0.2
        N = x.shape[0]
        src, dst = (edge_index[0], edge_index[1])
        h = (x @ W).reshape(N, HEADS, F_HEAD)
        a_src = jnp.einsum('nhf,hf->nh', h, att_src)
        a_dst = jnp.einsum('nhf,hf->nh', h, att_dst)
        e = jax.nn.leaky_relu(a_src[src] + a_dst[dst], NEG_SLOPE)
        e_max = jax.ops.segment_max(e, dst, num_segments=N)
        e_exp = jnp.exp(e - e_max[dst])
        denom = jax.ops.segment_sum(e_exp, dst, num_segments=N)
        alpha = e_exp / denom[dst]
        msgs = alpha[:, :, None] * h[src]
        out = jax.ops.segment_sum(msgs, dst, num_segments=N)
        return out.reshape(N, HEADS * F_HEAD) + bias
    edge_index = jnp.stack([src, dst])
    h = jnp.maximum(_layernorm(x, axis=-1), 0.0)
    x = x + _L0_gnn_ref(h, L0_gnn_Wf, L0_gnn_Wb, L0_gnn_loop_weight, L0_gnn_forward_bias, L0_gnn_backward_bias, L0_gnn_self_bias, src, dst, edge_type_16, 0, 0)
    h = jnp.maximum(_layernorm(x, axis=-1), 0.0)
    x = x + _L1_gnn_ref(h, L1_gnn_W, L1_gnn_att_src, L1_gnn_att_dst, L1_gnn_bias, edge_index)
    return x

_drawn_inputs = setup_inputs


def setup_inputs(seed=0):
    import zlib

    import numpy as np

    out = dict(_drawn_inputs(seed))
    spreads = {'L0_gnn_forward_bias': (0.0, 0.8),
     'L0_gnn_backward_bias': (0.0, 0.8),
     'L0_gnn_self_bias': (0.0, 0.8),
     'L1_gnn_bias': (0.0, 0.8)}
    factors = {'L1_gnn_att_src': 8.0, 'L1_gnn_att_dst': 8.0}
    for name, (base, spread) in spreads.items():
        noise = np.random.default_rng([zlib.crc32(name.encode()), seed]).standard_normal(out[name].shape)
        drawn = base * np.exp(spread * noise) if base else spread * noise
        out[name] = jnp.asarray(drawn.astype(out[name].dtype))
    for name, factor in factors.items():
        out[name] = (out[name] * factor).astype(out[name].dtype)
    return out
```

```python
from contextlib import ExitStack

import concourse.bass as bass
from concourse import mybir

F32 = mybir.dt.float32
F16 = mybir.dt.float16
BF16 = mybir.dt.bfloat16
I16 = mybir.dt.int16
I32 = mybir.dt.int32
ALU = mybir.AluOpType
ACT = mybir.ActivationFunctionType
AX = mybir.AxisListType

P = 128
EPS = 1e-05
SLOPE = 0.2
BIG = 1e30
TINY = 1e-30


class Link:

    def __init__(self, eng, sem):
        self.eng, self.sem, self.base, self.k = eng, sem, 0, 0

    def loop(self, i, per):
        self.start, self.per = self.base + self.k, per
        self.base = self.start + i * per
        self.k = 0

    def end_loop(self, n):
        assert self.k == self.per, (self.k, self.per)
        self.base, self.k = self.start + n * self.per, 0

    def __call__(self, ins, wait=True):
        ins.then_inc(self.sem, 1)
        self.k += 1
        if wait:
            self.eng.wait_ge(self.sem, self.base + self.k)


def build(nc, x, src, dst, typ, wf, wb, wloop, bf, bb, bself, w1, att_src, att_dst, b1, out):
    N, D = x.shape
    H, F_HEAD = att_src.shape
    R = wf.shape[0]
    E = src.shape[0]
    NB = -(-N // P)
    HALF = 8
    STEP = 2 * HALF
    ET = -(-E // (P * STEP)) * STEP
    ITS = ET // STEP
    TG = -(-ET // P)
    T = -(-(E // P + NB) // 16) * 16
    TH = T // 2
    TQ = T // 16
    IT2 = T // 16
    ARENA = 85120 // 4
    WREG = max(R * 2 * D, NB * D, 2 * T * H)
    SB = 7
    assert NB % SB == 0
    OB = 8
    OG = (NB - 1) // OB
    FULL = E // P
    REST = E - FULL * P

    with ExitStack() as ctx:
        def sb(name, shape, dt):
            return ctx.enter_context(nc.sbuf_tensor(name, shape, dt))

        def sem(name):
            return ctx.enter_context(nc.semaphore(name))

        bank = [ctx.enter_context(nc.psum_tensor(f"bank{i}", [P, 512], F32)) for i in range(8)]

        iota_row = sb("iota_row", [P, T], F16)
        iota_part = sb("iota_part", [P, 1], F32)
        ident16 = sb("ident16", [P, P], F16)
        ident32 = sb("ident32", [P, P], F32)
        before16 = sb("before16", [P, P], F16)
        above32 = sb("above32", [P, P], F32)
        ones32 = sb("ones32", [P, P], F32)
        zero16 = sb("zero16", [P, 512], F16)

        arena = sb("arena", [P, ARENA], F32)

        def carve(at, shape, dt):
            size = {F32: 4, I32: 4, F16: 2, BF16: 2}[dt]
            n = 1
            for d in shape:
                n *= d
            words = -(-n * size // 4)
            assert at % 4 == 0 and at // 4 + words <= ARENA, (at, words)
            v = arena[:, at // 4:at // 4 + words]
            if dt != F32:
                v = v.bitcast(dt)
            v = v[:, 0:n]
            if len(shape) == 2:
                v = v.rearrange("p (a b) -> p a b", b=shape[1])
            if len(shape) == 3:
                v = v.rearrange("p (a b c) -> p a b c", b=shape[1], c=shape[2])
            return v, at + 4 * words

        col, at = carve(0, [3, TG * P], I32)
        sort_at = at
        nat, at = carve(at, [3, TG, P], I32)
        natf, at = carve(at, [3, TG, P], F32)
        at = sort_at
        keyloc, at = carve(at, [ET], F32)
        keyblk, at = carve(at, [ET], F32)
        pay, at = carve(at, [3, ET], F32)
        tmpi, at = carve(at, [2, ET], I32)
        posf, at = carve(at, [ET], F32)
        oloc, at = carve(at, [STEP, P], F16)
        oblk, at = carve(at, [STEP, NB], F16)
        olocT16, at = carve(at, [STEP, P], F16)
        olocT32, at = carve(at, [STEP, P], F32)
        oblkT_all, at = carve(at, [STEP, P], F16)
        oblkT = oblkT_all[0:64]
        hist, at = carve(at, [STEP, NB], F32)
        gsel, at = carve(at, [HALF, NB], F32)
        gs, at = carve(at, [HALF], F32)
        rk, at = carve(at, [STEP], F32)
        junk, at = carve(at, [P], F16)
        cnt, at = carve(at, [NB], F32)
        tot, at = carve(at, [NB], F32)
        toti, at = carve(at, [NB], I32)
        tend, at = carve(at, [NB], F32)
        ohi, at = carve(at, [4, T], F16)
        olo, at = carve(at, [4, 3 * P], F16)
        olo = olo.rearrange("p a (k e) -> p a k e", e=P)
        ckb, at = carve(at, [T], F32)
        sort_end = at

        accf, at = carve(0, [NB * (D + H)], F32)
        rows, at = carve(at, [16, D + H], F32)
        acc0 = accf[:, 0:NB * D]
        oh, at = carve(at, [16, P], F32)
        ohT, at = carve(at, [16, P], F32)
        segmax, at1 = carve(0, [TQ * P], F32)
        locT, at1 = carve(at1, [TQ * P], F16)
        pen, at1 = carve(at1, [TQ * P], BF16)
        lastT, at1 = carve(at1, [TQ * P], F16)
        assert at1 <= 4 * NB * (D + H) + 4 * 16 * (D + H)

        wreg = sb("wreg", [P, WREG], F32)
        x_all = wreg[:, 0:NB * D].rearrange("p (b d) -> p b d", d=D)
        wrel = wreg[:, 0:R * 2 * D].rearrange("p (r c o) -> p r c o", c=2, o=D)
        asrc = wreg[:, 0:T * H]
        smax = wreg[:, T * H:2 * T * H]
        asrc3 = asrc.rearrange("p (t h) -> p t h", h=H)
        smax3 = smax.rearrange("p (t h) -> p t h", h=H)

        sidx = [sb(f"sidx{s}", [P, T], I32) for s in range(2)]
        sloc = [sb(f"sloc{s}", [P, T], F16) for s in range(2)]
        sblk = [sb(f"sblk{s}", [P, T], I16) for s in range(2)]
        deg = [sb(f"deg{s}", [P, NB], F32) for s in range(2)]
        inv = [sb(f"inv{s}", [P, NB], F32) for s in range(2)]
        has = [sb(f"has{s}", [P, NB], F32) for s in range(2)]

        stats = sb("stats", [P, SB, 6], F32)
        mvs = sb("mvs", [P, SB, 2], F32)
        mv = sb("mv", [P, NB, 2], F32)
        rstd = sb("rstd", [P, NB], F32)
        mv2 = mv[:, :, :].rearrange("p b j -> p (b j)")
        eps = sb("eps", [P, 1], F32)
        minus1 = sb("minus1", [P, 1], F32)
        xin = sb("xin", [P, D], F32)
        xh = sb("xh", [P, D], F32)
        hT = sb("hT", [P, 2, P], F32)
        stage = sb("stage", [P, 2, 4 * D], F32)
        wl = sb("wl", [P, 2, D], F32)
        bias_rows = sb("bias_rows", [P, 4, D], F32)
        w1x = sb("w1x", [P, 2, D + 2 * H], F32)
        grow = sb("grow", [P, D + 2 * H], F32)
        asn = sb("asn", [P, NB, H], F32)
        tab = sb("tab", [P, NB, 2 * H], F32)
        tab2 = tab[:, :, :].rearrange("p b j -> p (b j)")
        macc = sb("macc", [P, NB * H], F32)
        gm = sb("gm", [P, 1], F32)
        gmd = sb("gmd", [P, H], F32)
        att_rows = sb("att_rows", [P, 2, D], F32)
        selfst = sb("selfst", [P, D], F32)
        gsel8 = sb("gsel8", [P, P], F32)
        gmin_part = sb("gmin_part", [P, 1], F32)
        gmin_row = sb("gmin_row", [P, H], F32)
        idxst = sb("idxst", [P, 2, HALF], I32)
        ast = sb("ast", [P, 16, H], F32)
        score = sb("score", [P, 16, H], F32)
        rden = sb("rden", [P, NB, H], F32)
        stg = sb("stg", [P, 2, P], F32)

        def scratch(name, shape):
            return nc.dram_tensor(name, shape, F32, kind="Internal").ap()

        xpad = scratch("xpad", (NB * P, D))
        xself = scratch("xself", (NB * P, D))
        hTd = scratch("hTd", (NB * P, 2 * P))
        table = [scratch(f"table{s}", (NB * P * R, D)) for s in range(2)]
        x1d = scratch("x1d", (NB * P, D))
        gtab = scratch("gtab", (NB * P, D + H))
        stab = scratch("stab", (NB * P, H))

        consts = sem("consts")
        pads_set = sem("pads_set")
        loaded = sem("loaded")
        nat_ready = sem("nat_ready")
        col_psum = sem("col_psum")
        col_taken = sem("col_taken")
        dv = sem("dv")
        a_oh = sem("a_oh")
        a_used = sem("a_used")
        a_done = sem("a_done")
        b_cnt = sem("b_cnt")
        b_tot = sem("b_tot")
        s_oh = sem("s_oh")
        s_tr = sem("s_tr")
        s_trcopied = sem("s_trcopied")
        s_c = sem("s_c")
        s_h = sem("s_h")
        s_g = sem("s_g")
        s_eq = sem("s_eq")
        s_rk = sem("s_rk")
        s_pos = sem("s_pos")
        p_oh = sem("p_oh")
        p_used = sem("p_used")
        p_done = sem("p_done")
        p_taken = sem("p_taken")
        x_all_in = sem("x_all_in")
        x_all_zero = sem("x_all_zero")
        x_stored = sem("x_stored")
        w_in = sem("w_in")
        wb_in = sem("wb_in")
        stats_read = sem("stats_read")
        var_ready = sem("var_ready")
        std_ready = sem("std_ready")
        rstd_ready = sem("rstd_ready")
        xin_in = sem("xin_in")
        xin_used = sem("xin_used")
        xh_ready = sem("xh_ready")
        xT_psum = sem("xT_psum")
        hT_ready = sem("hT_ready")
        hT_out = sem("hT_out")
        hT_in = sem("hT_in")
        loop_psum = sem("loop_psum")
        self_ready = sem("self_ready")
        self_out = sem("self_out")
        self_stored = sem("self_stored")
        rel_psum = sem("rel_psum")
        rel_copied = sem("rel_copied")
        node_mm_done = sem("node_mm_done")
        acc_in = sem("acc_in")
        idx_copied = sem("idx_copied")
        rows_free = sem("rows_free")
        oh_ready = sem("oh_ready")
        agg_done = sem("agg_done")
        acc_free = sem("acc_free")
        x1_ready = sem("x1_ready")
        x1_out = sem("x1_out")
        w1_in = sem("w1_in")
        w1_ready = sem("w1_ready")
        n_xh = sem("n_xh")
        n_T = sem("n_T")
        n_hT = sem("n_hT")
        n_psum = sem("n_psum")
        n_grow = sem("n_grow")
        n_out = sem("n_out")
        n_used = sem("n_used")
        gm_T = sem("gm_T")
        gm_ready = sem("gm_ready")
        gm_mm = sem("gm_mm")
        ast_copied = sem("ast_copied")
        asrc_all = sem("asrc_all")
        f_stage = sem("f_stage")
        f_T = sem("f_T")
        f_copied = sem("f_copied")
        b_stage = sem("b_stage")
        b_T = sem("b_T")
        b_copied = sem("b_copied")
        m_max = sem("m_max")
        m_psum = sem("m_psum")
        m_free = sem("m_free")
        tab_ready = sem("tab_ready")
        weights_in = sem("weights_in")
        l_T = sem("l_T")
        l_ohT = sem("l_ohT")
        l_look = sem("l_look")
        l_sc = sem("l_sc")
        l_exp = sem("l_exp")
        l_exp_used = sem("l_exp_used")
        l_msg = sem("l_msg")
        x1_in = sem("x1_in")
        fin = sem("fin")
        out_done = sem("out_done")
        ast_free = sem("ast_free")
        pace = sem("pace")
        acc_zero = sem("acc_zero")
        idx_ready = sem("idx_ready")
        node_free = sem("node_free")
        w_all = sem("w_all")
        msg_ready = sem("msg_ready")
        agg4_done = sem("agg4_done")
        fin_start = sem("fin_start")
        n_T2 = sem("n_T2")
        gathered_all = sem("gathered_all")
        gathered = [sem(f"gathered{u}") for u in range(16)]
        stage_sem = [[sem(f"table_out{s}_{j}") for j in range(2)] for s in range(2)]
        NG = TG * 3

        def load_blocks(engine, s, t):
            return nc.values_load_multi_w_load_instructions(
                sblk[s][0:1, bass.ds(t, HALF)], engines=[engine], min_val=0, max_val=NB - 1,
                skip_runtime_bounds_check_because="made from at most NB - 1 comparisons")[1]

        block = ctx.enter_context(nc.Block())

        @block.sync
        def _(sp):
            sp.wait_ge(pads_set, 1)
            g = FULL // P
            for j, a in enumerate((dst, src, typ)):
                sp.dma_start(nat[:, j, 0:g, :], a[0:g * P * P].rearrange("(g t p) -> t g p", t=P, p=P)).then_inc(loaded, 16)
                sp.dma_start(nat[0:FULL - g * P, j, g, :], a[g * P * P:FULL * P].rearrange("(t p) -> t p", p=P)).then_inc(loaded, 16)
                sp.dma_start(nat[FULL - g * P:FULL - g * P + 1, j, g, 0:REST], a[FULL * P:E].rearrange("(t p) -> t p", t=1)).then_inc(loaded, 16)
            sp.wait_ge(x_all_zero, 1)
            full_rows = (NB - 1) * P
            sp.dma_start(x_all[:, 0:NB - 1, :], x[0:full_rows, :].rearrange("(b p) d -> p b d", p=P)).then_inc(x_all_in, 16)
            sp.dma_start(x_all[0:N - full_rows, NB - 1, :], x[full_rows:N, :]).then_inc(x_all_in, 16)
            sp.dma_start(wl[:, :, :], wloop.rearrange("(c i) o -> i c o", i=P)).then_inc(w_all, 16)
            sp.dma_start(w1x[:, :, 0:D], w1.rearrange("(c i) o -> i c o", i=P)).then_inc(w_all, 16)
            for j, b in enumerate((bself, bf, bb, b1)):
                sp.dma_start(bias_rows[:, j, :], b.partition_broadcast(P)).then_inc(w_all, 16)
            for j, b in enumerate((att_src, att_dst)):
                sp.dma_start(att_rows[:, j, :], b.rearrange("h f -> (h f)").partition_broadcast(P)).then_inc(w_all, 16)
            sp.wait_ge(x_all_in, 32)
            sp.dma_start(xpad.rearrange("(b p) d -> p b d", p=P), x_all[:, :, :]).then_inc(x_stored, 16)
            sp.wait_ge(x_stored, 16)
            sp.wait_ge(stats_read, NB)
            sp.dma_start(wrel, wf.rearrange("r (c i) o -> i r c o", i=P)).then_inc(w_in, 16)

            def table_rows(s, it):
                rows_of = table[s].rearrange("(n r) d -> n (r d)", r=R)
                for j in range(4):
                    sp.wait_ge(rel_copied, 8 * (s * NB + it) + 2 * (j + 1))
                    sp.dma_start(rows_of[bass.ds(it * P, P), j * 4 * D:(j + 1) * 4 * D], stage[:, j % 2, :]).then_inc(stage_sem[s][j % 2], 16)

            with sp.Fori(0, NB) as it:
                sp.wait_ge(xin_used, it + 1)
                sp.dma_start(xin[:, :], xpad[bass.ds(it * P, P), :]).then_inc(xin_in, 16)
                sp.wait_ge(hT_ready, it + 1)
                sp.dma_start(hTd[bass.ds(it * P, P), :], hT[:, :, :].rearrange("p c n -> p (c n)")).then_inc(hT_out, 16)
                sp.wait_ge(self_ready, it + 1)
                sp.dma_start(xself[bass.ds(it * P, P), :], selfst[:, :]).then_inc(self_out, 16)
                table_rows(0, it)
            sp.wait_ge(node_mm_done, NB)
            sp.dma_start(wrel, wb.rearrange("r (c i) o -> i r c o", i=P)).then_inc(wb_in, 16)
            sp.wait_ge(hT_out, 16 * (NB + 1))
            with sp.Fori(0, NB) as it:
                sp.wait_ge(node_mm_done, NB + it)
                sp.dma_start(hT[:, :, :].rearrange("p c n -> p (c n)"), hTd[bass.ds(it * P, P), :]).then_inc(hT_in, 16)
                table_rows(1, it)
            sp.wait_ge(p_taken, 2)
            sp.wait_ge(self_out, 16 * (NB + 1))
            sp.dma_start(acc0.rearrange("p (b d) -> p b d", d=D), xself.rearrange("(b p) d -> p b d", p=P)).then_inc(acc_in, 16)
            sp.wait_ge(x1_ready, 1)
            sp.dma_start(x1d.rearrange("(b p) d -> p b d", p=P), acc0.rearrange("p (b d) -> p b d", d=D)).then_inc(x1_out, 16)
            with sp.Fori(0, NB) as it:
                sp.wait_ge(n_grow, it + 1)
                sp.dma_start(gtab[bass.ds(it * P, P), :], grow[:, 0:D + H]).then_inc(n_out, 16)
                sp.dma_start(stab[bass.ds(it * P, P), :], grow[:, D:D + H]).then_inc(n_out, 16)
            sp.wait_ge(fin_start, 1)
            sp.wait_ge(x1_out, 16)
            sp.dma_start(x_all[:, :, :], x1d.rearrange("(b p) d -> p b d", p=P)).then_inc(x1_in, 16)
            for g in range(OG):
                sp.wait_ge(fin, g + 1)
                sp.dma_start(out[g * OB * P:(g + 1) * OB * P, :].rearrange("(b p) d -> p b d", p=P), x_all[:, g * OB:(g + 1) * OB, :]).then_inc(out_done, 16)
            sp.wait_ge(fin, OG + 1)
            sp.dma_start(out[full_rows:N, :], x_all[0:N - full_rows, NB - 1, :]).then_inc(out_done, 16)
            sp.wait_ge(out_done, 16 * (OG + 1))

        @block.gpsimd
        def _(pool):
            link = Link(pool, consts)
            pool.iota(iota_row[:, :], pattern=[[1, T]], base=0, channel_multiplier=0, allow_small_or_imprecise_dtypes=True).then_inc(consts, 1)
            pool.iota(iota_part[:, :], pattern=[[0, 1]], base=0, channel_multiplier=1, allow_small_or_imprecise_dtypes=True).then_inc(consts, 1)
            link.base = 2
            link(pool.memset(ident16[:, :], 0.0))
            link(pool.affine_select(out=ident16[:, :], in_=ident16[:, :], compare_op=ALU.not_equal, fill=1.0, base=0, pattern=[[-1, P]], channel_multiplier=1))
            link(pool.memset(ident32[:, :], 0.0))
            link(pool.affine_select(out=ident32[:, :], in_=ident32[:, :], compare_op=ALU.not_equal, fill=1.0, base=0, pattern=[[-1, P]], channel_multiplier=1))
            link(pool.memset(before16[:, :], 0.0))
            link(pool.affine_select(out=before16[:, :], in_=before16[:, :], compare_op=ALU.is_gt, fill=-1.0, base=0, pattern=[[-1, P]], channel_multiplier=1))
            link(pool.memset(above32[:, :], 1.0))
            link(pool.affine_select(out=above32[:, :], in_=above32[:, :], compare_op=ALU.is_gt, fill=0.0, base=0, pattern=[[1, P]], channel_multiplier=-1))
            link(pool.memset(ones32[:, :], 1.0))
            link(pool.memset(zero16[:, :], 0.0))
            link(pool.memset(oblkT[:, :, :], 0.0))

            def gather(k, from_table, to, idx, free):
                with pool.Fori(0, IT2) as it:
                    for h in range(2):
                        half = 2 * (k * IT2 + it) + h
                        pool.wait_ge(free, half + 1)
                        pool.sem_inc(pace, 1)
                        pool.tensor_copy(idxst[:, h, :], idx[:, bass.ds(it * 16 + h * HALF, HALF)]).then_inc(idx_copied, 1)
                        pool.wait_ge(idx_copied, half + 1)
                        pool.sem_inc(pace, 1)
                        for u in range(HALF):
                            pool.indirect_dma_start(to(h * HALF + u), None, from_table,
                                                    bass.IndirectOffsetOnAxis(idxst[:, h, u:u + 1], 0)).then_inc(gathered[h * HALF + u], 16)

            pool.wait_ge(p_taken, 2)
            for s in range(2):
                for q in range(2):
                    pool.wait_ge(stage_sem[s][q], 16 * (2 * NB + 1))
                gather(s, table[s], lambda u: rows[:, u, 0:D], sidx[s], rows_free)
            pool.wait_ge(n_out, 32 * NB + 32)
            pool.wait_ge(idx_ready, 1)
            gather(2, stab, lambda u: ast[:, u, :], sidx[0], rows_free)
            pool.wait_ge(b_stage, TQ)
            gather(3, gtab, lambda u: rows[:, u, :], sidx[0], rows_free)
        NCONST = 13

        @block.scalar
        def _(act):
            for n in range(NG):
                act.wait_ge(col_psum, n + 1)
                nc.scalar.copy(col[:, n // TG, (n % TG) * P:(n % TG + 1) * P], bank[n % 2][:, 0:P]).then_inc(col_taken, 1)
            act.wait_ge(var_ready, 1)
            nc.scalar.activation(rstd[:, :], mv[:, :, 1], ACT.Sqrt, bias=eps[:, 0:1]).then_inc(std_ready, 1)
            act.wait_ge(consts, NCONST)
            act.sem_inc(hT_out, 16)
            for s in range(2):
                for q in range(2):
                    act.sem_inc(stage_sem[s][q], 16)
            for s in range(2):

                def relation_rows(it, groups):
                    for g in groups:
                        n = 8 * (s * NB + it) + g
                        if g % 2 == 0:
                            act.wait_ge(stage_sem[s][g // 2 % 2], 16 * (2 * it + g // 4 + 1))
                            act.sem_inc(pace, 1)
                        act.wait_ge(rel_psum, n + 1)
                        nc.scalar.copy(stage[:, g // 2 % 2, (g % 2) * 2 * D:(g % 2 + 1) * 2 * D], bank[6 + g % 2][:, :]).then_inc(rel_copied, 1)

                with act.Fori(0, ITS) as it:
                    for h in range(2):
                        step = 2 * (s * ITS + it) + h
                        hs = slice(h * HALF, (h + 1) * HALF)
                        act.wait_ge(s_tr, step + 1)
                        t16 = bank[0][:, :].bitcast(F16).rearrange("p (t e) -> p t e", e=P)
                        nc.scalar.copy(olocT16[:, hs, :], t16).then_inc(s_trcopied, 1)
                        nc.scalar.copy(olocT32[:, hs, :], t16).then_inc(s_trcopied, 1)
                        nc.scalar.copy(oblkT[0:NB, hs, :], bank[1][0:NB, :].bitcast(F16).rearrange("p (t e) -> p t e", e=P)).then_inc(s_trcopied, 1)
                        if h == 0 and s == 0:
                            act.wait_ge(hT_out, 16 * (it + 1))
                            act.wait_ge(xT_psum, it + 1)
                            nc.scalar.activation(hT[:, :, :], bank[6][:, 0:2 * P].rearrange("p (c n) -> p c n", n=P), ACT.Relu).then_inc(hT_ready, 1)
                        act.wait_ge(s_eq, step + 1)
                        for u in range(HALF):
                            nc.scalar.activation(junk, bank[4 + u // 4][:, (u % 4) * P:(u % 4 + 1) * P], ACT.Relu, bias=minus1[:, 0:1],
                                                 accum_out=rk[:, h * HALF + u:h * HALF + u + 1]).then_inc(s_rk, 1)
                            act.wait_ge(s_rk, step * HALF + u + 1)
                        relation_rows(it, range(4 * h, 4 * h + 4))
            act.wait_ge(var_ready, 2)
            nc.scalar.activation(rstd[:, :], mv[:, :, 1], ACT.Sqrt, bias=eps[:, 0:1]).then_inc(std_ready, 1)
            act.sem_inc(n_out, 32)
            with act.Fori(0, NB) as it:
                act.wait_ge(n_T, it + 1)
                nc.scalar.activation(hT[:, :, :], bank[0][:, 0:2 * P].rearrange("p (c n) -> p c n", n=P), ACT.Relu).then_inc(n_hT, 1)
                act.wait_ge(n_out, 32 * (it + 1))
                act.sem_inc(pace, 1)
                act.wait_ge(n_psum, it + 1)
                nc.scalar.copy(grow[:, :], bank[1][:, 0:D + 2 * H]).then_inc(n_grow, 1)
            with act.Fori(0, IT2) as it:
                for h in range(2):
                    for u in range(h * HALF, (h + 1) * HALF):
                        act.wait_ge(gathered[u], 16 * (2 * IT2 + it + 1))
                    act.sem_inc(pace, 1)
                    nc.scalar.copy(asrc[:, bass.ds(it * 16 * H + h * HALF * H, HALF * H)],
                                   ast[:, h * HALF:(h + 1) * HALF, :].rearrange("p t h -> p (t h)")).then_inc(asrc_all, 1)
                    act.wait_ge(asrc_all, 2 * it + h + 1)
                    act.sem_inc(rows_free, 1)
            act.wait_ge(gm_ready, 1)
            with act.Fori(0, TQ) as q:
                act.wait_ge(f_T, q + 1)
                act.sem_inc(pace, 1)
                nc.scalar.activation(segmax[:, bass.ds(q * P, P)], bank[0][:, 0:P], ACT.Identity, bias=gmin_part[:, 0:1]).then_inc(f_copied, 1)
                nc.scalar.copy(locT[:, bass.ds(q * P, P)], bank[0][:, P:2 * P]).then_inc(f_copied, 1)
            with act.Fori(0, TQ) as q:
                act.wait_ge(b_T, q + 1)
                act.sem_inc(pace, 1)
                nc.scalar.copy(smax.rearrange("p (k q h) -> p q k h", q=TQ, h=H)[:, bass.ds(q, 1), :, :],
                               bank[1][:, 0:P].rearrange("p (q k h) -> p q k h", q=1, h=H)).then_inc(b_copied, 1)
            with act.Fori(0, IT2) as it:
                for q in range(4):
                    act.wait_ge(l_T, 4 * it + q + 1)
                    nc.scalar.copy(ohT[:, 4 * q:4 * q + 4, :], bank[q % 2][:, :].rearrange("p (t e) -> p t e", e=P)).then_inc(l_ohT, 1)
                act.wait_ge(l_sc, it + 1)
                nc.scalar.activation(score[:, :, :], score[:, :, :], ACT.Exp).then_inc(l_exp, 1)
                act.wait_ge(l_exp, it + 1)
                for h in range(2):
                    for u in range(h * HALF, (h + 1) * HALF):
                        act.wait_ge(gathered[u], 16 * (3 * IT2 + it + 1))
                    act.sem_inc(pace, 1)
                    nc.scalar.copy(rows[:, h * HALF:(h + 1) * HALF, D:D + H], score[:, h * HALF:(h + 1) * HALF, :]).then_inc(weights_in, 1)

        @block.tensor
        def _(pe):
            pe.wait_ge(consts, NCONST)
            pe.wait_ge(nat_ready, 1)
            for n in range(NG):
                if n >= 2:
                    pe.wait_ge(col_taken, n - 1)
                nc.tensor.transpose(bank[n % 2][:, 0:P], natf[:, n // TG, n % TG, :], ident32[:, :]).then_inc(col_psum, 1)
            pe.wait_ge(col_taken, NG)
            pe.sem_inc(a_used, 2)
            pe.sem_inc(p_used, 4)
            for s in range(2):
                if s:
                    pe.wait_ge(p_taken, s)
                nc.tensor.matmul(bank[6][:, 0:NB], zero16[:, 0:P], zero16[:, 0:NB], start=True, stop=False)
                with pe.Fori(0, ITS) as it:
                    for h in range(2):
                        step = 2 * (s * ITS + it) + h
                        pe.wait_ge(a_oh, step + 1)
                        for u in range(h * HALF, h * HALF + HALF):
                            mm = nc.tensor.matmul(bank[6][:, 0:NB], oloc[:, u, :], oblk[:, u, :], start=False, stop=False)
                        mm.then_inc(a_used, 1)
                nc.tensor.matmul(bank[6][:, 0:NB], zero16[:, 0:P], zero16[:, 0:NB], start=False, stop=True).then_inc(a_done, 1)
                pe.wait_ge(b_cnt, s + 1)
                nc.tensor.matmul(bank[7][:, 0:NB], ones32[:, :], cnt[:, :], start=True, stop=True).then_inc(b_tot, 1)
                nc.tensor.matmul(bank[7][:, 64:64 + NB], above32[:, :], cnt[:, :], start=True, stop=True).then_inc(b_tot, 1)
                pe.wait_ge(w_in if s == 0 else wb_in, 16)
                pe.wait_ge(w_all, 16 * 8)

                def relations(it, groups):
                    for g in groups:
                        n = 8 * (s * NB + it) + g
                        if g > 1:
                            pe.wait_ge(rel_copied, n - 1)
                        for c in range(2):
                            mm = nc.tensor.matmul(bank[6 + g % 2][:, :], hT[:, c, :], wrel[:, 2 * g:2 * g + 2, c, :], start=(c == 0), stop=(c == 1))
                        mm.then_inc(rel_psum, 1)

                with pe.Fori(0, ITS) as it:
                    for h in range(2):
                        step = 2 * (s * ITS + it) + h
                        us = range(h * HALF, h * HALF + HALF)
                        pe.wait_ge(s_oh, step + 1)
                        t16 = bank[0][:, :].bitcast(F16).rearrange("p (t e) -> p t e", e=P)
                        b16 = bank[1][:, :].bitcast(F16).rearrange("p (t e) -> p t e", e=P)
                        for u in us:
                            nc.tensor.transpose(t16[:, u % HALF, :], oloc[:, u, :], ident16[:, :])
                            mm = nc.tensor.transpose(b16[0:NB, u % HALF, :], oblk[:, u, :], ident16[:, :])
                        mm.then_inc(s_tr, 1)
                        for u in us:
                            q = u % HALF
                            mm = nc.tensor.matmul(bank[2][:, q * NB:(q + 1) * NB], oloc[:, u, :], oblk[:, u, :], start=True, stop=True)
                        mm.then_inc(s_c, 1)
                        if h == 0 and s == 0:
                            pe.wait_ge(xh_ready, it + 1)
                            for c in range(2):
                                mm = nc.tensor.transpose(bank[6][:, c * P:(c + 1) * P], xh[:, c * P:(c + 1) * P], ident32[:, :])
                            mm.then_inc(xT_psum, 1)
                        pe.wait_ge(s_trcopied, 3 * (step + 1))
                        for u in us:
                            q = u % HALF
                            o = bank[4 + q // 4][:, (q % 4) * P:(q % 4 + 1) * P]
                            nc.tensor.matmul(o, olocT16[:, u, :], olocT16[:, u, :], start=True, stop=False)
                            nc.tensor.matmul(o, oblkT[:, u, :], oblkT[:, u, :], start=False, stop=False)
                            mm = nc.tensor.matmul(o, ident16[:, :], before16[:, :], start=False, stop=True)
                        mm.then_inc(s_eq, 1)
                        pe.wait_ge(s_h, (step + 1) * HALF)
                        for u in us:
                            q = u % HALF
                            mm = nc.tensor.matmul(bank[3][:, q * NB:(q + 1) * NB], olocT32[:, u, :], hist[:, u, :], start=True, stop=True)
                        mm.then_inc(s_g, 1)
                        if h == 0 and s == 0:
                            pe.wait_ge(hT_ready, it + 1)
                            for c in range(2):
                                mm = nc.tensor.matmul(bank[7][:, 0:D], hT[:, c, :], wl[:, c, :], start=(c == 0), stop=(c == 1))
                            mm.then_inc(loop_psum, 1)
                            pe.wait_ge(self_ready, it + 1)
                        if h == 0 and s == 1:
                            pe.wait_ge(hT_in, 16 * (it + 1))
                        relations(it, range(4 * h, 4 * h + 4))
                        if h == 1:
                            pe.wait_ge(rel_copied, 8 * (s * NB + it) + 8)
                            pe.sem_inc(node_mm_done, 1)
                        pe.wait_ge(s_rk, (step + 1) * HALF)
                pe.wait_ge(s_pos, s + 1)
                for c in range(2):
                    for k in range(3):
                        nc.tensor.matmul(bank[2 * k + c][:, 0:TH], zero16[:, 0:P], zero16[:, 0:TH], start=True, stop=False)
                with pe.Fori(0, ET // 4) as it:
                    for u in range(4):
                        pe.wait_ge(p_oh, 4 * (s * (ET // 4) + it) + u + 1)
                        for k in range(3):
                            for c in range(2):
                                mm = nc.tensor.matmul(bank[2 * k + c][:, 0:TH], olo[:, u, k, :], ohi[:, u, c * TH:(c + 1) * TH], start=False, stop=False)
                        mm.then_inc(p_used, 1)
                for c in range(2):
                    for k in range(3):
                        mm = nc.tensor.matmul(bank[2 * k + c][:, 0:TH], zero16[:, 0:P], zero16[:, 0:TH], start=False, stop=True)
                mm.then_inc(p_done, 1)

            def sum_tiles(k):
                with pe.Fori(0, IT2) as it:
                    for h in range(2):
                        half = 2 * (k * IT2 + it) + h
                        for u in range(h * HALF, (h + 1) * HALF):
                            pe.wait_ge(oh_ready, HALF * half + u % HALF + 1)
                            pe.wait_ge(gathered[u], 16 * (k * IT2 + it + 1))
                            pe.wait_ge(acc_free, 16 * (k * IT2 + it) + u + 1)
                            nc.tensor.matmul(bank[u % 8][:, 0:D], oh[:, u, :], rows[:, u, 0:D], start=True, stop=True).then_inc(agg_done, 1)
                        pe.wait_ge(agg_done, 16 * (k * IT2 + it) + (h + 1) * HALF)
                        pe.sem_inc(rows_free, 1)

            for k in range(2):
                sum_tiles(k)
            with pe.Fori(0, NB) as it:
                pe.wait_ge(n_xh, it + 1)
                for c in range(2):
                    mm = nc.tensor.transpose(bank[0][:, c * P:(c + 1) * P], xh[:, c * P:(c + 1) * P], ident32[:, :])
                mm.then_inc(n_T, 1)
                pe.wait_ge(n_hT, it + 1)
                pe.wait_ge(n_used, it + 1)
                for c in range(2):
                    mm = nc.tensor.matmul(bank[1][:, 0:D + 2 * H], hT[:, c, :], w1x[:, c, :], start=(c == 0), stop=(c == 1))
                mm.then_inc(n_psum, 1)
            pe.wait_ge(gm_T, 1)
            nc.tensor.transpose(bank[2][0:H, 0:P], gmd[:, :], ident32[:, :]).then_inc(gm_mm, 1)
            pe.wait_ge(gm_T, 2)
            nc.tensor.matmul(bank[3][:, 0:1], gsel8[0:H, :], gm[0:H, :], start=True, stop=True).then_inc(gm_mm, 1)
            nc.tensor.matmul(bank[4][:, 0:H], ones32[0:H, :], gmd[0:H, :], start=True, stop=True).then_inc(gm_mm, 1)
            with pe.Fori(0, TQ) as q:
                pe.wait_ge(f_stage, q + 1)
                for j in range(2):
                    mm = nc.tensor.transpose(bank[0][:, j * P:(j + 1) * P], stg[:, j, :], ident32[:, :])
                mm.then_inc(f_T, 1)
            with pe.Fori(0, TQ) as q:
                pe.wait_ge(b_stage, q + 1)
                nc.tensor.transpose(bank[1][:, 0:P], stg[:, 0, :], ident32[:, :]).then_inc(b_T, 1)
            with pe.Fori(0, IT2) as it:
                for h in range(2):
                    pe.wait_ge(oh_ready, 16 * (2 * IT2 + it) + HALF * (h + 1))
                    for u in range(HALF):
                        mm = nc.tensor.matmul(bank[2 + h][:, u * H:(u + 1) * H], oh[:, h * HALF + u, :],
                                              smax[:, bass.ds(it * 16 * H + (h * HALF + u) * H, H)], start=True, stop=True)
                    mm.then_inc(m_psum, 1)
            pe.wait_ge(tab_ready, 1)
            with pe.Fori(0, IT2) as it:
                for q in range(4):
                    pe.wait_ge(oh_ready, 16 * (3 * IT2 + it) + 4 * (q + 1))
                    if q >= 2:
                        pe.wait_ge(l_ohT, 4 * it + q - 1)
                    for u in range(4):
                        mm = nc.tensor.transpose(bank[q % 2][:, u * P:(u + 1) * P], oh[:, 4 * q + u, :], ident32[:, :])
                    mm.then_inc(l_T, 1)
                pe.wait_ge(l_ohT, 4 * it + 4)
                for u in range(16):
                    if u % HALF == 0:
                        blks = load_blocks(mybir.EngineType.PE, 0, it * 16 + u)
                    blk = blks[u % HALF]
                    mm = nc.tensor.matmul(bank[2][:, u * 2 * H:(u + 1) * 2 * H], ohT[:, u, :],
                                          tab2[:, bass.ds(blk * 2 * H, 2 * H)], start=True, stop=True)
                mm.then_inc(l_look, 1)
                for h in range(2):
                    for u in range(h * HALF, (h + 1) * HALF):
                        pe.wait_ge(msg_ready, 16 * it + u + 1)
                        pe.wait_ge(weights_in, 2 * it + h + 1)
                        pe.wait_ge(acc_free, 16 * (2 * IT2 + it) + u + 1 - 4)
                        nc.tensor.matmul(bank[4 + u % 4][:, 0:D + H], oh[:, u, :], rows[:, u, :], start=True, stop=True).then_inc(agg_done, 1)
                    pe.wait_ge(agg_done, 16 * (2 * IT2 + it) + (h + 1) * HALF)
                    pe.sem_inc(rows_free, 1)

        @block.vector
        def _(dve):
            V = nc.vector
            link = Link(dve, dv)
            V.memset(nat[:, 1:3, :, :], 0).then_inc(dv, 1)
            link.base = 1
            link(V.memset(nat[:, 0, :, :], -1))
            V.memset(nat[:, 1, TG - 1, :], -1).then_inc(pads_set, 1)
            dve.wait_ge(loaded, 16 * 9)
            V.tensor_copy(natf[:, :, :, :], nat[:, :, :, :]).then_inc(nat_ready, 1)
            link(V.memset(eps[:, :], EPS), wait=False)
            link(V.memset(minus1[:, :], -1.0), wait=False)
            V.memset(x_all[:, NB - 1, :], 0.0).then_inc(x_all_zero, 1)

            def layer_norm_stats(blocks, n):
                with dve.Fori(0, NB // SB) as i:
                    link.loop(i, SB + 1)
                    for u in range(SB):
                        V.bn_stats(stats[:, u, :], blocks[:, bass.ds(i * SB + u, 1), :]).then_inc(stats_read, 1)
                    dve.wait_ge(stats_read, n * NB + i * SB + SB)
                    dve.sem_inc(pace, 1)
                    for u in range(SB):
                        link(V.bn_aggr(mvs[:, u, :], stats[:, u, :]), wait=u == SB - 1)
                    link(V.tensor_copy(mv[:, bass.ds(i * SB, SB), :], mvs[:, :, :]))
                link.end_loop(NB // SB)
                dve.sem_inc(var_ready, 1)
                dve.wait_ge(std_ready, n + 1)
                link(V.reciprocal(rstd[:, :], rstd[:, :]))

            dve.wait_ge(x_all_in, 32)
            layer_norm_stats(x_all, 0)
            dve.wait_ge(w_all, 16 * 8)
            for c in range(2):
                for j in range(2):
                    link(V.tensor_tensor(xh[:, :], w1x[:, c, 0:D], att_rows[:, j, :], ALU.mult))
                    link(V.tensor_reduce(w1x[:, c, D + j * H:D + (j + 1) * H], xh[:, :].rearrange("p (h f) -> p h f", h=H), AX.X, ALU.add))
            dve.sem_inc(xin_used, 1)
            dve.sem_inc(self_out, 16)
            dve.wait_ge(consts, NCONST)
            dve.wait_ge(col_taken, NG)
            for s in range(2):
                key, other = (col[:, s, 0:ET], col[:, 1 - s, 0:ET])
                ty = col[:, 2, 0:ET]
                link(V.tensor_scalar(tmpi[:, 0, :], key, 7, None, ALU.arith_shift_right), wait=False)
                link(V.tensor_scalar(tmpi[:, 1, :], key, 127, None, ALU.bitwise_and))
                link(V.tensor_copy(keyblk[:, :], tmpi[:, 0, :]), wait=False)
                link(V.tensor_copy(keyloc[:, :], tmpi[:, 1, :]))
                link(V.tensor_scalar(posf[:, :], key, 0.0, None, ALU.is_ge))
                link(V.scalar_tensor_tensor(pay[:, 0, :], keyloc[:, :], 1.0, posf[:, :], ALU.add, ALU.mult))
                link(V.scalar_tensor_tensor(pay[:, 1, :], other, 16.0, ty, ALU.mult, ALU.add))
                link(V.tensor_tensor(tmpi[:, 0, :], pay[:, 1, :], posf[:, :], ALU.mult))
                link(V.tensor_scalar(tmpi[:, 1, :], tmpi[:, 0, :], 1023, None, ALU.bitwise_and))
                link(V.tensor_copy(pay[:, 1, :], tmpi[:, 1, :]))
                link(V.tensor_scalar(tmpi[:, 1, :], tmpi[:, 0, :], 10, None, ALU.arith_shift_right))
                link(V.tensor_copy(pay[:, 2, :], tmpi[:, 1, :]))

                def one_hots(it, h, per_link):
                    q = h * HALF
                    for u in range(q, q + HALF):
                        V.tensor_scalar(oloc[:, u, :], iota_row[:, 0:P], keyloc[:, bass.ds(it * STEP + u, 1)], None, ALU.is_equal).then_inc(dv, 1)
                        link.k += 1
                    kb = keyblk[:, bass.ds(it * STEP + q, HALF)].unsqueeze(2).to_broadcast([P, HALF, NB])
                    ib = iota_row[:, 0:NB].unsqueeze(1).to_broadcast([P, HALF, NB])
                    return V.tensor_tensor(oblk[:, q:q + HALF, :], ib, kb, ALU.is_equal)

                with dve.Fori(0, ITS) as it:
                    link.loop(it, 2 * HALF + 2)
                    for h in range(2):
                        step = 2 * (s * ITS + it) + h
                        dve.wait_ge(a_used, step + 1)
                        link(one_hots(it, h, None))
                        dve.sem_inc(a_oh, 1)
                link.end_loop(ITS)
                dve.wait_ge(a_done, s + 1)
                link(V.tensor_copy(cnt[:, :], bank[6][:, 0:NB]))
                V.tensor_copy(deg[s][:, :], cnt[:, :]).then_inc(b_cnt, 1)
                dve.wait_ge(b_tot, 2 * (s + 1))
                link(V.tensor_scalar(toti[:, :], bank[7][:, 0:NB], 127.0, None, ALU.add))
                link(V.tensor_scalar(toti[:, :], toti[:, :], 7, None, ALU.arith_shift_right))
                link(V.tensor_copy(tot[:, :], toti[:, :]))
                link(V.tensor_tensor_scan(tend[:, :], tot[:, :], tot[:, :], 0.0, ALU.add, ALU.bypass))
                link(V.tensor_tensor(tot[:, :], tend[:, :], tot[:, :], ALU.subtract))
                link(V.scalar_tensor_tensor(hist[:, 0, :], tot[:, :], 128.0, bank[7][:, 64:64 + NB], ALU.mult, ALU.add))
                link(V.memset(ckb[:, :], 0.0))
                for b in range(NB - 1):
                    link(V.scalar_tensor_tensor(ckb[:, :], iota_row[:, :], tend[:, b:b + 1], ckb[:, :], ALU.is_ge, ALU.add))
                link(V.tensor_copy(sblk[s][:, :], ckb[:, :]))

                PER = 2 * (HALF + 1 + 3) + (1 if s == 0 else 0)
                with dve.Fori(0, ITS) as it:
                    link.loop(it, PER)
                    if s == 0:
                        dve.wait_ge(xin_in, 16 * (it + 1))
                        V.tensor_scalar(xh[:, :], xin[:, :], mv2[:, bass.ds(2 * it, 1)], rstd[:, bass.ds(it, 1)], ALU.subtract, ALU.mult).then_inc(xh_ready, 1)
                    for h in range(2):
                        step = 2 * (s * ITS + it) + h
                        q = h * HALF
                        link(one_hots(it, h, None))
                        dve.sem_inc(s_oh, 1)
                        dve.wait_ge(s_c, step + 1)
                        for u in range(HALF):
                            n = q + u
                            V.tensor_tensor(hist[:, (n + 1) % STEP, :], hist[:, n, :], bank[2][:, u * NB:(u + 1) * NB], ALU.add).then_inc(s_h, 1)
                            dve.wait_ge(s_h, step * HALF + u + 1)
                        dve.wait_ge(s_g, step + 1)
                        link(V.tensor_tensor(gsel[:, :, :], bank[3][:, 0:HALF * NB].rearrange("p (t b) -> p t b", b=NB), oblk[:, q:q + HALF, :], ALU.mult))
                        link(V.tensor_reduce(gs[:, :], gsel[:, :, :], AX.X, ALU.add))
                        dve.wait_ge(s_rk, (step + 1) * HALF)
                        link(V.tensor_tensor(posf[:, bass.ds(it * STEP + q, HALF)], gs[:, :], rk[:, q:q + HALF], ALU.add))
                        if h == 0 and s == 0:
                            dve.wait_ge(self_out, 16 * (it + 1))
                            link(V.tensor_tensor(selfst[:, :], xin[:, :], bias_rows[:, 0, :], ALU.add))
                            dve.sem_inc(xin_used, 1)
                            dve.wait_ge(loop_psum, it + 1)
                            V.scalar_tensor_tensor(selfst[:, :], bank[7][:, 0:D], 2.0, selfst[:, :], ALU.mult, ALU.add).then_inc(self_ready, 1)
                link.end_loop(ITS)
                link(V.tensor_copy(tmpi[:, 0, :], posf[:, :]))
                link(V.tensor_scalar(tmpi[:, 1, :], tmpi[:, 0, :], 7, None, ALU.arith_shift_right), wait=False)
                link(V.tensor_copy(posf[:, :], tmpi[:, 0, :]))
                link(V.tensor_copy(keyblk[:, :], tmpi[:, 1, :]), wait=False)
                link(V.tensor_scalar(tmpi[:, 0, :], tmpi[:, 0, :], 127, None, ALU.bitwise_and))
                link(V.tensor_copy(keyloc[:, :], tmpi[:, 0, :]))
                dve.sem_inc(s_pos, 1)
                with dve.Fori(0, ET // 4) as it:
                    for u in range(4):
                        dve.wait_ge(p_used, 4 * (s * (ET // 4) + it) + u + 1)
                        t = bass.ds(it * 4 + u, 1)
                        V.tensor_scalar(ohi[:, u, :], iota_row[:, :], keyblk[:, t], None, ALU.is_equal).then_inc(dv, 1)
                        for k in range(3):
                            V.tensor_scalar(olo[:, u, k, :], iota_row[:, 0:P], keyloc[:, t], pay[:, k, t], ALU.is_equal, ALU.mult).then_inc(dv, 1)
                        n = 16 * it + 4 * u + 4
                        dve.wait_ge(dv, link.base + link.k + n)
                        dve.sem_inc(p_oh, 1)
                link.base += 4 * ET
                dve.wait_ge(p_done, s + 1)
                for c in range(2):
                    cs = slice(c * TH, (c + 1) * TH)
                    link(V.tensor_scalar(sloc[s][:, cs], bank[c][:, 0:TH], -1.0, None, ALU.add))
                    link(V.tensor_copy(ckb[:, cs], bank[2 + c][:, 0:TH]))
                    link(V.scalar_tensor_tensor(sidx[s][:, cs], bank[4 + c][:, 0:TH], 1024.0, ckb[:, cs], ALU.mult, ALU.add))
                dve.sem_inc(p_taken, 1)
            for s in range(2):
                link(V.tensor_scalar(has[s][:, :], deg[s][:, :], 0.0, None, ALU.is_gt), wait=False)
                link(V.tensor_scalar(inv[s][:, :], deg[s][:, :], 1.0, None, ALU.max))
                link(V.reciprocal(inv[s][:, :], inv[s][:, :]))
                link(V.tensor_tensor(inv[s][:, :], inv[s][:, :], has[s][:, :], ALU.mult))
            dve.sem_inc(rows_free, 2)
            dve.sem_inc(acc_free, 8)

            def one_hots_ready(s, it, h):
                for u in range(h * HALF, (h + 1) * HALF):
                    V.tensor_scalar(oh[:, u, :], iota_row[:, 0:P], sloc[s][:, bass.ds(it * 16 + u, 1)], None, ALU.is_equal).then_inc(oh_ready, 1)

            def blocks_of(s, t):
                return load_blocks(mybir.EngineType.DVE, s, t)

            dve.wait_ge(acc_in, 16)
            for s in range(2):
                with dve.Fori(0, IT2) as it:
                    for h in range(2):
                        dve.wait_ge(rows_free, 2 * (s * IT2 + it) + h + 1)
                        dve.sem_inc(pace, 1)
                        blks = blocks_of(s, it * 16 + h * HALF)
                        one_hots_ready(s, it, h)
                        for u in range(h * HALF, (h + 1) * HALF):
                            blk = blks[u % HALF]
                            a = acc0[:, bass.ds(blk * D, D)]
                            tg = 16 * (s * IT2 + it) + u
                            dve.wait_ge(agg_done, tg + 1)
                            dve.wait_ge(acc_free, 8 + tg)
                            V.scalar_tensor_tensor(a, bank[u % 8][:, 0:D], inv[s][:, bass.ds(blk, 1)], a, ALU.mult, ALU.add).then_inc(acc_free, 1)
            dve.wait_ge(acc_free, 8 + 2 * T)
            acc3 = acc0.rearrange("p (b d) -> p b d", d=D)
            with dve.Fori(0, NB) as b:
                link.loop(b, 2)
                for s in range(2):
                    a = acc0[:, bass.ds(b * D, D)]
                    link(V.scalar_tensor_tensor(a, bias_rows[:, 1 + s, :], has[s][:, bass.ds(b, 1)], a, ALU.mult, ALU.add))
            link.end_loop(NB)
            dve.sem_inc(x1_ready, 1)
            layer_norm_stats(acc3, 1)
            link(V.tensor_scalar(sidx[0][:, :], sidx[0][:, :], 4, None, ALU.arith_shift_right))
            dve.sem_inc(idx_ready, 1)
            dve.sem_inc(n_used, 1)
            with dve.Fori(0, NB) as b:
                V.tensor_scalar(xh[:, :], acc0[:, bass.ds(b * D, D)], mv2[:, bass.ds(2 * b, 1)], rstd[:, bass.ds(b, 1)], ALU.subtract, ALU.mult).then_inc(n_xh, 1)
                dve.wait_ge(n_grow, b + 1)
                V.tensor_copy(asn[:, bass.ds(b, 1), :], grow[:, D:D + H].unsqueeze(1)).then_inc(dv, 1)
                V.tensor_copy(tab[:, bass.ds(b, 1), 0:H], grow[:, D + H:D + 2 * H].unsqueeze(1)).then_inc(dv, 1)
                dve.wait_ge(dv, link.base + link.k + 2 * b + 2)
                dve.sem_inc(n_used, 1)
            link.base += 2 * NB
            link(V.tensor_reduce(gmd[:, :], asn[:, :, :].rearrange("p b h -> p h b"), AX.X, ALU.min))
            dve.sem_inc(gm_T, 1)
            dve.wait_ge(gm_mm, 1)
            link(V.tensor_reduce(gm[0:H, :], bank[2][0:H, 0:P], AX.X, ALU.min))
            link(V.tensor_scalar(gmd[0:H, :], ident32[0:H, 0:H], gm[0:H, 0:1], None, ALU.mult))
            link(V.tensor_copy(gsel8[0:H, :].rearrange("p (k h) -> p k h", h=H), ident32[0:H, 0:H].unsqueeze(1).to_broadcast([H, P // H, H])))
            dve.sem_inc(gm_T, 1)
            dve.wait_ge(gm_mm, 3)
            link(V.tensor_copy(gmin_row[:, :], bank[4][:, 0:H]))
            link(V.tensor_scalar(gmin_part[:, :], bank[3][:, 0:1], -1.0, None, ALU.mult))
            dve.sem_inc(gm_ready, 1)
            dve.wait_ge(asrc_all, 2 * IT2)
            dve.wait_ge(x1_out, 16)
            a4 = asrc.rearrange("p (k q h) -> p q k h", q=TQ, h=H)
            l4 = sloc[0][:, :].rearrange("p (k q) -> p q k", q=TQ)
            stg4 = stg[:, :, :].rearrange("p j (q k h) -> p j q k h", q=1, h=H)
            dve.sem_inc(f_copied, 2)
            with dve.Fori(0, TQ) as q:
                dve.wait_ge(f_copied, 2 * q + 2)
                dve.sem_inc(pace, 1)
                V.tensor_copy(stg4[:, 0], a4[:, bass.ds(q, 1), :, :]).then_inc(dv, 1)
                V.tensor_copy(stg4[:, 1], l4[:, bass.ds(q, 1), :].unsqueeze(3).to_broadcast([P, 1, 16, H])).then_inc(dv, 1)
                dve.wait_ge(dv, link.base + link.k + 2 * q + 2)
                dve.sem_inc(f_stage, 1)
            link.base += 2 * TQ
            dve.wait_ge(f_copied, 2 * TQ + 2)
            l3 = locT.rearrange("p (q e) -> p q e", e=P)
            p3 = pen.rearrange("p (q e) -> p q e", e=P)
            z3 = lastT.rearrange("p (q e) -> p q e", e=P)
            link(V.memset(p3[:, :, 0:1], -BIG), wait=False)
            link(V.memset(z3[:, :, P - 1:P], 1.0), wait=False)
            link(V.tensor_tensor(z3[:, :, 0:P - 1], l3[:, :, 0:P - 1], l3[:, :, 1:P], ALU.not_equal))
            link(V.tensor_scalar(p3[:, :, 1:P], z3[:, :, 0:P - 1], -BIG, None, ALU.mult))
            link(V.tensor_tensor_scan(segmax, pen, segmax, 0.0, ALU.add, ALU.max))
            dve.sem_inc(b_copied, 1)
            with dve.Fori(0, TQ) as q:
                dve.wait_ge(b_copied, q + 1)
                dve.sem_inc(pace, 1)
                V.tensor_tensor(stg[:, 0, :], segmax[:, bass.ds(q * P, P)], lastT[:, bass.ds(q * P, P)], ALU.mult).then_inc(b_stage, 1)
            dve.wait_ge(b_copied, TQ + 1)
            link(V.memset(macc[:, :], 0.0))
            with dve.Fori(0, IT2) as it:
                for h in range(2):
                    blks = blocks_of(0, it * 16 + h * HALF)
                    one_hots_ready(0, it, h)
                    dve.wait_ge(m_psum, 2 * it + h + 1)
                    for u in range(HALF):
                        m = macc[:, bass.ds(blks[u] * H, H)]
                        V.tensor_tensor(m, m, bank[2 + h][:, u * H:(u + 1) * H], ALU.max).then_inc(m_max, 1)
                        dve.wait_ge(m_max, 16 * it + HALF * h + u + 1)
            m3 = macc[:, :].rearrange("p (b h) -> p b h", h=H)
            link(V.tensor_tensor(m3, m3, gmin_row[:, :].unsqueeze(1).to_broadcast([P, NB, H]), ALU.add))
            link(V.tensor_tensor(m3, m3, tab[:, :, 0:H], ALU.add))
            link(V.scalar_tensor_tensor(tab[:, :, H:2 * H], m3, SLOPE, m3, ALU.mult, ALU.max))
            dve.sem_inc(tab_ready, 1)
            link(V.memset(accf, 0.0))
            w8 = score[:, :, :]
            with dve.Fori(0, IT2) as it:
                link.loop(it, 4)
                for h in range(2):
                    one_hots_ready(0, it, h)
                dve.wait_ge(l_look, it + 1)
                look = bank[2][:, 0:16 * 2 * H].rearrange("p (t j) -> p t j", j=2 * H)
                link(V.tensor_tensor(w8, look[:, :, 0:H], asrc3[:, bass.ds(it * 16, 16), :], ALU.add))
                link(V.scalar_tensor_tensor(w8, w8, SLOPE, w8, ALU.mult, ALU.max))
                link(V.tensor_tensor(w8, w8, look[:, :, H:2 * H], ALU.subtract))
                link(V.tensor_scalar(w8, w8, 0.0, None, ALU.min))
                dve.sem_inc(l_sc, 1)
                dve.wait_ge(l_exp, it + 1)

                def message(u):
                    dve.wait_ge(gathered[u], 16 * (3 * IT2 + it + 1))
                    r = rows[:, u, 0:D].rearrange("p (h f) -> p h f", h=H)
                    V.tensor_tensor(r, r, score[:, u, :].unsqueeze(2).to_broadcast([P, H, F_HEAD]), ALU.mult).then_inc(msg_ready, 1)

                def add(u, blk):
                    a = accf[:, bass.ds(blk * (D + H), D + H)]
                    tg = 16 * (2 * IT2 + it) + u
                    dve.wait_ge(agg_done, tg + 1)
                    dve.wait_ge(acc_free, 8 + tg)
                    V.tensor_tensor(a, a, bank[4 + u % 4][:, 0:D + H], ALU.add).then_inc(acc_free, 1)

                for h in range(2):
                    blks = blocks_of(0, it * 16 + h * HALF)
                    for u in range(h * HALF, (h + 1) * HALF):
                        message(u)
                        if u % HALF >= 2:
                            add(u - 2, blks[u % HALF - 2])
                    add(u - 1, blks[HALF - 2])
                    add(u, blks[HALF - 1])
            link.end_loop(IT2)
            dve.wait_ge(acc_free, 8 + 3 * T)
            dve.sem_inc(fin_start, 1)
            af = accf.rearrange("p (b d) -> p b d", d=D + H)
            link(V.tensor_scalar(rden[:, :, :], af[:, :, D:D + H], TINY, None, ALU.max))
            link(V.reciprocal(rden[:, :, :], rden[:, :, :]))
            dve.wait_ge(x1_in, 16)
            groups = [(g * OB, OB) for g in range(OG)] + [(NB - 1, 1)]
            for b0, n in groups:
                for b in range(b0, b0 + n):
                    r = af[:, b, 0:D].rearrange("p (h f) -> p h f", h=H)
                    link(V.tensor_tensor(r, r, rden[:, b, :].unsqueeze(2).to_broadcast([P, H, F_HEAD]), ALU.mult), wait=False)
                    link(V.tensor_tensor(x_all[:, b, :], x_all[:, b, :], bias_rows[:, 3, :], ALU.add))
                    link(V.tensor_tensor(x_all[:, b, :], x_all[:, b, :], af[:, b, 0:D], ALU.add))
                dve.sem_inc(fin, 1)


def kernel(**inputs):
    import numpy as np
    import concourse.bacc as bacc
    from concourse.bass_utils import run_bass_kernel_spmd as run

    nc = bacc.Bacc("TRN2", target_bir_lowering=False, num_devices=1)
    arrays = {}

    def given(name):
        a = np.ascontiguousarray(inputs[name])
        arrays["in_" + name] = a
        return nc.dram_tensor("in_" + name, a.shape, mybir.dt.from_np(a.dtype), kind="ExternalInput").ap()

    xs = [given(n) for n in (
        "x", "src", "dst", "edge_type_16", "L0_gnn_Wf", "L0_gnn_Wb", "L0_gnn_loop_weight", "L0_gnn_forward_bias",
        "L0_gnn_backward_bias", "L0_gnn_self_bias", "L1_gnn_W", "L1_gnn_att_src", "L1_gnn_att_dst", "L1_gnn_bias")]
    out = nc.dram_tensor("out", inputs["x"].shape, F32, kind="ExternalOutput").ap()
    build(nc, *xs, out)
    return run(nc, [arrays], core_ids=[0]).results[0]["out"]
```

```python
from contextlib import ExitStack

import concourse.bass as bass
from concourse import mybir

F32 = mybir.dt.float32
F16 = mybir.dt.float16
BF16 = mybir.dt.bfloat16
I16 = mybir.dt.int16
I32 = mybir.dt.int32
ALU = mybir.AluOpType
ACT = mybir.ActivationFunctionType
AX = mybir.AxisListType

P = 128
EPS = 1e-05
SLOPE = 0.2
BIG = 1e30
TINY = 1e-30
NORMAL = 1024.0


class Link:

    def __init__(self, eng, sem):
        self.eng, self.sem, self.base, self.k = eng, sem, 0, 0

    def loop(self, i, per):
        self.start, self.per = self.base + self.k, per
        self.base = self.start + i * per
        self.k = 0

    def end_loop(self, n):
        assert self.k == self.per, (self.k, self.per)
        self.base, self.k = self.start + n * self.per, 0

    def __call__(self, ins, wait=True):
        ins.then_inc(self.sem, 1)
        self.k += 1
        if wait:
            self.eng.wait_ge(self.sem, self.base + self.k)


def build(nc, x, src, dst, typ, wf, wb, wloop, bf, bb, bself, w1, att_src, att_dst, b1, out):
    N, D = x.shape
    H, F_HEAD = att_src.shape
    R = wf.shape[0]
    E = src.shape[0]
    NB = -(-N // P)
    HALF = 8
    STEP = 2 * HALF
    ET = -(-E // (P * STEP)) * STEP
    ITS = ET // STEP
    EC = ET + STEP
    STEPS = 2 * ITS + 2
    TG = -(-ET // P)
    T = -(-(E // P + NB) // 16) * 16
    TH = T // 2
    TQ = T // 16
    IT2 = T // 16
    ARENA = 85120 // 4
    WREG = max(R * 2 * D, NB * D, 2 * T * H)
    SB = 7
    assert NB % SB == 0
    OB = 8
    OG = (NB - 1) // OB
    FULL = E // P
    REST = E - FULL * P

    with ExitStack() as ctx:
        def sb(name, shape, dt):
            return ctx.enter_context(nc.sbuf_tensor(name, shape, dt))

        def sem(name):
            return ctx.enter_context(nc.semaphore(name))

        bank = [ctx.enter_context(nc.psum_tensor(f"bank{i}", [P, 512], F32)) for i in range(8)]

        iota_row = sb("iota_row", [P, T], F16)
        iota_part = sb("iota_part", [P, 1], F32)
        ident16 = sb("ident16", [P, P], F16)
        ident32 = sb("ident32", [P, P], F32)
        before16 = sb("before16", [P, P], F16)
        above32 = sb("above32", [P, P], F32)
        ones32 = sb("ones32", [P, P], F32)
        ones16 = sb("ones16", [P, P], F16)
        zero16 = sb("zero16", [P, 512], F16)

        arena = sb("arena", [P, ARENA], F32)

        def carve(at, shape, dt):
            size = {F32: 4, I32: 4, F16: 2, BF16: 2, I16: 2}[dt]
            n = 1
            for d in shape:
                n *= d
            words = -(-n * size // 4)
            assert at % 4 == 0 and at // 4 + words <= ARENA, (at, words)
            v = arena[:, at // 4:at // 4 + words]
            if dt != F32:
                v = v.bitcast(dt)
            v = v[:, 0:n]
            if len(shape) == 2:
                v = v.rearrange("p (a b) -> p a b", b=shape[1])
            if len(shape) == 3:
                v = v.rearrange("p (a b c) -> p a b c", b=shape[1], c=shape[2])
            return v, at + 4 * words

        col, at = carve(0, [3, TG * P], I32)
        sort_at = at
        nat, at = carve(at, [3, TG, P], I32)
        natf, at = carve(at, [3, TG, P], F32)
        at = sort_at
        keyloc, at = carve(at, [EC], F32)
        keyblk, at = carve(at, [EC], F32)
        pay, at = carve(at, [2, ET], F32)
        tmpi, at = carve(at, [2, ET], I32)
        posf, at = carve(at, [ET], F32)
        enc_i, _ = carve(at, [ET], I16)
        enc_f, _ = carve(at, [ET], F16)
        oloc, at = carve(at, [STEP, P], F16)
        oblk, at = carve(at, [STEP, NB], F16)
        olocT16, at = carve(at, [STEP, P], F16)
        olocT32, at = carve(at, [STEP, P], F32)
        oblkT_all, at = carve(at, [STEP, P], F16)
        oblkT = oblkT_all[0:64]
        hist, at = carve(at, [STEP, NB], F32)
        gsel, at = carve(at, [HALF, NB], F32)
        gs, at = carve(at, [HALF], F32)
        equal, at = carve(at, [HALF, P], F16)
        blkT, at = carve(at, [T], F16)
        cnt, at = carve(at, [NB], F32)
        tot, at = carve(at, [NB], F32)
        toti, at = carve(at, [NB], I32)
        tend, at = carve(at, [NB], F32)
        tendT, at = carve(at, [1], F32)
        dec_i, _ = carve(at, [2, TH], I16)
        dec_f, _ = carve(at, [2, TH], F16)
        ohi, at = carve(at, [4, T], F16)
        olo, at = carve(at, [4, 2 * P], F16)
        olo = olo.rearrange("p a (k e) -> p a k e", e=P)
        ckb, at = carve(at, [T], F32)
        sort_end = at

        accf, at = carve(0, [NB * (D + H)], F32)
        rows, at = carve(at, [16, D], F32)
        acc0 = accf[:, 0:NB * D]
        oh, at = carve(at, [16, P], F32)
        ohT, at = carve(at, [16, P], F32)
        segmax, at1 = carve(0, [TQ * P], F32)
        locT, at1 = carve(at1, [TQ * P], F16)
        pen, at1 = carve(at1, [TQ * P], BF16)
        lastT, at1 = carve(at1, [TQ * P], F16)
        assert at1 <= 4 * NB * (D + H) + 4 * 16 * D

        wreg = sb("wreg", [P, WREG], F32)
        x_all = wreg[:, 0:NB * D].rearrange("p (b d) -> p b d", d=D)
        wrel = wreg[:, 0:R * 2 * D].rearrange("p (r c o) -> p r c o", c=2, o=D)
        asrc = wreg[:, 0:T * H]
        smax = wreg[:, T * H:2 * T * H]
        asrc3 = asrc.rearrange("p (t h) -> p t h", h=H)
        smax3 = smax.rearrange("p (t h) -> p t h", h=H)

        sidx = [sb(f"sidx{s}", [P, T], I32) for s in range(2)]
        sloc = [sb(f"sloc{s}", [P, T], F16) for s in range(2)]
        sblk = [sb(f"sblk{s}", [P, T], I16) for s in range(2)]
        deg = [sb(f"deg{s}", [P, NB], F32) for s in range(2)]
        inv = [sb(f"inv{s}", [P, NB], F32) for s in range(2)]
        has = [sb(f"has{s}", [P, NB], F32) for s in range(2)]

        stats = sb("stats", [P, SB, 6], F32)
        mvs = sb("mvs", [P, SB, 2], F32)
        mv = sb("mv", [P, NB, 2], F32)
        rstd = sb("rstd", [P, NB], F32)
        mv2 = mv[:, :, :].rearrange("p b j -> p (b j)")
        eps = sb("eps", [P, 1], F32)
        minus1 = sb("minus1", [P, 1], F32)
        xin = sb("xin", [P, D], F32)
        xh = sb("xh", [P, D], F32)
        hT = sb("hT", [P, 2, P], F32)
        stage = sb("stage", [P, 2, 4 * D], F32)
        wl = sb("wl", [P, 2, D], F32)
        bias_rows = sb("bias_rows", [P, 4, D], F32)
        w1x = sb("w1x", [P, 2, D + 2 * H], F32)
        grow = sb("grow", [P, D + 2 * H], F32)
        asn = sb("asn", [P, NB, H], F32)
        tab = sb("tab", [P, NB, 2 * H], F32)
        tab2 = tab[:, :, :].rearrange("p b j -> p (b j)")
        macc = sb("macc", [P, NB * H], F32)
        gm = sb("gm", [P, 1], F32)
        gmd = sb("gmd", [P, H], F32)
        att_rows = sb("att_rows", [P, 2, D], F32)
        selfst = sb("selfst", [P, D], F32)
        gsel8 = sb("gsel8", [P, P], F32)
        gmin_part = sb("gmin_part", [P, 1], F32)
        gmin_row = sb("gmin_row", [P, H], F32)
        idxst = sb("idxst", [P, 2, HALF], I32)
        ast = sb("ast", [P, 16, H], F32)
        score = sb("score", [P, 16, H], F32)
        rden = sb("rden", [P, NB, H], F32)
        stg = sb("stg", [P, 2, P], F32)

        def scratch(name, shape):
            return nc.dram_tensor(name, shape, F32, kind="Internal").ap()

        xpad = scratch("xpad", (NB * P, D))
        xself = scratch("xself", (NB * P, D))
        hTd = scratch("hTd", (NB * P, 2 * P))
        table = [scratch(f"table{s}", (NB * P * R, D)) for s in range(2)]
        x1d = scratch("x1d", (NB * P, D))
        gtab = scratch("gtab", (NB * P, D))
        stab = scratch("stab", (NB * P, H))

        consts = sem("consts")
        pads_set = sem("pads_set")
        loaded = sem("loaded")
        nat_ready = sem("nat_ready")
        col_psum = sem("col_psum")
        col_taken = sem("col_taken")
        dv = sem("dv")
        a_oh = sem("a_oh")
        a_used = sem("a_used")
        a_done = sem("a_done")
        b_cnt = sem("b_cnt")
        b_tot = sem("b_tot")
        s_oh = sem("s_oh")
        s_tr = sem("s_tr")
        s_trcopied = sem("s_trcopied")
        s_c = sem("s_c")
        s_h = sem("s_h")
        s_g = sem("s_g")
        s_eq = sem("s_eq")
        s_rk = sem("s_rk")
        s_pos = sem("s_pos")
        p_oh = sem("p_oh")
        p_used = sem("p_used")
        p_done = sem("p_done")
        p_taken = sem("p_taken")
        x_all_in = sem("x_all_in")
        x_all_zero = sem("x_all_zero")
        x_stored = sem("x_stored")
        w_in = sem("w_in")
        wb_in = sem("wb_in")
        stats_read = sem("stats_read")
        var_ready = sem("var_ready")
        std_ready = sem("std_ready")
        rstd_ready = sem("rstd_ready")
        xin_in = sem("xin_in")
        xin_used = sem("xin_used")
        xh_ready = sem("xh_ready")
        xT_psum = sem("xT_psum")
        hT_ready = sem("hT_ready")
        hT_out = sem("hT_out")
        hT_in = sem("hT_in")
        hT_again = sem("hT_again")
        loop_psum = sem("loop_psum")
        self_ready = sem("self_ready")
        self_out = sem("self_out")
        self_stored = sem("self_stored")
        rel_psum = sem("rel_psum")
        rel_copied = sem("rel_copied")
        tend_ready = sem("tend_ready")
        tend_psum = sem("tend_psum")
        tend_cmp = sem("tend_cmp")
        blk_psum = sem("blk_psum")
        blk_taken = sem("blk_taken")
        s_wide = sem("s_wide")
        s_rank = sem("s_rank")
        acc_in = sem("acc_in")
        idx_copied = sem("idx_copied")
        rows_free = sem("rows_free")
        oh_ready = sem("oh_ready")
        agg_done = sem("agg_done")
        acc_free = sem("acc_free")
        x1_ready = sem("x1_ready")
        x1_out = sem("x1_out")
        w1_in = sem("w1_in")
        w1_ready = sem("w1_ready")
        n_xh = sem("n_xh")
        n_T = sem("n_T")
        n_hT = sem("n_hT")
        n_psum = sem("n_psum")
        n_grow = sem("n_grow")
        n_out = sem("n_out")
        n_used = sem("n_used")
        gm_T = sem("gm_T")
        gm_ready = sem("gm_ready")
        gm_mm = sem("gm_mm")
        ast_copied = sem("ast_copied")
        asrc_all = sem("asrc_all")
        f_stage = sem("f_stage")
        f_T = sem("f_T")
        f_copied = sem("f_copied")
        b_stage = sem("b_stage")
        b_T = sem("b_T")
        b_copied = sem("b_copied")
        m_max = sem("m_max")
        m_psum = sem("m_psum")
        m_free = sem("m_free")
        tab_ready = sem("tab_ready")
        weights_in = sem("weights_in")
        l_T = sem("l_T")
        l_ohT = sem("l_ohT")
        l_look = sem("l_look")
        l_sc = sem("l_sc")
        l_exp = sem("l_exp")
        l_exp_used = sem("l_exp_used")
        l_msg = sem("l_msg")
        x1_in = sem("x1_in")
        fin = sem("fin")
        out_done = sem("out_done")
        ast_free = sem("ast_free")
        pace = sem("pace")
        acc_zero = sem("acc_zero")
        idx_ready = sem("idx_ready")
        node_free = sem("node_free")
        w_all = sem("w_all")
        msg_ready = sem("msg_ready")
        agg4_done = sem("agg4_done")
        fin_start = sem("fin_start")
        n_T2 = sem("n_T2")
        gathered_all = sem("gathered_all")
        gathered = [sem(f"gathered{u}") for u in range(16)]
        stage_sem = [[sem(f"table_out{s}_{j}") for j in range(2)] for s in range(2)]
        NG = TG * 3

        def load_blocks(engine, s, t):
            return nc.values_load_multi_w_load_instructions(
                sblk[s][0:1, bass.ds(t, HALF)], engines=[engine], min_val=0, max_val=NB - 1,
                skip_runtime_bounds_check_because="made from at most NB - 1 comparisons")[1]

        block = ctx.enter_context(nc.Block())

        @block.sync
        def _(sp):
            sp.wait_ge(pads_set, 1)
            g = FULL // P
            for j, a in enumerate((dst, src, typ)):
                sp.dma_start(nat[:, j, 0:g, :], a[0:g * P * P].rearrange("(g t p) -> t g p", t=P, p=P)).then_inc(loaded, 16)
                sp.dma_start(nat[0:FULL - g * P, j, g, :], a[g * P * P:FULL * P].rearrange("(t p) -> t p", p=P)).then_inc(loaded, 16)
                sp.dma_start(nat[FULL - g * P:FULL - g * P + 1, j, g, 0:REST], a[FULL * P:E].rearrange("(t p) -> t p", t=1)).then_inc(loaded, 16)
            sp.wait_ge(x_all_zero, 1)
            full_rows = (NB - 1) * P
            sp.dma_start(x_all[:, 0:NB - 1, :], x[0:full_rows, :].rearrange("(b p) d -> p b d", p=P)).then_inc(x_all_in, 16)
            sp.dma_start(x_all[0:N - full_rows, NB - 1, :], x[full_rows:N, :]).then_inc(x_all_in, 16)
            sp.dma_start(wl[:, :, :], wloop.rearrange("(c i) o -> i c o", i=P)).then_inc(w_all, 16)
            sp.dma_start(w1x[:, :, 0:D], w1.rearrange("(c i) o -> i c o", i=P)).then_inc(w_all, 16)
            for j, b in enumerate((bself, bf, bb, b1)):
                sp.dma_start(bias_rows[:, j, :], b.partition_broadcast(P)).then_inc(w_all, 16)
            for j, b in enumerate((att_src, att_dst)):
                sp.dma_start(att_rows[:, j, :], b.rearrange("h f -> (h f)").partition_broadcast(P)).then_inc(w_all, 16)
            sp.wait_ge(x_all_in, 32)
            sp.dma_start(xpad.rearrange("(b p) d -> p b d", p=P), x_all[:, :, :]).then_inc(x_stored, 16)
            sp.wait_ge(x_stored, 16)
            sp.wait_ge(stats_read, NB)
            sp.dma_start(wrel, wf.rearrange("r (c i) o -> i r c o", i=P)).then_inc(w_in, 16)

            def table_rows(s, it):
                rows_of = table[s].rearrange("(n r) d -> n (r d)", r=R)
                for j in range(4):
                    sp.wait_ge(rel_copied, 8 * (s * NB + it) + 2 * (j + 1))
                    sp.dma_start(rows_of[bass.ds(it * P, P), j * 4 * D:(j + 1) * 4 * D], stage[:, j % 2, :]).then_inc(stage_sem[s][j % 2], 16)

            with sp.Fori(0, NB) as it:
                sp.wait_ge(xin_used, it + 1)
                sp.dma_start(xin[:, :], xpad[bass.ds(it * P, P), :]).then_inc(xin_in, 16)
                sp.wait_ge(hT_ready, it + 1)
                sp.dma_start(hTd[bass.ds(it * P, P), :], hT[:, :, :].rearrange("p c n -> p (c n)")).then_inc(hT_out, 16)
                sp.wait_ge(self_ready, it + 1)
                sp.dma_start(xself[bass.ds(it * P, P), :], selfst[:, :]).then_inc(self_out, 16)
                table_rows(0, it)
            sp.wait_ge(rel_psum, 8 * NB)
            sp.dma_start(wrel, wb.rearrange("r (c i) o -> i r c o", i=P)).then_inc(wb_in, 16)
            sp.wait_ge(hT_out, 16 * (NB + 1))
            sp.wait_ge(p_taken, 2)
            sp.wait_ge(self_out, 16 * (NB + 1))
            sp.dma_start(acc0.rearrange("p (b d) -> p b d", d=D), xself.rearrange("(b p) d -> p b d", p=P)).then_inc(acc_in, 16)
            with sp.Fori(0, NB) as it:
                sp.wait_ge(hT_again, it)
                sp.dma_start(xin[:, :], hTd[bass.ds(it * P, P), :]).then_inc(hT_in, 16)
                table_rows(1, it)
            sp.wait_ge(x1_ready, 1)
            sp.dma_start(x1d.rearrange("(b p) d -> p b d", p=P), acc0.rearrange("p (b d) -> p b d", d=D)).then_inc(x1_out, 16)
            with sp.Fori(0, NB) as it:
                sp.wait_ge(n_grow, it + 1)
                sp.dma_start(gtab[bass.ds(it * P, P), :], grow[:, 0:D]).then_inc(n_out, 16)
                sp.dma_start(stab[bass.ds(it * P, P), :], grow[:, D:D + H]).then_inc(n_out, 16)
            sp.wait_ge(fin_start, 1)
            sp.wait_ge(x1_out, 16)
            sp.dma_start(x_all[:, :, :], x1d.rearrange("(b p) d -> p b d", p=P)).then_inc(x1_in, 16)
            for g in range(OG):
                sp.wait_ge(fin, g + 1)
                sp.dma_start(out[g * OB * P:(g + 1) * OB * P, :].rearrange("(b p) d -> p b d", p=P), x_all[:, g * OB:(g + 1) * OB, :]).then_inc(out_done, 16)
            sp.wait_ge(fin, OG + 1)
            sp.dma_start(out[full_rows:N, :], x_all[0:N - full_rows, NB - 1, :]).then_inc(out_done, 16)
            sp.wait_ge(out_done, 16 * (OG + 1))

        @block.gpsimd
        def _(pool):
            link = Link(pool, consts)
            pool.iota(iota_row[:, :], pattern=[[1, T]], base=0, channel_multiplier=0, allow_small_or_imprecise_dtypes=True).then_inc(consts, 1)
            pool.iota(iota_part[:, :], pattern=[[0, 1]], base=0, channel_multiplier=1, allow_small_or_imprecise_dtypes=True).then_inc(consts, 1)
            link.base = 2
            link(pool.memset(ident16[:, :], 0.0))
            link(pool.affine_select(out=ident16[:, :], in_=ident16[:, :], compare_op=ALU.not_equal, fill=1.0, base=0, pattern=[[-1, P]], channel_multiplier=1))
            link(pool.memset(ident32[:, :], 0.0))
            link(pool.affine_select(out=ident32[:, :], in_=ident32[:, :], compare_op=ALU.not_equal, fill=1.0, base=0, pattern=[[-1, P]], channel_multiplier=1))
            link(pool.memset(before16[:, :], 0.0))
            link(pool.affine_select(out=before16[:, :], in_=before16[:, :], compare_op=ALU.is_gt, fill=-1.0, base=0, pattern=[[1, P]], channel_multiplier=-1))
            link(pool.memset(above32[:, :], 1.0))
            link(pool.affine_select(out=above32[:, :], in_=above32[:, :], compare_op=ALU.is_gt, fill=0.0, base=0, pattern=[[1, P]], channel_multiplier=-1))
            link(pool.memset(ones32[:, :], 1.0))
            link(pool.memset(zero16[:, :], 0.0))
            link(pool.memset(ones16[:, :], 1.0))
            link(pool.memset(oblkT[:, :, :], 0.0))

            def gather(k, from_table, to, idx, free):
                with pool.Fori(0, IT2) as it:
                    for h in range(2):
                        half = 2 * (k * IT2 + it) + h
                        pool.wait_ge(free, half + 1)
                        pool.sem_inc(pace, 1)
                        pool.tensor_copy(idxst[:, h, :], idx[:, bass.ds(it * 16 + h * HALF, HALF)]).then_inc(idx_copied, 1)
                        pool.wait_ge(idx_copied, half + 1)
                        pool.sem_inc(pace, 1)
                        for u in range(HALF):
                            pool.indirect_dma_start(to(h * HALF + u), None, from_table,
                                                    bass.IndirectOffsetOnAxis(idxst[:, h, u:u + 1], 0)).then_inc(gathered[h * HALF + u], 16)

            for s in range(2):

                def widen(n, h):
                    pool.wait_ge(s_trcopied, 2 * (s * (STEPS - 1) + n) + 1)
                    pool.sem_inc(pace, 1)
                    hs = slice(h * HALF, (h + 1) * HALF)
                    pool.tensor_copy(olocT32[:, hs, :], olocT16[:, hs, :]).then_inc(s_wide, 1)

                widen(0, 0)
                with pool.Fori(0, ITS) as it:
                    widen(2 * it + 1, 1)
                    widen(2 * it + 2, 0)
            pool.wait_ge(p_taken, 2)
            for s in range(2):
                for q in range(2):
                    pool.wait_ge(stage_sem[s][q], 16 * (2 * NB + 1))
                gather(s, table[s], lambda u: rows[:, u, 0:D], sidx[s], rows_free)
            pool.wait_ge(n_out, 32 * NB + 32)
            pool.wait_ge(idx_ready, 1)
            gather(2, stab, lambda u: ast[:, u, :], sidx[0], rows_free)
            pool.wait_ge(b_stage, TQ)
            gather(3, gtab, lambda u: rows[:, u, :], sidx[0], rows_free)
        NCONST = 14

        @block.scalar
        def _(act):
            for n in range(NG):
                act.wait_ge(col_psum, n + 1)
                nc.scalar.copy(col[:, n // TG, (n % TG) * P:(n % TG + 1) * P], bank[n % 2][:, 0:P]).then_inc(col_taken, 1)
            act.wait_ge(var_ready, 1)
            nc.scalar.activation(rstd[:, :], mv[:, :, 1], ACT.Sqrt, bias=eps[:, 0:1]).then_inc(std_ready, 1)
            act.wait_ge(consts, NCONST)
            act.sem_inc(hT_out, 16)
            for s in range(2):
                for q in range(2):
                    act.sem_inc(stage_sem[s][q], 16)

            def relation_rows(s, it, groups, b0):
                for g in groups:
                    n = 8 * (s * NB + it) + g
                    if g % 2 == 0:
                        act.wait_ge(stage_sem[s][g // 2 % 2], 16 * (2 * it + g // 4 + 1))
                        act.sem_inc(pace, 1)
                    act.wait_ge(rel_psum, n + 1)
                    nc.scalar.copy(stage[:, g // 2 % 2, (g % 2) * 2 * D:(g % 2 + 1) * 2 * D], bank[b0 + g % 2][:, :]).then_inc(rel_copied, 1)

            for s in range(2):

                def turned(n, h):
                    hs = slice(h * HALF, (h + 1) * HALF)
                    act.wait_ge(s_tr, s * (STEPS - 1) + n + 1)
                    nc.scalar.copy(olocT16[:, hs, :], bank[0][:, :].bitcast(F16).rearrange("p (t e) -> p t e", e=P)).then_inc(s_trcopied, 1)
                    nc.scalar.copy(oblkT[0:NB, hs, :], bank[1][0:NB, :].bitcast(F16).rearrange("p (t e) -> p t e", e=P)).then_inc(s_trcopied, 1)

                if s:
                    act.wait_ge(s_wide, STEPS - 1)
                turned(0, 0)
                with act.Fori(0, ITS) as it:
                    for h in range(2):
                        n = 2 * it + h + 1
                        act.wait_ge(s_eq, s * 2 * ITS + n)
                        act.wait_ge(s_rank, s * 2 * ITS + n)
                        for c in range(2):
                            nc.scalar.activation(equal[:, 4 * c:4 * c + 4, :], bank[4 + c][:, :].rearrange("p (t e) -> p t e", e=P), ACT.Relu,
                                                 bias=minus1[:, 0:1]).then_inc(s_rk, 1)
                        turned(n, (h + 1) % 2)
                        if h == 0 and s == 0:
                            act.wait_ge(hT_out, 16 * (it + 1))
                            act.wait_ge(xT_psum, it + 1)
                            nc.scalar.activation(hT[:, :, :], bank[6][:, 0:2 * P].rearrange("p (c n) -> p c n", n=P), ACT.Relu).then_inc(hT_ready, 1)
                        if s == 0:
                            relation_rows(0, it, range(4 * h, 4 * h + 4), 6)
            with act.Fori(0, NB) as it:
                act.wait_ge(hT_in, 16 * (it + 1))
                act.wait_ge(rel_psum, 8 * (NB + it))
                nc.scalar.copy(hT[:, :, :].rearrange("p c n -> p (c n)"), xin[:, :]).then_inc(hT_again, 1)
                relation_rows(1, it, range(8), 0)
            act.wait_ge(var_ready, 2)
            nc.scalar.activation(rstd[:, :], mv[:, :, 1], ACT.Sqrt, bias=eps[:, 0:1]).then_inc(std_ready, 1)
            act.sem_inc(n_out, 32)
            with act.Fori(0, NB) as it:
                act.wait_ge(n_T, it + 1)
                nc.scalar.activation(hT[:, :, :], bank[0][:, 0:2 * P].rearrange("p (c n) -> p c n", n=P), ACT.Relu).then_inc(n_hT, 1)
                act.wait_ge(n_out, 32 * (it + 1))
                act.sem_inc(pace, 1)
                act.wait_ge(n_psum, it + 1)
                nc.scalar.copy(grow[:, :], bank[1][:, 0:D + 2 * H]).then_inc(n_grow, 1)
            with act.Fori(0, IT2) as it:
                for h in range(2):
                    for u in range(h * HALF, (h + 1) * HALF):
                        act.wait_ge(gathered[u], 16 * (2 * IT2 + it + 1))
                    act.sem_inc(pace, 1)
                    nc.scalar.copy(asrc[:, bass.ds(it * 16 * H + h * HALF * H, HALF * H)],
                                   ast[:, h * HALF:(h + 1) * HALF, :].rearrange("p t h -> p (t h)")).then_inc(asrc_all, 1)
                    act.wait_ge(asrc_all, 2 * it + h + 1)
                    act.sem_inc(rows_free, 1)
            act.wait_ge(gm_ready, 1)
            with act.Fori(0, TQ) as q:
                act.wait_ge(f_T, q + 1)
                act.sem_inc(pace, 1)
                nc.scalar.activation(segmax[:, bass.ds(q * P, P)], bank[0][:, 0:P], ACT.Identity, bias=gmin_part[:, 0:1]).then_inc(f_copied, 1)
                nc.scalar.copy(locT[:, bass.ds(q * P, P)], bank[0][:, P:2 * P]).then_inc(f_copied, 1)
            with act.Fori(0, TQ) as q:
                act.wait_ge(b_T, q + 1)
                act.sem_inc(pace, 1)
                nc.scalar.copy(smax.rearrange("p (k q h) -> p q k h", q=TQ, h=H)[:, bass.ds(q, 1), :, :],
                               bank[1][:, 0:P].rearrange("p (q k h) -> p q k h", q=1, h=H)).then_inc(b_copied, 1)
            with act.Fori(0, IT2) as it:
                for h in range(2):
                    for q in range(2):
                        act.wait_ge(l_T, 2 * (2 * it + h) + q + 1)
                        nc.scalar.copy(ohT[:, h * HALF + 4 * q:h * HALF + 4 * q + 4, :], bank[q][:, :].rearrange("p (t e) -> p t e", e=P)).then_inc(l_ohT, 1)
                    act.wait_ge(l_sc, 2 * it + h + 1)
                    w8 = score[:, h * HALF:(h + 1) * HALF, :]
                    nc.scalar.activation(w8, w8, ACT.Exp).then_inc(l_exp, 1)

        @block.tensor
        def _(pe):
            pe.wait_ge(consts, NCONST)
            pe.wait_ge(nat_ready, 1)
            for n in range(NG):
                if n >= 2:
                    pe.wait_ge(col_taken, n - 1)
                nc.tensor.transpose(bank[n % 2][:, 0:P], natf[:, n // TG, n % TG, :], ident32[:, :]).then_inc(col_psum, 1)
            pe.wait_ge(col_taken, NG)

            def relations(s, it, groups, b0):
                for g in groups:
                    n = 8 * (s * NB + it) + g
                    if g > 1 or s == 1:
                        pe.wait_ge(rel_copied, n - 1)
                    for c in range(2):
                        mm = nc.tensor.matmul(bank[b0 + g % 2][:, :], hT[:, c, :], wrel[:, 2 * g:2 * g + 2, c, :], start=(c == 0), stop=(c == 1))
                    mm.then_inc(rel_psum, 1)

            pe.sem_inc(a_used, 2)
            pe.sem_inc(p_used, 4)
            for s in range(2):
                if s:
                    pe.wait_ge(p_taken, s)
                nc.tensor.matmul(bank[6][:, 0:NB], zero16[:, 0:P], zero16[:, 0:NB], start=True, stop=False)
                with pe.Fori(0, ITS) as it:
                    for h in range(2):
                        step = 2 * (s * ITS + it) + h
                        pe.wait_ge(a_oh, (HALF + 1) * (step + 1))
                        for u in range(h * HALF, h * HALF + HALF):
                            mm = nc.tensor.matmul(bank[6][:, 0:NB], oloc[:, u, :], oblk[:, u, :], start=False, stop=False)
                        mm.then_inc(a_used, 1)
                nc.tensor.matmul(bank[6][:, 0:NB], zero16[:, 0:P], zero16[:, 0:NB], start=False, stop=True).then_inc(a_done, 1)
                pe.wait_ge(b_cnt, s + 1)
                nc.tensor.matmul(bank[7][:, 0:NB], ones32[:, :], cnt[:, :], start=True, stop=True).then_inc(b_tot, 1)
                nc.tensor.matmul(bank[7][:, 64:64 + NB], above32[:, :], cnt[:, :], start=True, stop=True).then_inc(b_tot, 1)
                pe.wait_ge(tend_ready, s + 1)
                nc.tensor.transpose(bank[4][0:NB, 0:P], tend[:, :], ident32[:, :]).then_inc(tend_psum, 1)
                pe.wait_ge(tend_cmp, s + 1)
                for c in range(2):
                    mm = nc.tensor.matmul(bank[4 + c][:, 0:TH], ones16[0:NB - 1, :], blkT[0:NB - 1, c * TH:(c + 1) * TH], start=True, stop=True)
                mm.then_inc(blk_psum, 1)
                pe.wait_ge(blk_taken, 2 * (s + 1))

                def turn(n, h):
                    pe.wait_ge(s_oh, (HALF + 1) * (s * STEPS + n + 1))
                    t16 = bank[0][:, :].bitcast(F16).rearrange("p (t e) -> p t e", e=P)
                    b16 = bank[1][:, :].bitcast(F16).rearrange("p (t e) -> p t e", e=P)
                    for u in range(HALF):
                        nc.tensor.transpose(t16[:, u, :], oloc[:, h * HALF + u, :], ident16[:, :])
                        mm = nc.tensor.transpose(b16[0:NB, u, :], oblk[:, h * HALF + u, :], ident16[:, :])
                    mm.then_inc(s_tr, 1)
                    for u in range(HALF):
                        mm = nc.tensor.matmul(bank[2][:, u * NB:(u + 1) * NB], oloc[:, h * HALF + u, :], oblk[:, h * HALF + u, :], start=True, stop=True)
                    mm.then_inc(s_c, 1)

                turn(0, 0)
                if s == 0:
                    pe.wait_ge(w_in, 16)
                    pe.wait_ge(w_all, 16 * 8)
                    pe.sem_inc(s_rank, 1)
                with pe.Fori(0, ITS) as it:
                    for h in range(2):
                        n = 2 * it + h + 1
                        pe.wait_ge(s_trcopied, 2 * (s * (STEPS - 1) + n))
                        for u in range(HALF):
                            o = bank[4 + u // 4][:, (u % 4) * P:(u % 4 + 1) * P]
                            q = h * HALF + u
                            nc.tensor.matmul(o, olocT16[:, q, :], olocT16[:, q, :], start=True, stop=False)
                            nc.tensor.matmul(o, oblkT[:, q, :], oblkT[:, q, :], start=False, stop=False)
                            mm = nc.tensor.matmul(o, ident16[:, :], before16[:, :], start=False, stop=True)
                        mm.then_inc(s_eq, 1)
                        pe.wait_ge(s_h, HALF * (s * (STEPS - 1) + n))
                        turn(n, (h + 1) % 2)
                        if h == 0 and s == 0:
                            pe.wait_ge(xh_ready, it + 1)
                            for c in range(2):
                                mm = nc.tensor.transpose(bank[6][:, c * P:(c + 1) * P], xh[:, c * P:(c + 1) * P], ident32[:, :])
                            mm.then_inc(xT_psum, 1)
                        pe.wait_ge(s_wide, s * (STEPS - 1) + n)
                        for u in range(HALF):
                            q = h * HALF + u
                            nc.tensor.matmul(bank[3][:, u * NB:(u + 1) * NB], olocT32[:, q, :], hist[:, q, :], start=True, stop=True)
                        pe.wait_ge(s_rk, 2 * (s * 2 * ITS + n))
                        for u in range(HALF):
                            c = HALF * NB + u
                            mm = nc.tensor.matmul(bank[3][:, c:c + 1], equal[:, u, :], ones16[:, 0:1], start=True, stop=True)
                        mm.then_inc(s_g, 1)
                        pe.sem_inc(s_rank, 1)
                        if h == 0 and s == 0:
                            pe.wait_ge(hT_ready, it + 1)
                            for c in range(2):
                                mm = nc.tensor.matmul(bank[7][:, 0:D], hT[:, c, :], wl[:, c, :], start=(c == 0), stop=(c == 1))
                            mm.then_inc(loop_psum, 1)
                            pe.wait_ge(self_ready, it + 1)
                        if s == 0:
                            relations(0, it, range(4 * h, 4 * h + 4), 6)
                            if h == 1:
                                pe.wait_ge(rel_copied, 8 * (it + 1))
                pe.wait_ge(s_pos, s + 1)
                pe.wait_ge(s_trcopied, 2 * (s + 1) * (STEPS - 1))
                for c in range(2):
                    for k in range(2):
                        nc.tensor.matmul(bank[2 * k + c][:, 0:TH], zero16[:, 0:P], zero16[:, 0:TH], start=True, stop=False)
                with pe.Fori(0, ET // 4) as it:
                    for u in range(4):
                        pe.wait_ge(p_oh, 3 * (4 * (s * (ET // 4) + it) + u + 1))
                        for k in range(2):
                            for c in range(2):
                                mm = nc.tensor.matmul(bank[2 * k + c][:, 0:TH], olo[:, u, k, :], ohi[:, u, c * TH:(c + 1) * TH], start=False, stop=False)
                        mm.then_inc(p_used, 1)
                for c in range(2):
                    for k in range(2):
                        mm = nc.tensor.matmul(bank[2 * k + c][:, 0:TH], zero16[:, 0:P], zero16[:, 0:TH], start=False, stop=True)
                mm.then_inc(p_done, 1)

            def sum_tiles(k, it, nodes):
                for h in range(2):
                    half = 2 * (k * IT2 + it) + h
                    for u in range(h * HALF, (h + 1) * HALF):
                        pe.wait_ge(oh_ready, HALF * half + u % HALF + 1)
                        pe.wait_ge(gathered[u], 16 * (k * IT2 + it + 1))
                        pe.wait_ge(acc_free, 16 * (k * IT2 + it) + u + 1)
                        nc.tensor.matmul(bank[4 + u % 4][:, 0:D], oh[:, u, :], rows[:, u, 0:D], start=True, stop=True).then_inc(agg_done, 1)
                        if nodes and u % 2:
                            relations(1, it, [u // 2], 0)
                    pe.wait_ge(agg_done, 16 * (k * IT2 + it) + (h + 1) * HALF)
                    pe.sem_inc(rows_free, 1)

            pe.wait_ge(wb_in, 16)
            with pe.Fori(0, NB) as it:
                pe.wait_ge(hT_again, it + 1)
                sum_tiles(0, it, True)
            with pe.Fori(NB, IT2) as it:
                sum_tiles(0, it, False)
            with pe.Fori(0, IT2) as it:
                sum_tiles(1, it, False)
            with pe.Fori(0, NB) as it:
                pe.wait_ge(n_xh, it + 1)
                for c in range(2):
                    mm = nc.tensor.transpose(bank[0][:, c * P:(c + 1) * P], xh[:, c * P:(c + 1) * P], ident32[:, :])
                mm.then_inc(n_T, 1)
                pe.wait_ge(n_hT, it + 1)
                pe.wait_ge(n_used, it + 1)
                for c in range(2):
                    mm = nc.tensor.matmul(bank[1][:, 0:D + 2 * H], hT[:, c, :], w1x[:, c, :], start=(c == 0), stop=(c == 1))
                mm.then_inc(n_psum, 1)
            pe.wait_ge(gm_T, 1)
            nc.tensor.transpose(bank[2][0:H, 0:P], gmd[:, :], ident32[:, :]).then_inc(gm_mm, 1)
            pe.wait_ge(gm_T, 2)
            nc.tensor.matmul(bank[3][:, 0:1], gsel8[0:H, :], gm[0:H, :], start=True, stop=True).then_inc(gm_mm, 1)
            nc.tensor.matmul(bank[4][:, 0:H], ones32[0:H, :], gmd[0:H, :], start=True, stop=True).then_inc(gm_mm, 1)
            with pe.Fori(0, TQ) as q:
                pe.wait_ge(f_stage, q + 1)
                for j in range(2):
                    mm = nc.tensor.transpose(bank[0][:, j * P:(j + 1) * P], stg[:, j, :], ident32[:, :])
                mm.then_inc(f_T, 1)
            with pe.Fori(0, TQ) as q:
                pe.wait_ge(b_stage, q + 1)
                nc.tensor.transpose(bank[1][:, 0:P], stg[:, 0, :], ident32[:, :]).then_inc(b_T, 1)
            with pe.Fori(0, IT2) as it:
                for h in range(2):
                    pe.wait_ge(oh_ready, 16 * (2 * IT2 + it) + HALF * (h + 1))
                    for u in range(HALF):
                        mm = nc.tensor.matmul(bank[2 + h][:, u * H:(u + 1) * H], oh[:, h * HALF + u, :],
                                              smax[:, bass.ds(it * 16 * H + (h * HALF + u) * H, H)], start=True, stop=True)
                    mm.then_inc(m_psum, 1)
            pe.wait_ge(tab_ready, 1)

            def turn_one_hots(it, h, q):
                pe.wait_ge(oh_ready, 16 * (3 * IT2 + it) + HALF * h + 4 * (q + 1))
                for u in range(4):
                    mm = nc.tensor.transpose(bank[q][:, u * P:(u + 1) * P], oh[:, h * HALF + 4 * q + u, :], ident32[:, :])
                mm.then_inc(l_T, 1)

            def look_up(it, h, blks):
                pe.wait_ge(l_ohT, 2 * (2 * it + h) + 2)
                for u in range(HALF):
                    mm = nc.tensor.matmul(bank[2 + h][:, u * 2 * H:(u + 1) * 2 * H], ohT[:, h * HALF + u, :],
                                          tab2[:, bass.ds(blks[u] * 2 * H, 2 * H)], start=True, stop=True)
                mm.then_inc(l_look, 1)

            def sum_messages(it, last):
                for h in range(2):
                    ahead = not (last and h)
                    if ahead:
                        blks = load_blocks(mybir.EngineType.PE, 0, (it + h) * 16 + (1 - h) * HALF)
                    for j in range(HALF):
                        u = h * HALF + j
                        pe.wait_ge(msg_ready, 16 * it + u + 1)
                        pe.wait_ge(acc_free, 16 * (2 * IT2 + it) + u + 1)
                        nc.tensor.matmul(bank[4 + u % 4][:, 0:D], oh[:, u, :], rows[:, u, 0:D], start=True, stop=True)
                        nc.tensor.matmul(bank[4 + u % 4][:, D:D + H], oh[:, u, :], score[:, u, :], start=True, stop=True).then_inc(agg_done, 1)
                        if ahead and j in (1, 3):
                            turn_one_hots(it + h, 1 - h, j // 2)
                        if ahead and j == 5:
                            look_up(it + h, 1 - h, blks)
                    pe.wait_ge(agg_done, 16 * (2 * IT2 + it) + (h + 1) * HALF)
                    pe.sem_inc(rows_free, 1)

            first_blks = load_blocks(mybir.EngineType.PE, 0, 0)
            turn_one_hots(0, 0, 0)
            turn_one_hots(0, 0, 1)
            look_up(0, 0, first_blks)
            with pe.Fori(0, IT2 - 1) as it:
                sum_messages(it, False)
            sum_messages(IT2 - 1, True)

        @block.vector
        def _(dve):
            V = nc.vector
            link = Link(dve, dv)
            V.memset(nat[:, 1:3, :, :], 0).then_inc(dv, 1)
            link.base = 1
            link(V.memset(nat[:, 0, :, :], -1))
            V.memset(nat[:, 1, TG - 1, :], -1).then_inc(pads_set, 1)
            dve.wait_ge(loaded, 16 * 9)
            V.tensor_copy(natf[:, :, :, :], nat[:, :, :, :]).then_inc(nat_ready, 1)
            link(V.memset(eps[:, :], EPS), wait=False)
            link(V.memset(minus1[:, :], -1.0), wait=False)
            V.memset(x_all[:, NB - 1, :], 0.0).then_inc(x_all_zero, 1)

            def layer_norm_stats(blocks, n):
                with dve.Fori(0, NB // SB) as i:
                    link.loop(i, SB + 1)
                    for u in range(SB):
                        V.bn_stats(stats[:, u, :], blocks[:, bass.ds(i * SB + u, 1), :]).then_inc(stats_read, 1)
                    dve.wait_ge(stats_read, n * NB + i * SB + SB)
                    dve.sem_inc(pace, 1)
                    for u in range(SB):
                        link(V.bn_aggr(mvs[:, u, :], stats[:, u, :]), wait=u == SB - 1)
                    link(V.tensor_copy(mv[:, bass.ds(i * SB, SB), :], mvs[:, :, :]))
                link.end_loop(NB // SB)
                dve.sem_inc(var_ready, 1)
                dve.wait_ge(std_ready, n + 1)
                link(V.reciprocal(rstd[:, :], rstd[:, :]))

            dve.wait_ge(x_all_in, 32)
            layer_norm_stats(x_all, 0)
            dve.wait_ge(w_all, 16 * 8)
            for c in range(2):
                for j in range(2):
                    link(V.tensor_tensor(xh[:, :], w1x[:, c, 0:D], att_rows[:, j, :], ALU.mult))
                    link(V.tensor_reduce(w1x[:, c, D + j * H:D + (j + 1) * H], xh[:, :].rearrange("p (h f) -> p h f", h=H), AX.X, ALU.add))
            dve.sem_inc(xin_used, 1)
            dve.sem_inc(self_out, 16)
            dve.wait_ge(consts, NCONST)
            dve.wait_ge(col_taken, NG)
            for s in range(2):
                key, other = (col[:, s, 0:ET], col[:, 1 - s, 0:ET])
                link(V.memset(keyblk[:, ET:EC], -1.0), wait=False)
                link(V.memset(keyloc[:, ET:EC], 0.0), wait=False)
                ty = col[:, 2, 0:ET]
                link(V.tensor_scalar(tmpi[:, 0, :], key, 7, None, ALU.arith_shift_right), wait=False)
                link(V.tensor_scalar(tmpi[:, 1, :], key, 127, None, ALU.bitwise_and))
                link(V.tensor_copy(keyblk[:, 0:ET], tmpi[:, 0, :]), wait=False)
                link(V.tensor_copy(keyloc[:, 0:ET], tmpi[:, 1, :]))
                link(V.tensor_scalar(posf[:, :], key, 0.0, None, ALU.is_ge))
                link(V.scalar_tensor_tensor(pay[:, 1, :], other, 16.0, ty, ALU.mult, ALU.add))
                link(V.tensor_tensor(tmpi[:, 0, :], pay[:, 1, :], posf[:, :], ALU.mult))
                link(V.tensor_scalar(tmpi[:, 1, :], tmpi[:, 0, :], 7, None, ALU.arith_shift_right))
                link(V.tensor_scalar(enc_i, tmpi[:, 1, :], NORMAL, None, ALU.add))
                link(V.tensor_tensor(pay[:, 1, :], enc_f, posf[:, :], ALU.mult))
                link(V.tensor_scalar(tmpi[:, 1, :], tmpi[:, 0, :], 127, None, ALU.bitwise_and))
                link(V.tensor_scalar(pay[:, 0, :], keyloc[:, 0:ET], 128.0, NORMAL, ALU.mult, ALU.add))
                link(V.tensor_tensor(enc_i, pay[:, 0, :], tmpi[:, 1, :], ALU.add))
                link(V.tensor_tensor(pay[:, 0, :], enc_f, posf[:, :], ALU.mult))

                def local_one_hots(t, h, done):
                    for u in range(HALF):
                        V.tensor_scalar(oloc[:, h * HALF + u, :], iota_row[:, 0:P], keyloc[:, bass.ds(t + u, 1)], None, ALU.is_equal).then_inc(done, 1)

                def block_one_hots(t, h, done):
                    kb = keyblk[:, bass.ds(t, HALF)].unsqueeze(2).to_broadcast([P, HALF, NB])
                    ib = iota_row[:, 0:NB].unsqueeze(1).to_broadcast([P, HALF, NB])
                    V.tensor_tensor(oblk[:, h * HALF:(h + 1) * HALF, :], ib, kb, ALU.is_equal).then_inc(done, 1)

                with dve.Fori(0, ITS) as it:
                    for h in range(2):
                        dve.wait_ge(a_used, 2 * (s * ITS + it) + h + 1)
                        dve.sem_inc(pace, 1)
                        local_one_hots(it * STEP + h * HALF, h, a_oh)
                        block_one_hots(it * STEP + h * HALF, h, a_oh)
                dve.wait_ge(a_done, s + 1)
                link(V.tensor_copy(cnt[:, :], bank[6][:, 0:NB]))
                V.tensor_copy(deg[s][:, :], cnt[:, :]).then_inc(b_cnt, 1)
                dve.wait_ge(b_tot, 2 * (s + 1))
                link(V.tensor_scalar(toti[:, :], bank[7][:, 0:NB], 127.0, None, ALU.add))
                link(V.tensor_scalar(toti[:, :], toti[:, :], 7, None, ALU.arith_shift_right))
                link(V.tensor_copy(tot[:, :], toti[:, :]))
                link(V.tensor_tensor_scan(tend[:, :], tot[:, :], tot[:, :], 0.0, ALU.add, ALU.bypass))
                link(V.tensor_tensor(tot[:, :], tend[:, :], tot[:, :], ALU.subtract))
                link(V.scalar_tensor_tensor(hist[:, 0, :], tot[:, :], 128.0, bank[7][:, 64:64 + NB], ALU.mult, ALU.add))
                dve.sem_inc(tend_ready, 1)
                dve.wait_ge(tend_psum, s + 1)
                link(V.tensor_copy(tendT[0:NB, :], bank[4][0:NB, 0:1]))
                V.tensor_scalar(blkT[0:NB, :], iota_row[0:NB, :], tendT[0:NB, 0:1], None, ALU.is_ge).then_inc(tend_cmp, 1)
                dve.wait_ge(blk_psum, s + 1)
                for c in range(2):
                    V.tensor_copy(sblk[s][:, c * TH:(c + 1) * TH], bank[4 + c][:, 0:TH]).then_inc(blk_taken, 1)

                def count_on(n, h, first=False):
                    for u in range(HALF):
                        q = h * HALF + u
                        if u or not first:
                            dve.wait_ge(s_h, HALF * (s * (STEPS - 1) + n) + u)
                        V.tensor_tensor(hist[:, (q + 1) % STEP, :], hist[:, q, :], bank[2][:, u * NB:(u + 1) * NB], ALU.add).then_inc(s_h, 1)

                for n in range(2):
                    local_one_hots(n * HALF, n, s_oh)
                    block_one_hots(n * HALF, n, s_oh)
                dve.wait_ge(s_c, s * (STEPS - 1) + 1)
                count_on(0, 0, first=s == 0)
                with dve.Fori(0, ITS) as it:
                    link.loop(it, 2 * 3 + (1 if s == 0 else 0))
                    if s == 0:
                        dve.wait_ge(xin_in, 16 * (it + 1))
                        V.tensor_scalar(xh[:, :], xin[:, :], mv2[:, bass.ds(2 * it, 1)], rstd[:, bass.ds(it, 1)], ALU.subtract, ALU.mult).then_inc(xh_ready, 1)
                    for h in range(2):
                        n = 2 * it + h + 1
                        local_one_hots(it * STEP + (h + 2) * HALF, h, s_oh)
                        dve.wait_ge(s_g, s * 2 * ITS + n)
                        link(V.tensor_tensor(gsel[:, :, :], bank[3][:, 0:HALF * NB].rearrange("p (t b) -> p t b", b=NB), oblk[:, h * HALF:(h + 1) * HALF, :], ALU.mult))
                        block_one_hots(it * STEP + (h + 2) * HALF, h, s_oh)
                        link(V.tensor_reduce(gs[:, :], gsel[:, :, :], AX.X, ALU.add))
                        link(V.tensor_tensor(posf[:, bass.ds(it * STEP + h * HALF, HALF)], gs[:, :], bank[3][:, HALF * NB:HALF * (NB + 1)], ALU.add))
                        dve.wait_ge(s_c, s * (STEPS - 1) + n + 1)
                        count_on(n, (h + 1) % 2)
                        if h == 0 and s == 0:
                            dve.wait_ge(self_out, 16 * (it + 1))
                            link(V.tensor_tensor(selfst[:, :], xin[:, :], bias_rows[:, 0, :], ALU.add))
                            dve.sem_inc(xin_used, 1)
                            dve.wait_ge(loop_psum, it + 1)
                            V.scalar_tensor_tensor(selfst[:, :], bank[7][:, 0:D], 2.0, selfst[:, :], ALU.mult, ALU.add).then_inc(self_ready, 1)
                link.end_loop(ITS)
                link(V.tensor_copy(tmpi[:, 0, :], posf[:, :]))
                link(V.tensor_scalar(tmpi[:, 1, :], tmpi[:, 0, :], 7, None, ALU.arith_shift_right), wait=False)
                link(V.tensor_copy(posf[:, :], tmpi[:, 0, :]))
                link(V.tensor_copy(keyblk[:, 0:ET], tmpi[:, 1, :]), wait=False)
                link(V.tensor_scalar(tmpi[:, 0, :], tmpi[:, 0, :], 127, None, ALU.bitwise_and))
                link(V.tensor_copy(keyloc[:, 0:ET], tmpi[:, 0, :]))
                dve.sem_inc(s_pos, 1)
                with dve.Fori(0, ET // 4) as it:
                    for u in range(4):
                        dve.wait_ge(p_used, 4 * (s * (ET // 4) + it) + u + 1)
                        t = bass.ds(it * 4 + u, 1)
                        dve.sem_inc(pace, 1)
                        V.tensor_scalar(ohi[:, u, :], iota_row[:, :], keyblk[:, t], None, ALU.is_equal).then_inc(p_oh, 1)
                        for k in range(2):
                            V.tensor_scalar(olo[:, u, k, :], iota_row[:, 0:P], keyloc[:, t], pay[:, k, t], ALU.is_equal, ALU.mult).then_inc(p_oh, 1)
                dve.wait_ge(p_done, s + 1)
                for c in range(2):
                    cs = slice(c * TH, (c + 1) * TH)
                    link(V.tensor_copy(dec_f[:, 0, :], bank[c][:, 0:TH]), wait=False)
                    link(V.tensor_copy(dec_f[:, 1, :], bank[2 + c][:, 0:TH]))
                    link(V.tensor_scalar(tmpi[:, 0, 0:TH], dec_i[:, 0, :], -NORMAL, None, ALU.add))
                    link(V.tensor_scalar(tmpi[:, 1, 0:TH], tmpi[:, 0, 0:TH], 7, None, ALU.arith_shift_right))
                    link(V.tensor_scalar(sloc[s][:, cs], tmpi[:, 1, 0:TH], -1.0, None, ALU.max))
                    link(V.tensor_scalar(tmpi[:, 1, 0:TH], tmpi[:, 0, 0:TH], 127, None, ALU.bitwise_and))
                    link(V.tensor_scalar(ckb[:, cs], dec_i[:, 1, :], -NORMAL, 0.0, ALU.add, ALU.max))
                    link(V.scalar_tensor_tensor(sidx[s][:, cs], ckb[:, cs], 128.0, tmpi[:, 1, 0:TH], ALU.mult, ALU.add))
                dve.wait_ge(s_wide, (s + 1) * (STEPS - 1))
                dve.sem_inc(p_taken, 1)
            for s in range(2):
                link(V.tensor_scalar(has[s][:, :], deg[s][:, :], 0.0, None, ALU.is_gt), wait=False)
                link(V.tensor_scalar(inv[s][:, :], deg[s][:, :], 1.0, None, ALU.max))
                link(V.reciprocal(inv[s][:, :], inv[s][:, :]))
                link(V.tensor_tensor(inv[s][:, :], inv[s][:, :], has[s][:, :], ALU.mult))
            dve.sem_inc(rows_free, 2)
            dve.sem_inc(acc_free, 4)

            def one_hots_ready(s, it, h, first=0, end=HALF):
                for u in range(h * HALF + first, h * HALF + end):
                    V.tensor_scalar(oh[:, u, :], iota_row[:, 0:P], sloc[s][:, bass.ds(it * 16 + u, 1)], None, ALU.is_equal).then_inc(oh_ready, 1)

            def blocks_of(s, t):
                return load_blocks(mybir.EngineType.DVE, s, t)

            dve.wait_ge(acc_in, 16)
            for s in range(2):
                with dve.Fori(0, IT2) as it:
                    for h in range(2):
                        dve.wait_ge(rows_free, 2 * (s * IT2 + it) + h + 1)
                        dve.sem_inc(pace, 1)
                        blks = blocks_of(s, it * 16 + h * HALF)
                        one_hots_ready(s, it, h)
                        for u in range(h * HALF, (h + 1) * HALF):
                            blk = blks[u % HALF]
                            a = acc0[:, bass.ds(blk * D, D)]
                            tg = 16 * (s * IT2 + it) + u
                            dve.wait_ge(agg_done, tg + 1)
                            dve.wait_ge(acc_free, 4 + tg)
                            V.scalar_tensor_tensor(a, bank[4 + u % 4][:, 0:D], inv[s][:, bass.ds(blk, 1)], a, ALU.mult, ALU.add).then_inc(acc_free, 1)
            dve.wait_ge(acc_free, 4 + 2 * T)
            acc3 = acc0.rearrange("p (b d) -> p b d", d=D)
            with dve.Fori(0, NB) as b:
                link.loop(b, 2)
                for s in range(2):
                    a = acc0[:, bass.ds(b * D, D)]
                    link(V.scalar_tensor_tensor(a, bias_rows[:, 1 + s, :], has[s][:, bass.ds(b, 1)], a, ALU.mult, ALU.add))
            link.end_loop(NB)
            dve.sem_inc(x1_ready, 1)
            layer_norm_stats(acc3, 1)
            link(V.tensor_scalar(sidx[0][:, :], sidx[0][:, :], 4, None, ALU.arith_shift_right))
            dve.sem_inc(idx_ready, 1)
            dve.sem_inc(n_used, 1)
            with dve.Fori(0, NB) as b:
                V.tensor_scalar(xh[:, :], acc0[:, bass.ds(b * D, D)], mv2[:, bass.ds(2 * b, 1)], rstd[:, bass.ds(b, 1)], ALU.subtract, ALU.mult).then_inc(n_xh, 1)
                dve.wait_ge(n_grow, b + 1)
                V.tensor_copy(asn[:, bass.ds(b, 1), :], grow[:, D:D + H].unsqueeze(1)).then_inc(dv, 1)
                V.tensor_copy(tab[:, bass.ds(b, 1), 0:H], grow[:, D + H:D + 2 * H].unsqueeze(1)).then_inc(dv, 1)
                dve.wait_ge(dv, link.base + link.k + 2 * b + 2)
                dve.sem_inc(n_used, 1)
            link.base += 2 * NB
            link(V.tensor_reduce(gmd[:, :], asn[:, :, :].rearrange("p b h -> p h b"), AX.X, ALU.min))
            dve.sem_inc(gm_T, 1)
            dve.wait_ge(gm_mm, 1)
            link(V.tensor_reduce(gm[0:H, :], bank[2][0:H, 0:P], AX.X, ALU.min))
            link(V.tensor_scalar(gmd[0:H, :], ident32[0:H, 0:H], gm[0:H, 0:1], None, ALU.mult))
            link(V.tensor_copy(gsel8[0:H, :].rearrange("p (k h) -> p k h", h=H), ident32[0:H, 0:H].unsqueeze(1).to_broadcast([H, P // H, H])))
            dve.sem_inc(gm_T, 1)
            dve.wait_ge(gm_mm, 3)
            link(V.tensor_copy(gmin_row[:, :], bank[4][:, 0:H]))
            link(V.tensor_scalar(gmin_part[:, :], bank[3][:, 0:1], -1.0, None, ALU.mult))
            dve.sem_inc(gm_ready, 1)
            dve.wait_ge(asrc_all, 2 * IT2)
            dve.wait_ge(x1_out, 16)
            a4 = asrc.rearrange("p (k q h) -> p q k h", q=TQ, h=H)
            l4 = sloc[0][:, :].rearrange("p (k q) -> p q k", q=TQ)
            stg4 = stg[:, :, :].rearrange("p j (q k h) -> p j q k h", q=1, h=H)
            dve.sem_inc(f_copied, 2)
            with dve.Fori(0, TQ) as q:
                dve.wait_ge(f_copied, 2 * q + 2)
                dve.sem_inc(pace, 1)
                V.tensor_copy(stg4[:, 0], a4[:, bass.ds(q, 1), :, :]).then_inc(dv, 1)
                V.tensor_copy(stg4[:, 1], l4[:, bass.ds(q, 1), :].unsqueeze(3).to_broadcast([P, 1, 16, H])).then_inc(dv, 1)
                dve.wait_ge(dv, link.base + link.k + 2 * q + 2)
                dve.sem_inc(f_stage, 1)
            link.base += 2 * TQ
            dve.wait_ge(f_copied, 2 * TQ + 2)
            l3 = locT.rearrange("p (q e) -> p q e", e=P)
            p3 = pen.rearrange("p (q e) -> p q e", e=P)
            z3 = lastT.rearrange("p (q e) -> p q e", e=P)
            link(V.memset(p3[:, :, 0:1], -BIG), wait=False)
            link(V.memset(z3[:, :, P - 1:P], 1.0), wait=False)
            link(V.tensor_tensor(z3[:, :, 0:P - 1], l3[:, :, 0:P - 1], l3[:, :, 1:P], ALU.not_equal))
            link(V.tensor_scalar(p3[:, :, 1:P], z3[:, :, 0:P - 1], -BIG, None, ALU.mult))
            link(V.tensor_tensor_scan(segmax, pen, segmax, 0.0, ALU.add, ALU.max))
            dve.sem_inc(b_copied, 1)
            with dve.Fori(0, TQ) as q:
                dve.wait_ge(b_copied, q + 1)
                dve.sem_inc(pace, 1)
                V.tensor_tensor(stg[:, 0, :], segmax[:, bass.ds(q * P, P)], lastT[:, bass.ds(q * P, P)], ALU.mult).then_inc(b_stage, 1)
            dve.wait_ge(b_copied, TQ + 1)
            link(V.memset(macc[:, :], 0.0))
            one_hots_ready(0, 0, 0)

            def tile_maxima(it, last):
                for h in range(2):
                    blks = blocks_of(0, it * 16 + h * HALF)
                    if not (last and h):
                        one_hots_ready(0, it + h, 1 - h, 0, 4)
                    dve.wait_ge(m_psum, 2 * it + h + 1)
                    for u in range(HALF):
                        m = macc[:, bass.ds(blks[u] * H, H)]
                        V.tensor_tensor(m, m, bank[2 + h][:, u * H:(u + 1) * H], ALU.max).then_inc(m_max, 1)
                        if u < 4 and not (last and h):
                            one_hots_ready(0, it + h, 1 - h, 4 + u, 5 + u)
                        dve.wait_ge(m_max, 16 * it + HALF * h + u + 1)

            with dve.Fori(0, IT2 - 1) as it:
                tile_maxima(it, False)
            tile_maxima(IT2 - 1, True)
            m3 = macc[:, :].rearrange("p (b h) -> p b h", h=H)
            link(V.tensor_tensor(m3, m3, gmin_row[:, :].unsqueeze(1).to_broadcast([P, NB, H]), ALU.add))
            link(V.tensor_tensor(m3, m3, tab[:, :, 0:H], ALU.add))
            link(V.scalar_tensor_tensor(tab[:, :, H:2 * H], m3, SLOPE, m3, ALU.mult, ALU.max))
            dve.sem_inc(tab_ready, 1)
            link(V.memset(accf, 0.0))

            def scores(it, h):
                w8 = score[:, h * HALF:(h + 1) * HALF, :]
                look = bank[2 + h][:, 0:HALF * 2 * H].rearrange("p (t j) -> p t j", j=2 * H)
                dve.wait_ge(l_look, 2 * it + h + 1)
                link(V.tensor_tensor(w8, look[:, :, 0:H], asrc3[:, bass.ds(it * 16 + h * HALF, HALF), :], ALU.add))
                link(V.scalar_tensor_tensor(w8, w8, SLOPE, w8, ALU.mult, ALU.max))
                link(V.tensor_tensor(w8, w8, look[:, :, H:2 * H], ALU.subtract))
                link(V.tensor_scalar(w8, w8, 0.0, None, ALU.min))
                dve.sem_inc(l_sc, 1)

            def message(it, u):
                dve.wait_ge(gathered[u], 16 * (3 * IT2 + it + 1))
                r = rows[:, u, 0:D].rearrange("p (h f) -> p h f", h=H)
                V.tensor_tensor(r, r, score[:, u, :].unsqueeze(2).to_broadcast([P, H, F_HEAD]), ALU.mult).then_inc(msg_ready, 1)

            def add(it, u, blk):
                a = accf[:, bass.ds(blk * (D + H), D + H)]
                tg = 16 * (2 * IT2 + it) + u
                dve.wait_ge(agg_done, tg + 1)
                dve.wait_ge(acc_free, 4 + tg)
                V.tensor_tensor(a, a, bank[4 + u % 4][:, 0:D + H], ALU.add).then_inc(acc_free, 1)

            def attend(it, last):
                for h in range(2):
                    ahead = not (last and h)
                    blks = blocks_of(0, it * 16 + h * HALF)
                    dve.wait_ge(l_exp, 2 * it + h + 1)
                    for j in range(HALF):
                        if ahead and j < 4:
                            one_hots_ready(0, it + h, 1 - h, 2 * j, 2 * j + 2)
                        message(it, h * HALF + j)
                        if j >= 2:
                            add(it, h * HALF + j - 2, blks[j - 2])
                    if ahead:
                        scores(it + h, 1 - h)
                    add(it, h * HALF + 6, blks[6])
                    add(it, h * HALF + 7, blks[7])

            one_hots_ready(0, 0, 0)
            scores(0, 0)
            with dve.Fori(0, IT2 - 1) as it:
                link.loop(it, 2 * 4)
                attend(it, False)
            link.end_loop(IT2 - 1)
            attend(IT2 - 1, True)
            dve.wait_ge(acc_free, 4 + 3 * T)
            dve.sem_inc(fin_start, 1)
            af = accf.rearrange("p (b d) -> p b d", d=D + H)
            link(V.tensor_scalar(rden[:, :, :], af[:, :, D:D + H], TINY, None, ALU.max))
            link(V.reciprocal(rden[:, :, :], rden[:, :, :]))
            dve.wait_ge(x1_in, 16)
            groups = [(g * OB, OB) for g in range(OG)] + [(NB - 1, 1)]
            for b0, n in groups:
                for b in range(b0, b0 + n):
                    r = af[:, b, 0:D].rearrange("p (h f) -> p h f", h=H)
                    link(V.tensor_tensor(r, r, rden[:, b, :].unsqueeze(2).to_broadcast([P, H, F_HEAD]), ALU.mult), wait=False)
                    link(V.tensor_tensor(x_all[:, b, :], x_all[:, b, :], bias_rows[:, 3, :], ALU.add))
                    link(V.tensor_tensor(x_all[:, b, :], x_all[:, b, :], af[:, b, 0:D], ALU.add))
                dve.sem_inc(fin, 1)


def kernel(**inputs):
    import numpy as np
    import concourse.bacc as bacc
    from concourse.bass_utils import run_bass_kernel_spmd as run

    nc = bacc.Bacc("TRN2", target_bir_lowering=False, num_devices=1)
    arrays = {}

    def given(name):
        a = np.ascontiguousarray(inputs[name])
        arrays["in_" + name] = a
        return nc.dram_tensor("in_" + name, a.shape, mybir.dt.from_np(a.dtype), kind="ExternalInput").ap()

    xs = [given(n) for n in (
        "x", "src", "dst", "edge_type_16", "L0_gnn_Wf", "L0_gnn_Wb", "L0_gnn_loop_weight", "L0_gnn_forward_bias",
        "L0_gnn_backward_bias", "L0_gnn_self_bias", "L1_gnn_W", "L1_gnn_att_src", "L1_gnn_att_dst", "L1_gnn_bias")]
    out = nc.dram_tensor("out", inputs["x"].shape, F32, kind="ExternalOutput").ap()
    build(nc, *xs, out)
    return run(nc, [arrays], core_ids=[0]).results[0]["out"]
```

```python
from contextlib import ExitStack

import concourse.bass as bass
from concourse import mybir

F32 = mybir.dt.float32
F16 = mybir.dt.float16
BF16 = mybir.dt.bfloat16
I16 = mybir.dt.int16
I32 = mybir.dt.int32
ALU = mybir.AluOpType
ACT = mybir.ActivationFunctionType
AX = mybir.AxisListType

P = 128
EPS = 1e-05
SLOPE = 0.2
BIG = 1e30
TINY = 1e-30
NORMAL = 1024.0


class Link:

    def __init__(self, eng, sem):
        self.eng, self.sem, self.base, self.k = eng, sem, 0, 0

    def loop(self, i, per):
        self.start, self.per = self.base + self.k, per
        self.base = self.start + i * per
        self.k = 0

    def end_loop(self, n):
        assert self.k == self.per, (self.k, self.per)
        self.base, self.k = self.start + n * self.per, 0

    def settle(self):
        self.eng.wait_ge(self.sem, self.base + self.k)

    def __call__(self, ins, wait=True):
        ins.then_inc(self.sem, 1)
        self.k += 1
        if wait:
            self.eng.wait_ge(self.sem, self.base + self.k)


def build(nc, x, src, dst, typ, wf, wb, wloop, bf, bb, bself, w1, att_src, att_dst, b1, out):
    N, D = x.shape
    H, F_HEAD = att_src.shape
    R = wf.shape[0]
    E = src.shape[0]
    NB = -(-N // P)
    HALF = 8
    STEP = 2 * HALF
    ET = -(-E // (P * STEP)) * STEP
    ITS = ET // STEP
    EC = ET + STEP
    STEPS = 2 * ITS + 2
    TG = -(-ET // P)
    T = -(-(E // P + NB) // 16) * 16
    TH = T // 2
    TQ = T // 16
    IT2 = T // 16
    ARENA = 85120 // 4
    WREG = max(R * 2 * D, NB * D, 2 * T * H)
    SB = 7
    assert NB % SB == 0
    OB = 8
    OG = (NB - 1) // OB
    FULL = E // P
    REST = E - FULL * P

    with ExitStack() as ctx:
        def sb(name, shape, dt):
            return ctx.enter_context(nc.sbuf_tensor(name, shape, dt))

        def sem(name):
            return ctx.enter_context(nc.semaphore(name))

        bank = [ctx.enter_context(nc.psum_tensor(f"bank{i}", [P, 512], F32)) for i in range(8)]

        iota_row = sb("iota_row", [P, T], F16)
        ident16 = sb("ident16", [P, P], F16)
        ident32 = sb("ident32", [P, P], F32)
        before16 = sb("before16", [P, P], F16)
        above32 = sb("above32", [P, P], F32)
        ones32 = sb("ones32", [P, P], F32)
        ones16 = sb("ones16", [P, P], F16)
        zero16 = sb("zero16", [P, 512], F16)

        arena = sb("arena", [P, ARENA], F32)

        def carve(at, shape, dt):
            size = {F32: 4, I32: 4, F16: 2, BF16: 2, I16: 2}[dt]
            n = 1
            for d in shape:
                n *= d
            words = -(-n * size // 4)
            assert at % 4 == 0 and at // 4 + words <= ARENA, (at, words)
            v = arena[:, at // 4:at // 4 + words]
            if dt != F32:
                v = v.bitcast(dt)
            v = v[:, 0:n]
            if len(shape) == 2:
                v = v.rearrange("p (a b) -> p a b", b=shape[1])
            if len(shape) == 3:
                v = v.rearrange("p (a b c) -> p a b c", b=shape[1], c=shape[2])
            return v, at + 4 * words

        col, at = carve(0, [3, TG * P], I32)
        sort_at = at
        nat, at = carve(at, [3, TG, P], I32)
        natf, at = carve(at, [3, TG, P], F32)
        at = sort_at
        keyloc, at = carve(at, [EC], F32)
        keyblk, at = carve(at, [EC], F32)
        pay, at = carve(at, [2, ET], F32)
        tmpi, at = carve(at, [2, ET], I32)
        posf, at = carve(at, [ET], F32)
        enc_i, _ = carve(at, [ET], I16)
        enc_f, _ = carve(at, [ET], F16)
        oloc, at = carve(at, [STEP, P], F16)
        oblk, at = carve(at, [STEP, NB], F16)
        olocT16, at = carve(at, [STEP, P], F16)
        oblkT_all, at = carve(at, [STEP, P], F16)
        oblkT = oblkT_all[0:64]
        place, at = carve(at, [NB], I32)
        place_i, at = carve(at, [2, NB], I32)
        place16, at = carve(at, [4, NB], F16)
        seen, at = carve(at, [2, NB * HALF], F16)
        later, at = carve(at, [NB * HALF], F16)
        gsel, at = carve(at, [HALF, NB], F32)
        gs, at = carve(at, [HALF], F32)
        equal, at = carve(at, [HALF, P], F16)
        blkT, at = carve(at, [T], F16)
        cnt, at = carve(at, [NB], F32)
        tot, at = carve(at, [NB], F32)
        toti, at = carve(at, [NB], I32)
        tend, at = carve(at, [NB], F32)
        tendT, at = carve(at, [1], F32)
        dec_i, _ = carve(at, [2, TH], I16)
        dec_f, _ = carve(at, [2, TH], F16)
        ohi, at = carve(at, [4, T], F16)
        olo, at = carve(at, [4, 2 * P], F16)
        olo = olo.rearrange("p a (k e) -> p a k e", e=P)
        ckb, at = carve(at, [T], F32)

        def seen_of(h, u):
            return seen[:, h, :].rearrange("p (b t) -> p b t", t=HALF)[:, :, u]

        accf, at = carve(0, [NB * (D + H)], F32)
        rows, at = carve(at, [16, D], F32)
        acc0 = accf[:, 0:NB * D]
        oh, at = carve(at, [16, P], F32)
        ohT, at = carve(at, [16, P], F32)
        four = [v[:, h * HALF:(h + 1) * HALF, :] for v in (oh, ohT) for h in range(2)]
        assert IT2 % 2 == 0
        segmax, at1 = carve(0, [TQ * P], F32)
        locT, at1 = carve(at1, [TQ * P], F16)
        pen, at1 = carve(at1, [TQ * P], BF16)
        lastT, at1 = carve(at1, [TQ * P], F16)
        assert at1 <= 4 * NB * (D + H) + 4 * 16 * D

        wreg = sb("wreg", [P, WREG], F32)
        x_all = wreg[:, 0:NB * D].rearrange("p (b d) -> p b d", d=D)
        wrel = wreg[:, 0:R * 2 * D].rearrange("p (r c o) -> p r c o", c=2, o=D)
        asrc = wreg[:, 0:T * H]
        smax = wreg[:, T * H:2 * T * H]
        asrc3 = asrc.rearrange("p (t h) -> p t h", h=H)

        sidx = [sb(f"sidx{s}", [P, T], I32) for s in range(2)]
        sloc = [sb(f"sloc{s}", [P, T], F16) for s in range(2)]
        sblk = [sb(f"sblk{s}", [P, T], I16) for s in range(2)]
        deg = [sb(f"deg{s}", [P, NB], F32) for s in range(2)]
        inv = [sb(f"inv{s}", [P, NB], F32) for s in range(2)]
        has = [sb(f"has{s}", [P, NB], F32) for s in range(2)]

        stats = sb("stats", [P, SB, 6], F32)
        mvs = sb("mvs", [P, SB, 2], F32)
        mv = sb("mv", [P, NB, 2], F32)
        rstd = sb("rstd", [P, NB], F32)
        mv2 = mv[:, :, :].rearrange("p b j -> p (b j)")
        eps = sb("eps", [P, 1], F32)
        minus1 = sb("minus1", [P, 1], F32)
        xin = sb("xin", [P, D], F32)
        xh = sb("xh", [P, D], F32)
        hT = sb("hT", [P, 2, P], F32)
        stage = sb("stage", [P, 2, 4 * D], F32)
        wl = sb("wl", [P, 2, D], F32)
        bias_rows = sb("bias_rows", [P, 4, D], F32)
        w1x = sb("w1x", [P, 2, D + 2 * H], F32)
        grow = sb("grow", [P, D + 2 * H], F32)
        asn = sb("asn", [P, NB, H], F32)
        tab = sb("tab", [P, NB, 2 * H], F32)
        tab2 = tab[:, :, :].rearrange("p b j -> p (b j)")
        macc = sb("macc", [P, NB * H], F32)
        gm = sb("gm", [P, 1], F32)
        gmd = sb("gmd", [P, H], F32)
        att_rows = sb("att_rows", [P, 2, D], F32)
        selfst = sb("selfst", [P, D], F32)
        gsel8 = sb("gsel8", [P, P], F32)
        gmin_part = sb("gmin_part", [P, 1], F32)
        gmin_row = sb("gmin_row", [P, H], F32)
        idxst = sb("idxst", [P, 2, HALF], I32)
        ast = sb("ast", [P, 16, H], F32)
        score = sb("score", [P, 16, H], F32)
        rden = sb("rden", [P, NB, H], F32)
        stg = sb("stg", [P, 2, P], F32)

        def scratch(name, shape):
            return nc.dram_tensor(name, shape, F32, kind="Internal").ap()

        xpad = scratch("xpad", (NB * P, D))
        xself = scratch("xself", (NB * P, D))
        hTd = scratch("hTd", (NB * P, 2 * P))
        table = [scratch(f"table{s}", (NB * P * R, D)) for s in range(2)]
        x1d = scratch("x1d", (NB * P, D))
        gtab = scratch("gtab", (NB * P, D))
        stab = scratch("stab", (NB * P, H))

        consts = sem("consts")
        pads_set = sem("pads_set")
        loaded = sem("loaded")
        nat_ready = sem("nat_ready")
        col_psum = sem("col_psum")
        col_taken = sem("col_taken")
        dv = sem("dv")
        a_oh = sem("a_oh")
        a_used = sem("a_used")
        a_done = sem("a_done")
        b_cnt = sem("b_cnt")
        b_tot = sem("b_tot")
        s_oh = sem("s_oh")
        s_tr = sem("s_tr")
        s_trcopied = sem("s_trcopied")
        s_c = sem("s_c")
        s_h = sem("s_h")
        s_g = sem("s_g")
        s_eq = sem("s_eq")
        s_rk = sem("s_rk")
        s_pos = sem("s_pos")
        p_oh = sem("p_oh")
        p_used = sem("p_used")
        p_done = sem("p_done")
        p_taken = sem("p_taken")
        x_all_in = sem("x_all_in")
        x_all_zero = sem("x_all_zero")
        x_stored = sem("x_stored")
        w_in = sem("w_in")
        wb_in = sem("wb_in")
        stats_read = sem("stats_read")
        var_ready = sem("var_ready")
        std_ready = sem("std_ready")
        xin_in = sem("xin_in")
        xin_used = sem("xin_used")
        xh_ready = sem("xh_ready")
        xT_psum = sem("xT_psum")
        hT_ready = sem("hT_ready")
        hT_out = sem("hT_out")
        hT_in = sem("hT_in")
        hT_again = sem("hT_again")
        loop_psum = sem("loop_psum")
        self_ready = sem("self_ready")
        self_out = sem("self_out")
        rel_psum = sem("rel_psum")
        rel_copied = sem("rel_copied")
        rel_round = sem("rel_round")
        tend_ready = sem("tend_ready")
        tend_psum = sem("tend_psum")
        tend_cmp = sem("tend_cmp")
        blk_psum = sem("blk_psum")
        blk_taken = sem("blk_taken")
        s_read = sem("s_read")
        s_rank = sem("s_rank")
        acc_in = sem("acc_in")
        idx_copied = sem("idx_copied")
        rows_free = sem("rows_free")
        oh_ready = sem("oh_ready")
        agg_done = sem("agg_done")
        acc_free = sem("acc_free")
        x1_ready = sem("x1_ready")
        x1_out = sem("x1_out")
        n_xh = sem("n_xh")
        n_T = sem("n_T")
        n_hT = sem("n_hT")
        n_psum = sem("n_psum")
        n_grow = sem("n_grow")
        n_out = sem("n_out")
        n_used = sem("n_used")
        gm_T = sem("gm_T")
        gm_ready = sem("gm_ready")
        gm_mm = sem("gm_mm")
        asrc_all = sem("asrc_all")
        f_stage = sem("f_stage")
        f_T = sem("f_T")
        f_copied = sem("f_copied")
        b_stage = sem("b_stage")
        b_T = sem("b_T")
        b_copied = sem("b_copied")
        m_max = sem("m_max")
        m_psum = sem("m_psum")
        tab_ready = sem("tab_ready")
        l_T = sem("l_T")
        l_ohT = sem("l_ohT")
        l_look = sem("l_look")
        l_sc = sem("l_sc")
        l_exp = sem("l_exp")
        x1_in = sem("x1_in")
        fin = sem("fin")
        out_done = sem("out_done")
        pace = sem("pace")
        idx_ready = sem("idx_ready")
        w_all = sem("w_all")
        msg_ready = sem("msg_ready")
        fin_start = sem("fin_start")
        gathered = [sem(f"gathered{u}") for u in range(16)]
        stage_sem = [[sem(f"table_out{s}_{j}") for j in range(2)] for s in range(2)]
        NG = TG * 3

        def load_blocks(engine, s, t):
            return nc.values_load_multi_w_load_instructions(
                sblk[s][0:1, bass.ds(t, HALF)], engines=[engine], min_val=0, max_val=NB - 1,
                skip_runtime_bounds_check_because="made from at most NB - 1 comparisons")[1]

        block = ctx.enter_context(nc.Block())

        @block.sync
        def _(sp):
            sp.wait_ge(pads_set, 1)
            g = FULL // P
            for j, a in enumerate((dst, src, typ)):
                sp.dma_start(nat[:, j, 0:g, :], a[0:g * P * P].rearrange("(g t p) -> t g p", t=P, p=P)).then_inc(loaded, 16)
                sp.dma_start(nat[0:FULL - g * P, j, g, :], a[g * P * P:FULL * P].rearrange("(t p) -> t p", p=P)).then_inc(loaded, 16)
                sp.dma_start(nat[FULL - g * P:FULL - g * P + 1, j, g, 0:REST], a[FULL * P:E].rearrange("(t p) -> t p", t=1)).then_inc(loaded, 16)
            sp.wait_ge(x_all_zero, 1)
            full_rows = (NB - 1) * P
            sp.dma_start(x_all[:, 0:NB - 1, :], x[0:full_rows, :].rearrange("(b p) d -> p b d", p=P)).then_inc(x_all_in, 16)
            sp.dma_start(x_all[0:N - full_rows, NB - 1, :], x[full_rows:N, :]).then_inc(x_all_in, 16)
            sp.dma_start(wl[:, :, :], wloop.rearrange("(c i) o -> i c o", i=P)).then_inc(w_all, 16)
            sp.dma_start(w1x[:, :, 0:D], w1.rearrange("(c i) o -> i c o", i=P)).then_inc(w_all, 16)
            for j, b in enumerate((bself, bf, bb, b1)):
                sp.dma_start(bias_rows[:, j, :], b.partition_broadcast(P)).then_inc(w_all, 16)
            for j, b in enumerate((att_src, att_dst)):
                sp.dma_start(att_rows[:, j, :], b.rearrange("h f -> (h f)").partition_broadcast(P)).then_inc(w_all, 16)
            sp.wait_ge(x_all_in, 32)
            sp.dma_start(xpad.rearrange("(b p) d -> p b d", p=P), x_all[:, :, :]).then_inc(x_stored, 16)
            sp.wait_ge(x_stored, 16)
            sp.wait_ge(stats_read, NB)
            sp.dma_start(wrel, wf.rearrange("r (c i) o -> i r c o", i=P)).then_inc(w_in, 16)

            def table_rows(s, it):
                rows_of = table[s].rearrange("(n r) d -> n (r d)", r=R)
                for j in range(4):
                    sp.wait_ge(rel_copied, 8 * (s * NB + it) + 2 * (j + 1))
                    sp.dma_start(rows_of[bass.ds(it * P, P), j * 4 * D:(j + 1) * 4 * D], stage[:, j % 2, :]).then_inc(stage_sem[s][j % 2], 16)

            def load_x(it):
                sp.wait_ge(xin_used, it + 1)
                sp.dma_start(xin[:, :], xpad[bass.ds(it * P, P), :]).then_inc(xin_in, 16)

            def store_block(it, last):
                sp.wait_ge(hT_ready, it + 1)
                sp.dma_start(hTd[bass.ds(it * P, P), :], hT[:, :, :].rearrange("p c n -> p (c n)")).then_inc(hT_out, 16)
                if not last:
                    load_x(it + 1)
                sp.wait_ge(self_ready, it + 1)
                sp.dma_start(xself[bass.ds(it * P, P), :], selfst[:, :]).then_inc(self_out, 16)
                table_rows(0, it)

            load_x(0)
            with sp.Fori(0, NB - 1) as it:
                store_block(it, False)
            store_block(NB - 1, True)
            sp.wait_ge(rel_psum, 8 * NB)
            sp.dma_start(wrel, wb.rearrange("r (c i) o -> i r c o", i=P)).then_inc(wb_in, 16)
            sp.wait_ge(hT_out, 16 * (NB + 1))
            sp.wait_ge(p_taken, 2)
            sp.wait_ge(self_out, 16 * (NB + 1))
            sp.dma_start(acc0.rearrange("p (b d) -> p b d", d=D), xself.rearrange("(b p) d -> p b d", p=P)).then_inc(acc_in, 16)

            def load_hT(it):
                sp.wait_ge(hT_again, it + 1)
                sp.dma_start(xin[:, :], hTd[bass.ds(it * P, P), :]).then_inc(hT_in, 16)

            load_hT(0)
            with sp.Fori(0, NB - 1) as it:
                load_hT(it + 1)
                table_rows(1, it)
            table_rows(1, NB - 1)
            sp.wait_ge(x1_ready, 1)
            sp.dma_start(x1d.rearrange("(b p) d -> p b d", p=P), acc0.rearrange("p (b d) -> p b d", d=D)).then_inc(x1_out, 16)
            with sp.Fori(0, NB) as it:
                sp.wait_ge(n_grow, it + 1)
                sp.dma_start(gtab[bass.ds(it * P, P), :], grow[:, 0:D]).then_inc(n_out, 16)
                sp.dma_start(stab[bass.ds(it * P, P), :], grow[:, D:D + H]).then_inc(n_out, 16)
            sp.wait_ge(fin_start, 1)
            sp.wait_ge(x1_out, 16)
            sp.dma_start(x_all[:, :, :], x1d.rearrange("(b p) d -> p b d", p=P)).then_inc(x1_in, 16)
            for g in range(OG):
                sp.wait_ge(fin, g + 1)
                sp.dma_start(out[g * OB * P:(g + 1) * OB * P, :].rearrange("(b p) d -> p b d", p=P), x_all[:, g * OB:(g + 1) * OB, :]).then_inc(out_done, 16)
            sp.wait_ge(fin, OG + 1)
            sp.dma_start(out[full_rows:N, :], x_all[0:N - full_rows, NB - 1, :]).then_inc(out_done, 16)
            sp.wait_ge(out_done, 16 * (OG + 1))

        @block.gpsimd
        def _(pool):
            link = Link(pool, consts)
            pool.iota(iota_row[:, :], pattern=[[1, T]], base=0, channel_multiplier=0, allow_small_or_imprecise_dtypes=True).then_inc(consts, 1)
            link.base = 1
            link(pool.memset(ident16[:, :], 0.0))
            link(pool.affine_select(out=ident16[:, :], in_=ident16[:, :], compare_op=ALU.not_equal, fill=1.0, base=0, pattern=[[-1, P]], channel_multiplier=1))
            link(pool.memset(ident32[:, :], 0.0))
            link(pool.affine_select(out=ident32[:, :], in_=ident32[:, :], compare_op=ALU.not_equal, fill=1.0, base=0, pattern=[[-1, P]], channel_multiplier=1))
            link(pool.memset(before16[:, :], 0.0))
            link(pool.affine_select(out=before16[:, :], in_=before16[:, :], compare_op=ALU.is_gt, fill=-1.0, base=0, pattern=[[1, P]], channel_multiplier=-1))
            link(pool.memset(above32[:, :], 1.0))
            link(pool.affine_select(out=above32[:, :], in_=above32[:, :], compare_op=ALU.is_gt, fill=0.0, base=0, pattern=[[1, P]], channel_multiplier=-1))
            link(pool.memset(ones32[:, :], 1.0))
            link(pool.memset(zero16[:, :], 0.0))
            link(pool.memset(ones16[:, :], 1.0))
            link(pool.memset(oblkT[:, :, :], 0.0))

            def gather(k, from_table, to, idx, free):
                with pool.Fori(0, IT2) as it:
                    for h in range(2):
                        half = 2 * (k * IT2 + it) + h
                        pool.wait_ge(free, half + 1)
                        pool.sem_inc(pace, 1)
                        pool.tensor_copy(idxst[:, h, :], idx[:, bass.ds(it * 16 + h * HALF, HALF)]).then_inc(idx_copied, 1)
                        pool.wait_ge(idx_copied, half + 1)
                        pool.sem_inc(pace, 1)
                        for u in range(HALF):
                            pool.indirect_dma_start(to(h * HALF + u), None, from_table,
                                                    bass.IndirectOffsetOnAxis(idxst[:, h, u:u + 1], 0)).then_inc(gathered[h * HALF + u], 16)

            pool.wait_ge(p_taken, 2)
            for s in range(2):
                for q in range(2):
                    pool.wait_ge(stage_sem[s][q], 16 * (2 * NB + 1))
                gather(s, table[s], lambda u: rows[:, u, 0:D], sidx[s], rows_free)
            pool.wait_ge(n_out, 32 * NB + 32)
            pool.wait_ge(idx_ready, 1)
            gather(2, stab, lambda u: ast[:, u, :], sidx[0], rows_free)
            pool.wait_ge(b_stage, TQ)
            gather(3, gtab, lambda u: rows[:, u, :], sidx[0], rows_free)
        NCONST = 13

        @block.scalar
        def _(act):
            for n in range(NG):
                act.wait_ge(col_psum, n + 1)
                nc.scalar.copy(col[:, n // TG, (n % TG) * P:(n % TG + 1) * P], bank[n % 2][:, 0:P]).then_inc(col_taken, 1)
            act.wait_ge(var_ready, 1)
            nc.scalar.activation(rstd[:, :], mv[:, :, 1], ACT.Sqrt, bias=eps[:, 0:1]).then_inc(std_ready, 1)
            act.wait_ge(consts, NCONST)
            act.sem_inc(hT_out, 16)
            act.sem_inc(rel_round, 1)
            for s in range(2):
                for q in range(2):
                    act.sem_inc(stage_sem[s][q], 16)

            def relation_rows(s, it, groups, b0):
                for g in groups:
                    n = 8 * (s * NB + it) + g
                    if g % 2 == 0:
                        act.wait_ge(stage_sem[s][g // 2 % 2], 16 * (2 * it + g // 4 + 1))
                        act.sem_inc(pace, 1)
                    act.wait_ge(rel_psum, n + 1)
                    nc.scalar.copy(stage[:, g // 2 % 2, (g % 2) * 2 * D:(g % 2 + 1) * 2 * D], bank[b0 + g % 2][:, :]).then_inc(rel_copied, 1)

            for s in range(2):

                def turned(n, h):
                    hs = slice(h * HALF, (h + 1) * HALF)
                    act.wait_ge(s_tr, s * (STEPS - 1) + n + 1)
                    nc.scalar.copy(olocT16[:, hs, :], bank[0][:, :].bitcast(F16).rearrange("p (t e) -> p t e", e=P)).then_inc(s_trcopied, 1)
                    nc.scalar.copy(oblkT[0:NB, hs, :], bank[1][0:NB, :].bitcast(F16).rearrange("p (t e) -> p t e", e=P)).then_inc(s_trcopied, 1)

                turned(0, 0)
                with act.Fori(0, ITS) as it:
                    for h in range(2):
                        n = 2 * it + h + 1
                        turned(n, (h + 1) % 2)
                        if h == 0 and s == 0:
                            act.wait_ge(hT_out, 16 * (it + 1))
                            act.wait_ge(xT_psum, it + 1)
                            nc.scalar.activation(hT[:, :, :], bank[6][:, 0:2 * P].rearrange("p (c n) -> p c n", n=P), ACT.Relu).then_inc(hT_ready, 1)
                        act.wait_ge(s_rank, s * 2 * ITS + n)
                        for c in range(2):
                            act.wait_ge(s_eq, 2 * (s * 2 * ITS + n) + c - 1)
                            nc.scalar.activation(equal[:, 4 * c:4 * c + 4, :], bank[4 + c][:, :].rearrange("p (t e) -> p t e", e=P), ACT.Relu,
                                                 bias=minus1[:, 0:1]).then_inc(s_rk, 1)
                        if s == 0:
                            relation_rows(0, it, range(4 * h, 4 * h + 4), 6)
                            if h == 1:
                                act.wait_ge(rel_copied, 8 * (it + 1))
                                act.sem_inc(rel_round, 1)
            act.sem_inc(hT_again, 1)
            with act.Fori(0, NB) as it:
                act.wait_ge(hT_in, 16 * (it + 1))
                act.wait_ge(rel_psum, 8 * (NB + it))
                nc.scalar.copy(hT[:, :, :].rearrange("p c n -> p (c n)"), xin[:, :]).then_inc(hT_again, 1)
                relation_rows(1, it, range(8), 0)
            act.wait_ge(var_ready, 2)
            nc.scalar.activation(rstd[:, :], mv[:, :, 1], ACT.Sqrt, bias=eps[:, 0:1]).then_inc(std_ready, 1)
            act.sem_inc(n_out, 32)
            with act.Fori(0, NB) as it:
                act.wait_ge(n_T, it + 1)
                nc.scalar.activation(hT[:, :, :], bank[0][:, 0:2 * P].rearrange("p (c n) -> p c n", n=P), ACT.Relu).then_inc(n_hT, 1)
                act.wait_ge(n_out, 32 * (it + 1))
                act.sem_inc(pace, 1)
                act.wait_ge(n_psum, it + 1)
                nc.scalar.copy(grow[:, :], bank[1][:, 0:D + 2 * H]).then_inc(n_grow, 1)
            with act.Fori(0, IT2) as it:
                for h in range(2):
                    for u in range(h * HALF, (h + 1) * HALF):
                        act.wait_ge(gathered[u], 16 * (2 * IT2 + it + 1))
                    act.sem_inc(pace, 1)
                    nc.scalar.copy(asrc[:, bass.ds(it * 16 * H + h * HALF * H, HALF * H)],
                                   ast[:, h * HALF:(h + 1) * HALF, :].rearrange("p t h -> p (t h)")).then_inc(asrc_all, 1)
                    act.wait_ge(asrc_all, 2 * it + h + 1)
                    act.sem_inc(rows_free, 1)
            act.wait_ge(gm_ready, 1)
            with act.Fori(0, TQ) as q:
                act.wait_ge(f_T, q + 1)
                act.sem_inc(pace, 1)
                nc.scalar.activation(segmax[:, bass.ds(q * P, P)], bank[0][:, 0:P], ACT.Identity, bias=gmin_part[:, 0:1]).then_inc(f_copied, 1)
                nc.scalar.copy(locT[:, bass.ds(q * P, P)], bank[0][:, P:2 * P]).then_inc(f_copied, 1)
            with act.Fori(0, TQ) as q:
                act.wait_ge(b_T, q + 1)
                act.sem_inc(pace, 1)
                nc.scalar.copy(smax.rearrange("p (k q h) -> p q k h", q=TQ, h=H)[:, bass.ds(q, 1), :, :],
                               bank[1][:, 0:P].rearrange("p (q k h) -> p q k h", q=1, h=H)).then_inc(b_copied, 1)
            with act.Fori(0, IT2) as it:
                for h in range(2):
                    for q in range(2):
                        act.wait_ge(l_T, 2 * (2 * it + h) + q + 1)
                        nc.scalar.copy(ohT[:, h * HALF + 4 * q:h * HALF + 4 * q + 4, :], bank[q][:, :].rearrange("p (t e) -> p t e", e=P)).then_inc(l_ohT, 1)
                    act.wait_ge(l_sc, 2 * it + h + 1)
                    w8 = score[:, h * HALF:(h + 1) * HALF, :]
                    nc.scalar.activation(w8, w8, ACT.Exp).then_inc(l_exp, 1)

        @block.tensor
        def _(pe):
            pe.wait_ge(consts, NCONST)
            pe.wait_ge(nat_ready, 1)
            for n in range(NG):
                if n >= 2:
                    pe.wait_ge(col_taken, n - 1)
                nc.tensor.transpose(bank[n % 2][:, 0:P], natf[:, n // TG, n % TG, :], ident32[:, :]).then_inc(col_psum, 1)
            pe.wait_ge(col_taken, NG)

            def relations(s, it, groups, b0):
                for g in groups:
                    n = 8 * (s * NB + it) + g
                    if g > 1 or s == 1:
                        pe.wait_ge(rel_copied, n - 1)
                    for c in range(2):
                        mm = nc.tensor.matmul(bank[b0 + g % 2][:, :], hT[:, c, :], wrel[:, 2 * g:2 * g + 2, c, :], start=(c == 0), stop=(c == 1))
                    mm.then_inc(rel_psum, 1)

            pe.sem_inc(a_used, 2)
            pe.sem_inc(p_used, 4)
            for s in range(2):
                if s:
                    pe.wait_ge(p_taken, s)
                nc.tensor.matmul(bank[6][:, 0:NB], zero16[:, 0:P], zero16[:, 0:NB], start=True, stop=False)
                with pe.Fori(0, ITS) as it:
                    for h in range(2):
                        step = 2 * (s * ITS + it) + h
                        pe.wait_ge(a_oh, (HALF + 1) * (step + 1))
                        for u in range(h * HALF, h * HALF + HALF):
                            mm = nc.tensor.matmul(bank[6][:, 0:NB], oloc[:, u, :], oblk[:, u, :], start=False, stop=False)
                        mm.then_inc(a_used, 1)
                nc.tensor.matmul(bank[6][:, 0:NB], zero16[:, 0:P], zero16[:, 0:NB], start=False, stop=True).then_inc(a_done, 1)
                pe.wait_ge(b_cnt, s + 1)
                nc.tensor.matmul(bank[7][:, 0:NB], ones32[:, :], cnt[:, :], start=True, stop=True).then_inc(b_tot, 1)
                nc.tensor.matmul(bank[7][:, 64:64 + NB], above32[:, :], cnt[:, :], start=True, stop=True).then_inc(b_tot, 1)
                pe.wait_ge(tend_ready, s + 1)
                nc.tensor.transpose(bank[4][0:NB, 0:P], tend[:, :], ident32[:, :]).then_inc(tend_psum, 1)
                pe.wait_ge(tend_cmp, s + 1)
                for c in range(2):
                    mm = nc.tensor.matmul(bank[4 + c][:, 0:TH], ones16[0:NB - 1, :], blkT[0:NB - 1, c * TH:(c + 1) * TH], start=True, stop=True)
                mm.then_inc(blk_psum, 1)
                pe.wait_ge(blk_taken, 2 * (s + 1))

                def turn(n, h):
                    hs = [h * HALF + u for u in range(HALF)]
                    pe.wait_ge(s_oh, (HALF + 1) * (s * STEPS + n + 1) - 1)
                    t16 = bank[0][:, :].bitcast(F16).rearrange("p (t e) -> p t e", e=P)
                    b16 = bank[1][:, :].bitcast(F16).rearrange("p (t e) -> p t e", e=P)
                    for u in range(HALF):
                        nc.tensor.transpose(t16[:, u, :], oloc[:, hs[u], :], ident16[:, :])
                    pe.wait_ge(s_oh, (HALF + 1) * (s * STEPS + n + 1))
                    pe.sem_inc(pace, 1)
                    for u in range(HALF):
                        mm = nc.tensor.transpose(b16[0:NB, u, :], oblk[:, hs[u], :], ident16[:, :])
                    mm.then_inc(s_tr, 1)
                    for u in range(HALF):
                        counts = bank[2][:, 0:NB * HALF].rearrange("p (b t) -> p b t", t=HALF)[:, :, u]
                        mm = nc.tensor.matmul(counts, oloc[:, hs[u], :], oblk[:, hs[u], :], start=True, stop=True)
                    mm.then_inc(s_c, 1)

                turn(0, 0)
                if s == 0:
                    pe.wait_ge(w_in, 16)
                    pe.wait_ge(w_all, 16 * 8)
                    pe.sem_inc(s_rank, 1)
                    pe.sem_inc(s_rk, 2)
                    pe.sem_inc(s_read, 1)
                with pe.Fori(0, ITS) as it:
                    for h in range(2):
                        n = 2 * it + h + 1
                        last = s * 2 * ITS + n
                        pe.wait_ge(s_trcopied, 2 * (s * (STEPS - 1) + n))
                        pe.wait_ge(s_h, s * (STEPS - 1) + n)
                        turn(n, (h + 1) % 2)
                        if h == 0 and s == 0:
                            pe.wait_ge(rel_round, it + 1)
                            pe.wait_ge(xh_ready, it + 1)
                            for c in range(2):
                                mm = nc.tensor.transpose(bank[6][:, c * P:(c + 1) * P], xh[:, c * P:(c + 1) * P], ident32[:, :])
                            mm.then_inc(xT_psum, 1)
                        pe.wait_ge(s_rk, 2 * (last - 1) + 2)
                        for u in range(HALF):
                            o = bank[4 + u // 4][:, (u % 4) * P:(u % 4 + 1) * P]
                            q = h * HALF + u
                            nc.tensor.matmul(o, olocT16[:, q, :], olocT16[:, q, :], start=True, stop=False)
                            nc.tensor.matmul(o, oblkT[:, q, :], oblkT[:, q, :], start=False, stop=False)
                            mm = nc.tensor.matmul(o, ident16[:, :], before16[:, :], start=False, stop=True)
                            if u % 4 == 3:
                                mm.then_inc(s_eq, 1)
                        pe.wait_ge(s_read, last)
                        for u in range(HALF):
                            q = h * HALF + u
                            o = bank[3][:, u * NB:(u + 1) * NB]
                            parts = [place16[:, 2 * h + 1, :], place16[:, 2 * h + 1, :], place16[:, 2 * h, :]]
                            if u:
                                parts.append(seen_of(h, u - 1))
                            for j, part in enumerate(parts):
                                nc.tensor.matmul(o, olocT16[:, q, :], part, start=j == 0, stop=j == len(parts) - 1)
                        pe.wait_ge(s_rk, 2 * last + 2)
                        for u in range(HALF):
                            c = HALF * NB + u
                            mm = nc.tensor.matmul(bank[3][:, c:c + 1], equal[:, u, :], ones16[:, 0:1], start=True, stop=True)
                        mm.then_inc(s_g, 1)
                        pe.sem_inc(s_rank, 1)
                        if s == 0:
                            if h == 0:
                                pe.wait_ge(hT_ready, it + 1)
                                for c in range(2):
                                    mm = nc.tensor.matmul(bank[7][:, 0:D], hT[:, c, :], wl[:, c, :], start=(c == 0), stop=(c == 1))
                                mm.then_inc(loop_psum, 1)
                            relations(0, it, [4 * h], 6)
                            if h == 0:
                                pe.wait_ge(self_ready, it + 1)
                            relations(0, it, range(4 * h + 1, 4 * h + 4), 6)
                if s == 0:
                    pe.wait_ge(rel_copied, 8 * NB)
                pe.wait_ge(s_pos, s + 1)
                pe.wait_ge(s_trcopied, 2 * (s + 1) * (STEPS - 1))
                for c in range(2):
                    for k in range(2):
                        nc.tensor.matmul(bank[2 * k + c][:, 0:TH], zero16[:, 0:P], zero16[:, 0:TH], start=True, stop=False)
                with pe.Fori(0, ET // 4) as it:
                    for u in range(4):
                        pe.wait_ge(p_oh, 3 * (4 * (s * (ET // 4) + it) + u + 1))
                        for k in range(2):
                            for c in range(2):
                                mm = nc.tensor.matmul(bank[2 * k + c][:, 0:TH], olo[:, u, k, :], ohi[:, u, c * TH:(c + 1) * TH], start=False, stop=False)
                        mm.then_inc(p_used, 1)
                for c in range(2):
                    for k in range(2):
                        mm = nc.tensor.matmul(bank[2 * k + c][:, 0:TH], zero16[:, 0:P], zero16[:, 0:TH], start=False, stop=True)
                mm.then_inc(p_done, 1)

            def sum_tiles(k, it, nodes):
                for h in range(2):
                    half = 2 * (k * IT2 + it) + h
                    for u in range(h * HALF, (h + 1) * HALF):
                        pe.wait_ge(oh_ready, HALF * half + u % HALF + 1)
                        pe.wait_ge(gathered[u], 16 * (k * IT2 + it + 1))
                        pe.wait_ge(acc_free, 16 * (k * IT2 + it) + u + 1)
                        nc.tensor.matmul(bank[4 + u % 4][:, 0:D], oh[:, u, :], rows[:, u, 0:D], start=True, stop=True).then_inc(agg_done, 1)
                        if nodes and u == 1:
                            pe.wait_ge(hT_again, it + 2)
                        if nodes and u % 2:
                            relations(1, it, [u // 2], 0)
                    pe.wait_ge(agg_done, 16 * (k * IT2 + it) + (h + 1) * HALF)
                    pe.sem_inc(rows_free, 1)

            pe.wait_ge(wb_in, 16)
            with pe.Fori(0, NB) as it:
                sum_tiles(0, it, True)
            with pe.Fori(NB, IT2) as it:
                sum_tiles(0, it, False)
            with pe.Fori(0, IT2) as it:
                sum_tiles(1, it, False)

            def turn_node(it):
                pe.wait_ge(n_xh, it + 1)
                for c in range(2):
                    mm = nc.tensor.transpose(bank[0][:, c * P:(c + 1) * P], xh[:, c * P:(c + 1) * P], ident32[:, :])
                mm.then_inc(n_T, 1)

            def node_row(it, last):
                pe.wait_ge(n_hT, it + 1)
                if not last:
                    turn_node(it + 1)
                pe.wait_ge(n_used, it + 1)
                for c in range(2):
                    mm = nc.tensor.matmul(bank[1][:, 0:D + 2 * H], hT[:, c, :], w1x[:, c, :], start=(c == 0), stop=(c == 1))
                mm.then_inc(n_psum, 1)

            turn_node(0)
            with pe.Fori(0, NB - 1) as it:
                node_row(it, False)
            node_row(NB - 1, True)
            pe.wait_ge(gm_T, 1)
            nc.tensor.transpose(bank[2][0:H, 0:P], gmd[:, :], ident32[:, :]).then_inc(gm_mm, 1)
            pe.wait_ge(gm_T, 2)
            nc.tensor.matmul(bank[3][:, 0:1], gsel8[0:H, :], gm[0:H, :], start=True, stop=True).then_inc(gm_mm, 1)
            nc.tensor.matmul(bank[4][:, 0:H], ones32[0:H, :], gmd[0:H, :], start=True, stop=True).then_inc(gm_mm, 1)
            with pe.Fori(0, TQ) as q:
                pe.wait_ge(f_stage, q + 1)
                for j in range(2):
                    mm = nc.tensor.transpose(bank[0][:, j * P:(j + 1) * P], stg[:, j, :], ident32[:, :])
                mm.then_inc(f_T, 1)
            with pe.Fori(0, TQ) as q:
                pe.wait_ge(b_stage, q + 1)
                nc.tensor.transpose(bank[1][:, 0:P], stg[:, 0, :], ident32[:, :]).then_inc(b_T, 1)
            with pe.Fori(0, IT2 // 2) as it:
                for j in range(4):
                    g = 4 * it + j
                    pe.wait_ge(oh_ready, 16 * 2 * IT2 + HALF * (g + 1))
                    for u in range(HALF):
                        mm = nc.tensor.matmul(bank[2 + j][:, u * H:(u + 1) * H], four[j][:, u, :],
                                              smax[:, bass.ds((g * HALF + u) * H, H)], start=True, stop=True)
                    mm.then_inc(m_psum, 1)
            pe.wait_ge(tab_ready, 1)

            def turn_one_hots(it, h, q):
                pe.wait_ge(oh_ready, 16 * (3 * IT2 + it) + HALF * h + 4 * (q + 1))
                for u in range(4):
                    mm = nc.tensor.transpose(bank[q][:, u * P:(u + 1) * P], oh[:, h * HALF + 4 * q + u, :], ident32[:, :])
                mm.then_inc(l_T, 1)

            def look_up(it, h, blks):
                pe.wait_ge(l_ohT, 2 * (2 * it + h) + 2)
                for u in range(HALF):
                    mm = nc.tensor.matmul(bank[2 + h][:, u * 2 * H:(u + 1) * 2 * H], ohT[:, h * HALF + u, :],
                                          tab2[:, bass.ds(blks[u] * 2 * H, 2 * H)], start=True, stop=True)
                mm.then_inc(l_look, 1)

            def sum_messages(it, last):
                for h in range(2):
                    ahead = not (last and h)
                    if ahead:
                        blks = load_blocks(mybir.EngineType.PE, 0, (it + h) * 16 + (1 - h) * HALF)
                    for j in range(HALF):
                        u = h * HALF + j
                        pe.wait_ge(msg_ready, 16 * it + u + 1)
                        pe.wait_ge(acc_free, 16 * (2 * IT2 + it) + u + 1)
                        nc.tensor.matmul(bank[4 + u % 4][:, 0:D], oh[:, u, :], rows[:, u, 0:D], start=True, stop=True)
                        nc.tensor.matmul(bank[4 + u % 4][:, D:D + H], oh[:, u, :], score[:, u, :], start=True, stop=True).then_inc(agg_done, 1)
                        if ahead and j in (1, 2):
                            turn_one_hots(it + h, 1 - h, j - 1)
                        if ahead and j == 4:
                            look_up(it + h, 1 - h, blks)
                    pe.wait_ge(agg_done, 16 * (2 * IT2 + it) + (h + 1) * HALF)
                    pe.sem_inc(rows_free, 1)

            first_blks = load_blocks(mybir.EngineType.PE, 0, 0)
            turn_one_hots(0, 0, 0)
            turn_one_hots(0, 0, 1)
            look_up(0, 0, first_blks)
            with pe.Fori(0, IT2 - 1) as it:
                sum_messages(it, False)
            sum_messages(IT2 - 1, True)

        @block.vector
        def _(dve):
            V = nc.vector
            link = Link(dve, dv)
            V.memset(nat[:, 1:3, :, :], 0).then_inc(dv, 1)
            link.base = 1
            link(V.memset(nat[:, 0, :, :], -1))
            V.memset(nat[:, 1, TG - 1, :], -1).then_inc(pads_set, 1)
            dve.wait_ge(loaded, 16 * 9)
            V.tensor_copy(natf[:, :, :, :], nat[:, :, :, :]).then_inc(nat_ready, 1)
            link(V.memset(eps[:, :], EPS), wait=False)
            link(V.memset(minus1[:, :], -1.0), wait=False)
            V.memset(x_all[:, NB - 1, :], 0.0).then_inc(x_all_zero, 1)

            def layer_norm_stats(blocks, n):
                with dve.Fori(0, NB // SB) as i:
                    link.loop(i, SB + 1)
                    for u in range(SB):
                        V.bn_stats(stats[:, u, :], blocks[:, bass.ds(i * SB + u, 1), :]).then_inc(stats_read, 1)
                    dve.wait_ge(stats_read, n * NB + i * SB + SB)
                    dve.sem_inc(pace, 1)
                    for u in range(SB):
                        link(V.bn_aggr(mvs[:, u, :], stats[:, u, :]), wait=u == SB - 1)
                    link(V.tensor_copy(mv[:, bass.ds(i * SB, SB), :], mvs[:, :, :]))
                link.end_loop(NB // SB)
                dve.sem_inc(var_ready, 1)
                dve.wait_ge(std_ready, n + 1)
                link(V.reciprocal(rstd[:, :], rstd[:, :]))

            dve.wait_ge(x_all_in, 32)
            layer_norm_stats(x_all, 0)
            dve.wait_ge(w_all, 16 * 8)
            for c in range(2):
                for j in range(2):
                    link(V.tensor_tensor(xh[:, :], w1x[:, c, 0:D], att_rows[:, j, :], ALU.mult))
                    link(V.tensor_reduce(w1x[:, c, D + j * H:D + (j + 1) * H], xh[:, :].rearrange("p (h f) -> p h f", h=H), AX.X, ALU.add))
            dve.sem_inc(xin_used, 1)
            dve.sem_inc(self_out, 16)
            dve.wait_ge(consts, NCONST)
            dve.wait_ge(col_taken, NG)
            for s in range(2):
                key, other = (col[:, s, 0:ET], col[:, 1 - s, 0:ET])
                link(V.memset(keyblk[:, ET:EC], -1.0), wait=False)
                link(V.memset(keyloc[:, ET:EC], 0.0), wait=False)
                ty = col[:, 2, 0:ET]
                link(V.tensor_scalar(tmpi[:, 0, :], key, 7, None, ALU.arith_shift_right), wait=False)
                link(V.tensor_scalar(tmpi[:, 1, :], key, 127, None, ALU.bitwise_and))
                link(V.tensor_copy(keyblk[:, 0:ET], tmpi[:, 0, :]), wait=False)
                link(V.tensor_copy(keyloc[:, 0:ET], tmpi[:, 1, :]))
                link(V.tensor_scalar(posf[:, :], key, 0.0, None, ALU.is_ge))
                link(V.scalar_tensor_tensor(pay[:, 1, :], other, 16.0, ty, ALU.mult, ALU.add))
                link(V.tensor_tensor(tmpi[:, 0, :], pay[:, 1, :], posf[:, :], ALU.mult))
                link(V.tensor_scalar(tmpi[:, 1, :], tmpi[:, 0, :], 7, None, ALU.arith_shift_right))
                link(V.tensor_scalar(enc_i, tmpi[:, 1, :], NORMAL, None, ALU.add))
                link(V.tensor_tensor(pay[:, 1, :], enc_f, posf[:, :], ALU.mult))
                link(V.tensor_scalar(tmpi[:, 1, :], tmpi[:, 0, :], 127, None, ALU.bitwise_and))
                link(V.tensor_scalar(pay[:, 0, :], keyloc[:, 0:ET], 128.0, NORMAL, ALU.mult, ALU.add))
                link(V.tensor_tensor(enc_i, pay[:, 0, :], tmpi[:, 1, :], ALU.add))
                link(V.tensor_tensor(pay[:, 0, :], enc_f, posf[:, :], ALU.mult))

                def local_one_hots(t, h, done, first=0, end=HALF):
                    for u in range(first, end):
                        V.tensor_scalar(oloc[:, h * HALF + u, :], iota_row[:, 0:P], keyloc[:, bass.ds(t + u, 1)], None, ALU.is_equal).then_inc(done, 1)

                def block_one_hots(t, h, done):
                    kb = keyblk[:, bass.ds(t, HALF)].unsqueeze(2).to_broadcast([P, HALF, NB])
                    ib = iota_row[:, 0:NB].unsqueeze(1).to_broadcast([P, HALF, NB])
                    V.tensor_tensor(oblk[:, h * HALF:(h + 1) * HALF, :], ib, kb, ALU.is_equal).then_inc(done, 1)

                with dve.Fori(0, ITS) as it:
                    for h in range(2):
                        dve.wait_ge(a_used, 2 * (s * ITS + it) + h + 1)
                        dve.sem_inc(pace, 1)
                        local_one_hots(it * STEP + h * HALF, h, a_oh)
                        block_one_hots(it * STEP + h * HALF, h, a_oh)
                dve.wait_ge(a_done, s + 1)
                link(V.tensor_copy(cnt[:, :], bank[6][:, 0:NB]))
                V.tensor_copy(deg[s][:, :], cnt[:, :]).then_inc(b_cnt, 1)
                dve.wait_ge(b_tot, 2 * (s + 1))
                link(V.tensor_scalar(toti[:, :], bank[7][:, 0:NB], 127.0, None, ALU.add))
                link(V.tensor_scalar(toti[:, :], toti[:, :], 7, None, ALU.arith_shift_right))
                link(V.tensor_copy(tot[:, :], toti[:, :]))
                link(V.tensor_tensor_scan(tend[:, :], tot[:, :], tot[:, :], 0.0, ALU.add, ALU.bypass))
                link(V.tensor_tensor(tot[:, :], tend[:, :], tot[:, :], ALU.subtract))
                link(V.scalar_tensor_tensor(place, tot[:, :], 128.0, bank[7][:, 64:64 + NB], ALU.mult, ALU.add))
                dve.sem_inc(tend_ready, 1)
                dve.wait_ge(tend_psum, s + 1)
                link(V.tensor_copy(tendT[0:NB, :], bank[4][0:NB, 0:1]))
                V.tensor_scalar(blkT[0:NB, :], iota_row[0:NB, :], tendT[0:NB, 0:1], None, ALU.is_ge).then_inc(tend_cmp, 1)
                dve.wait_ge(blk_psum, s + 1)
                for c in range(2):
                    V.tensor_copy(sblk[s][:, c * TH:(c + 1) * TH], bank[4 + c][:, 0:TH]).then_inc(blk_taken, 1)

                def split_places(n, h, t, sem):
                    link(V.tensor_scalar(place_i[:, 0, :], place, 1023, None, ALU.bitwise_and), wait=False)
                    link(V.tensor_scalar(place_i[:, 1, :], place, 10, None, ALU.arith_shift_right), wait=False)
                    local_one_hots(t, 1 - h, sem, 0, 4)
                    link.settle()
                    link(V.tensor_copy(place16[:, 2 * h, :], place_i[:, 0, :]), wait=False)
                    link(V.tensor_scalar(place16[:, 2 * h + 1, :], place_i[:, 1, :], 512.0, None, ALU.mult), wait=False)
                    local_one_hots(t, 1 - h, sem, 4, HALF)

                def count_on(n, h):
                    dve.wait_ge(s_c, s * (STEPS - 1) + n + 1)
                    link(V.tensor_tensor_scan(seen[:, h, :], later, bank[2][:, 0:HALF * NB], 0.0, ALU.mult, ALU.add))
                    link(V.tensor_tensor(place, place, seen_of(h, HALF - 1), ALU.add))
                    dve.sem_inc(s_h, 1)

                link(V.memset(later, 1.0))
                link(V.memset(later.rearrange("p (b t) -> p b t", t=HALF)[:, :, 0:1], 0.0))
                local_one_hots(0, 0, s_oh, 0, HALF)
                block_one_hots(0, 0, s_oh)
                split_places(0, 0, HALF, s_oh)
                block_one_hots(HALF, 1, s_oh)
                count_on(0, 0)
                with dve.Fori(0, ITS) as it:
                    link.loop(it, 2 * 9 + (1 if s == 0 else 0))
                    if s == 0:
                        dve.wait_ge(xin_in, 16 * (it + 1))
                        V.tensor_scalar(xh[:, :], xin[:, :], mv2[:, bass.ds(2 * it, 1)], rstd[:, bass.ds(it, 1)], ALU.subtract, ALU.mult).then_inc(xh_ready, 1)
                    for h in range(2):
                        n = 2 * it + h + 1
                        split_places(n, 1 - h, it * STEP + (h + 2) * HALF, s_oh)
                        count_on(n, 1 - h)
                        dve.wait_ge(s_g, s * 2 * ITS + n)
                        link(V.tensor_tensor(gsel[:, :, :], bank[3][:, 0:HALF * NB].rearrange("p (t b) -> p t b", b=NB), oblk[:, h * HALF:(h + 1) * HALF, :], ALU.mult))
                        block_one_hots(it * STEP + (h + 2) * HALF, h, s_oh)
                        link(V.tensor_reduce(gs[:, :], gsel[:, :, :], AX.X, ALU.add))
                        link(V.tensor_tensor(posf[:, bass.ds(it * STEP + h * HALF, HALF)], gs[:, :], bank[3][:, HALF * NB:HALF * (NB + 1)], ALU.add))
                        dve.sem_inc(s_read, 1)
                        if h == 0 and s == 0:
                            dve.wait_ge(self_out, 16 * (it + 1))
                            link(V.tensor_tensor(selfst[:, :], xin[:, :], bias_rows[:, 0, :], ALU.add))
                            dve.sem_inc(xin_used, 1)
                            dve.wait_ge(loop_psum, it + 1)
                            V.scalar_tensor_tensor(selfst[:, :], bank[7][:, 0:D], 2.0, selfst[:, :], ALU.mult, ALU.add).then_inc(self_ready, 1)
                link.end_loop(ITS)
                link(V.tensor_copy(tmpi[:, 0, :], posf[:, :]))
                link(V.tensor_scalar(tmpi[:, 1, :], tmpi[:, 0, :], 7, None, ALU.arith_shift_right), wait=False)
                link(V.tensor_copy(posf[:, :], tmpi[:, 0, :]))
                link(V.tensor_copy(keyblk[:, 0:ET], tmpi[:, 1, :]), wait=False)
                link(V.tensor_scalar(tmpi[:, 0, :], tmpi[:, 0, :], 127, None, ALU.bitwise_and))
                link(V.tensor_copy(keyloc[:, 0:ET], tmpi[:, 0, :]))
                dve.sem_inc(s_pos, 1)
                with dve.Fori(0, ET // 4) as it:
                    for u in range(4):
                        dve.wait_ge(p_used, 4 * (s * (ET // 4) + it) + u + 1)
                        t = bass.ds(it * 4 + u, 1)
                        dve.sem_inc(pace, 1)
                        V.tensor_scalar(ohi[:, u, :], iota_row[:, :], keyblk[:, t], None, ALU.is_equal).then_inc(p_oh, 1)
                        for k in range(2):
                            V.tensor_scalar(olo[:, u, k, :], iota_row[:, 0:P], keyloc[:, t], pay[:, k, t], ALU.is_equal, ALU.mult).then_inc(p_oh, 1)
                dve.wait_ge(p_done, s + 1)
                for c in range(2):
                    cs = slice(c * TH, (c + 1) * TH)
                    link(V.tensor_copy(dec_f[:, 0, :], bank[c][:, 0:TH]), wait=False)
                    link(V.tensor_copy(dec_f[:, 1, :], bank[2 + c][:, 0:TH]))
                    link(V.tensor_scalar(tmpi[:, 0, 0:TH], dec_i[:, 0, :], -NORMAL, None, ALU.add))
                    link(V.tensor_scalar(tmpi[:, 1, 0:TH], tmpi[:, 0, 0:TH], 7, None, ALU.arith_shift_right))
                    link(V.tensor_scalar(sloc[s][:, cs], tmpi[:, 1, 0:TH], -1.0, None, ALU.max))
                    link(V.tensor_scalar(tmpi[:, 1, 0:TH], tmpi[:, 0, 0:TH], 127, None, ALU.bitwise_and))
                    link(V.tensor_scalar(ckb[:, cs], dec_i[:, 1, :], -NORMAL, 0.0, ALU.add, ALU.max))
                    link(V.scalar_tensor_tensor(sidx[s][:, cs], ckb[:, cs], 128.0, tmpi[:, 1, 0:TH], ALU.mult, ALU.add))
                dve.sem_inc(p_taken, 1)
            for s in range(2):
                link(V.tensor_scalar(has[s][:, :], deg[s][:, :], 0.0, None, ALU.is_gt), wait=False)
                link(V.tensor_scalar(inv[s][:, :], deg[s][:, :], 1.0, None, ALU.max))
                link(V.reciprocal(inv[s][:, :], inv[s][:, :]))
                link(V.tensor_tensor(inv[s][:, :], inv[s][:, :], has[s][:, :], ALU.mult))
            dve.sem_inc(rows_free, 2)
            dve.sem_inc(acc_free, 4)

            def one_hots_ready(s, it, h, first=0, end=HALF):
                for u in range(h * HALF + first, h * HALF + end):
                    V.tensor_scalar(oh[:, u, :], iota_row[:, 0:P], sloc[s][:, bass.ds(it * 16 + u, 1)], None, ALU.is_equal).then_inc(oh_ready, 1)

            def blocks_of(s, t):
                return load_blocks(mybir.EngineType.DVE, s, t)

            dve.wait_ge(acc_in, 16)
            for s in range(2):
                with dve.Fori(0, IT2) as it:
                    for h in range(2):
                        dve.wait_ge(rows_free, 2 * (s * IT2 + it) + h + 1)
                        dve.sem_inc(pace, 1)
                        blks = blocks_of(s, it * 16 + h * HALF)
                        one_hots_ready(s, it, h)
                        for u in range(h * HALF, (h + 1) * HALF):
                            blk = blks[u % HALF]
                            a = acc0[:, bass.ds(blk * D, D)]
                            tg = 16 * (s * IT2 + it) + u
                            dve.wait_ge(agg_done, tg + 1)
                            dve.wait_ge(acc_free, 4 + tg)
                            V.scalar_tensor_tensor(a, bank[4 + u % 4][:, 0:D], inv[s][:, bass.ds(blk, 1)], a, ALU.mult, ALU.add).then_inc(acc_free, 1)
            dve.wait_ge(acc_free, 4 + 2 * T)
            acc3 = acc0.rearrange("p (b d) -> p b d", d=D)
            with dve.Fori(0, NB) as b:
                link.loop(b, 2)
                for s in range(2):
                    a = acc0[:, bass.ds(b * D, D)]
                    link(V.scalar_tensor_tensor(a, bias_rows[:, 1 + s, :], has[s][:, bass.ds(b, 1)], a, ALU.mult, ALU.add))
            link.end_loop(NB)
            dve.sem_inc(x1_ready, 1)
            layer_norm_stats(acc3, 1)
            link(V.tensor_scalar(sidx[0][:, :], sidx[0][:, :], 4, None, ALU.arith_shift_right))
            dve.sem_inc(idx_ready, 1)
            dve.sem_inc(n_used, 1)

            def normalised(b):
                V.tensor_scalar(xh[:, :], acc0[:, bass.ds(b * D, D)], mv2[:, bass.ds(2 * b, 1)], rstd[:, bass.ds(b, 1)], ALU.subtract, ALU.mult).then_inc(n_xh, 1)

            def take_attention_terms(b, last):
                if not last:
                    dve.wait_ge(n_T, b + 1)
                    dve.sem_inc(pace, 1)
                    normalised(b + 1)
                dve.wait_ge(n_grow, b + 1)
                V.tensor_copy(asn[:, bass.ds(b, 1), :], grow[:, D:D + H].unsqueeze(1)).then_inc(dv, 1)
                V.tensor_copy(tab[:, bass.ds(b, 1), 0:H], grow[:, D + H:D + 2 * H].unsqueeze(1)).then_inc(dv, 1)
                dve.wait_ge(dv, link.base + link.k + 2 * b + 2)
                dve.sem_inc(n_used, 1)

            normalised(0)
            with dve.Fori(0, NB - 1) as b:
                take_attention_terms(b, False)
            take_attention_terms(NB - 1, True)
            link.base += 2 * NB
            link(V.tensor_reduce(gmd[:, :], asn[:, :, :].rearrange("p b h -> p h b"), AX.X, ALU.min))
            dve.sem_inc(gm_T, 1)
            dve.wait_ge(gm_mm, 1)
            link(V.tensor_reduce(gm[0:H, :], bank[2][0:H, 0:P], AX.X, ALU.min))
            link(V.tensor_scalar(gmd[0:H, :], ident32[0:H, 0:H], gm[0:H, 0:1], None, ALU.mult))
            link(V.tensor_copy(gsel8[0:H, :].rearrange("p (k h) -> p k h", h=H), ident32[0:H, 0:H].unsqueeze(1).to_broadcast([H, P // H, H])))
            dve.sem_inc(gm_T, 1)
            dve.wait_ge(gm_mm, 3)
            link(V.tensor_copy(gmin_row[:, :], bank[4][:, 0:H]))
            link(V.tensor_scalar(gmin_part[:, :], bank[3][:, 0:1], -1.0, None, ALU.mult))
            dve.sem_inc(gm_ready, 1)
            dve.wait_ge(asrc_all, 2 * IT2)
            dve.wait_ge(x1_out, 16)
            a4 = asrc.rearrange("p (k q h) -> p q k h", q=TQ, h=H)
            l4 = sloc[0][:, :].rearrange("p (k q) -> p q k", q=TQ)
            stg4 = stg[:, :, :].rearrange("p j (q k h) -> p j q k h", q=1, h=H)
            dve.sem_inc(f_copied, 2)
            with dve.Fori(0, TQ) as q:
                dve.wait_ge(f_copied, 2 * q + 2)
                dve.sem_inc(pace, 1)
                V.tensor_copy(stg4[:, 0], a4[:, bass.ds(q, 1), :, :]).then_inc(dv, 1)
                V.tensor_copy(stg4[:, 1], l4[:, bass.ds(q, 1), :].unsqueeze(3).to_broadcast([P, 1, 16, H])).then_inc(dv, 1)
                dve.wait_ge(dv, link.base + link.k + 2 * q + 2)
                dve.sem_inc(f_stage, 1)
            link.base += 2 * TQ
            dve.wait_ge(f_copied, 2 * TQ + 2)
            l3 = locT.rearrange("p (q e) -> p q e", e=P)
            p3 = pen.rearrange("p (q e) -> p q e", e=P)
            z3 = lastT.rearrange("p (q e) -> p q e", e=P)
            link(V.memset(p3[:, :, 0:1], -BIG), wait=False)
            link(V.memset(z3[:, :, P - 1:P], 1.0), wait=False)
            link(V.tensor_tensor(z3[:, :, 0:P - 1], l3[:, :, 0:P - 1], l3[:, :, 1:P], ALU.not_equal))
            link(V.tensor_scalar(p3[:, :, 1:P], z3[:, :, 0:P - 1], -BIG, None, ALU.mult))
            link(V.tensor_tensor_scan(segmax, pen, segmax, 0.0, ALU.add, ALU.max))
            dve.sem_inc(b_copied, 1)
            with dve.Fori(0, TQ) as q:
                dve.wait_ge(b_copied, q + 1)
                dve.sem_inc(pace, 1)
                V.tensor_tensor(stg[:, 0, :], segmax[:, bass.ds(q * P, P)], lastT[:, bass.ds(q * P, P)], ALU.mult).then_inc(b_stage, 1)
            dve.wait_ge(b_copied, TQ + 1)
            link(V.memset(macc[:, :], 0.0))

            def group_one_hots(g, slot, first=0, end=HALF):
                for u in range(first, end):
                    V.tensor_scalar(four[slot][:, u, :], iota_row[:, 0:P], sloc[0][:, bass.ds(g * HALF + u, 1)], None, ALU.is_equal).then_inc(oh_ready, 1)

            def tile_maxima(it, last):
                for j in range(4):
                    g = 4 * it + j
                    ahead = not (last and j >= 2)
                    blks = blocks_of(0, g * HALF)
                    dve.wait_ge(m_psum, g + 1)
                    for u in range(HALF):
                        m = macc[:, bass.ds(blks[u] * H, H)]
                        V.tensor_tensor(m, m, bank[2 + j][:, u * H:(u + 1) * H], ALU.max).then_inc(m_max, 1)
                        if ahead:
                            group_one_hots(g + 2, (j + 2) % 4, u, u + 1)
                        dve.wait_ge(m_max, HALF * g + u + 1)

            group_one_hots(0, 0)
            group_one_hots(1, 1)
            with dve.Fori(0, IT2 // 2 - 1) as it:
                tile_maxima(it, False)
            tile_maxima(IT2 // 2 - 1, True)
            m3 = macc[:, :].rearrange("p (b h) -> p b h", h=H)
            link(V.tensor_tensor(m3, m3, gmin_row[:, :].unsqueeze(1).to_broadcast([P, NB, H]), ALU.add))
            link(V.tensor_tensor(m3, m3, tab[:, :, 0:H], ALU.add))
            link(V.scalar_tensor_tensor(tab[:, :, H:2 * H], m3, SLOPE, m3, ALU.mult, ALU.max))
            dve.sem_inc(tab_ready, 1)
            link(V.memset(accf, 0.0))

            def scores(it, h):
                w8 = score[:, h * HALF:(h + 1) * HALF, :]
                look = bank[2 + h][:, 0:HALF * 2 * H].rearrange("p (t j) -> p t j", j=2 * H)
                dve.wait_ge(l_look, 2 * it + h + 1)
                link(V.tensor_tensor(w8, look[:, :, 0:H], asrc3[:, bass.ds(it * 16 + h * HALF, HALF), :], ALU.add))
                link(V.scalar_tensor_tensor(w8, w8, SLOPE, w8, ALU.mult, ALU.max))
                link(V.tensor_tensor(w8, w8, look[:, :, H:2 * H], ALU.subtract))
                link(V.tensor_scalar(w8, w8, 0.0, None, ALU.min))
                dve.sem_inc(l_sc, 1)

            def message(it, u):
                dve.wait_ge(gathered[u], 16 * (3 * IT2 + it + 1))
                r = rows[:, u, 0:D].rearrange("p (h f) -> p h f", h=H)
                V.tensor_tensor(r, r, score[:, u, :].unsqueeze(2).to_broadcast([P, H, F_HEAD]), ALU.mult).then_inc(msg_ready, 1)

            def add(it, u, blk):
                a = accf[:, bass.ds(blk * (D + H), D + H)]
                tg = 16 * (2 * IT2 + it) + u
                dve.wait_ge(agg_done, tg + 1)
                dve.wait_ge(acc_free, 4 + tg)
                V.tensor_tensor(a, a, bank[4 + u % 4][:, 0:D + H], ALU.add).then_inc(acc_free, 1)

            def attend(it, last):
                for h in range(2):
                    ahead = not (last and h)
                    blks = blocks_of(0, it * 16 + h * HALF)
                    for j in range(HALF):
                        if j >= 2:
                            message(it, h * HALF + j)
                        if ahead and j < 3:
                            one_hots_ready(0, it + h, 1 - h, 3 * j, min(3 * j + 3, HALF))
                        if j >= 3:
                            add(it, h * HALF + j - 3, blks[j - 3])
                    if ahead:
                        scores(it + h, 1 - h)
                    add(it, h * HALF + 5, blks[5])
                    add(it, h * HALF + 6, blks[6])
                    if ahead:
                        first_message(it + h, 1 - h)
                    add(it, h * HALF + 7, blks[7])
                    if ahead:
                        message(it + h, (1 - h) * HALF + 1)

            def first_message(it, h):
                dve.wait_ge(l_exp, 2 * it + h + 1)
                dve.sem_inc(pace, 1)
                message(it, h * HALF)

            one_hots_ready(0, 0, 0)
            scores(0, 0)
            first_message(0, 0)
            message(0, 1)
            with dve.Fori(0, IT2 - 1) as it:
                link.loop(it, 2 * 4)
                attend(it, False)
            link.end_loop(IT2 - 1)
            attend(IT2 - 1, True)
            dve.wait_ge(acc_free, 4 + 3 * T)
            dve.sem_inc(fin_start, 1)
            af = accf.rearrange("p (b d) -> p b d", d=D + H)
            link(V.tensor_scalar(rden[:, :, :], af[:, :, D:D + H], TINY, None, ALU.max))
            link(V.reciprocal(rden[:, :, :], rden[:, :, :]))
            dve.wait_ge(x1_in, 16)
            groups = [(g * OB, OB) for g in range(OG)] + [(NB - 1, 1)]
            for b0, n in groups:
                for b in range(b0, b0 + n):
                    r = af[:, b, 0:D].rearrange("p (h f) -> p h f", h=H)
                    link(V.tensor_tensor(r, r, rden[:, b, :].unsqueeze(2).to_broadcast([P, H, F_HEAD]), ALU.mult), wait=False)
                    link(V.tensor_tensor(x_all[:, b, :], x_all[:, b, :], bias_rows[:, 3, :], ALU.add))
                    link(V.tensor_tensor(x_all[:, b, :], x_all[:, b, :], af[:, b, 0:D], ALU.add))
                dve.sem_inc(fin, 1)


def kernel(**inputs):
    import numpy as np
    import concourse.bacc as bacc
    from concourse.bass_utils import run_bass_kernel_spmd as run

    nc = bacc.Bacc("TRN2", target_bir_lowering=False, num_devices=1)
    arrays = {}

    def given(name):
        a = np.ascontiguousarray(inputs[name])
        arrays["in_" + name] = a
        return nc.dram_tensor("in_" + name, a.shape, mybir.dt.from_np(a.dtype), kind="ExternalInput").ap()

    xs = [given(n) for n in (
        "x", "src", "dst", "edge_type_16", "L0_gnn_Wf", "L0_gnn_Wb", "L0_gnn_loop_weight", "L0_gnn_forward_bias",
        "L0_gnn_backward_bias", "L0_gnn_self_bias", "L1_gnn_W", "L1_gnn_att_src", "L1_gnn_att_dst", "L1_gnn_bias")]
    out = nc.dram_tensor("out", inputs["x"].shape, F32, kind="ExternalOutput").ap()
    build(nc, *xs, out)
    return run(nc, [arrays], core_ids=[0]).results[0]["out"]
```
